# Optimizing a Trainium2 kernel written in Bass

```python
import numpy as np
import jax
import jax.numpy as jnp

def _softmax(x, axis=-1):
    return jax.nn.softmax(x, axis=axis)

def _gelu(x):
    return jax.nn.gelu(x, approximate=True)

def _silu(x):
    return jax.nn.silu(x)

def _sigmoid(x):
    return jax.nn.sigmoid(x)

def _layernorm(x, axis=-1, eps=1e-05):
    m = jnp.mean(x, axis=axis, keepdims=True)
    v = jnp.var(x, axis=axis, keepdims=True)
    return (x - m) / jnp.sqrt(v + eps)

def _scatter_add(tgt, idx, src, axis=0):
    return tgt.at[idx].add(src)

def _segment_sum(src, seg, n):
    return jax.ops.segment_sum(src, seg, n)
kernel_name = 'mk_xattn_ffn_d4_seqx_r8_d719de'

def setup_inputs(seed: int=0):
    np.random.seed(seed)
    _w = jnp.asarray

    def _rec_inputs():
        import jax
        import jax.numpy as jnp
        _rk = jax.random.key(seed)
        x = -0.0002928 + 1 * jax.random.normal(jax.random.fold_in(_rk, 1), (32, 128, 128), jnp.float32)
        _lenS = 128 - jax.random.randint(jax.random.fold_in(_rk, 7), (32,), 0, max(1, 128 // 4) + 1, jnp.int32)
        _lenS2 = 128 - jax.random.randint(jax.random.fold_in(_rk, 8), (32,), 0, max(1, 128 // 4) + 1, jnp.int32)
        _ctx_1024P = jax.random.normal(jax.random.fold_in(_rk, 11), (32, 16, 128), jnp.float32)
        _ctx_1024c = jax.random.dirichlet(jax.random.fold_in(_rk, 511), 0.3 * jnp.ones((16,), jnp.float32), (32, 128))
        _ctx_1024t = jnp.einsum('bsk,bkd->bsd', _ctx_1024c, _ctx_1024P)
        _ctx_1024t = _ctx_1024t * jax.lax.rsqrt(jnp.mean(jnp.square(_ctx_1024t)) + 1e-12) * 0.953939
        ctx_1024 = -1.39393e-06 + 0.999914 * (_ctx_1024t + 0.3 * jax.random.normal(jax.random.fold_in(_rk, 611), (32, 128, 128), jnp.float32))
        _validS = jnp.arange(128)[None, :] < _lenS[:, None]
        _validS2 = jnp.arange(128)[None, :] < _lenS2[:, None]
        _causal = jnp.tril(jnp.ones((128, 128), dtype=bool))
        mask_Bx1xSxS2_ff0 = jnp.where(jnp.ones((32, 1, 128, 128), dtype=bool), 0.0, -1000000000.0).astype(jnp.float32)
        mask_Bx1xSxS2_ik1 = jnp.where(jnp.broadcast_to(_validS2[:, None, None, :], (32, 1, 128, 128)), 1, 0).astype(jnp.int32)
        return (x, ctx_1024, mask_Bx1xSxS2_ff0, mask_Bx1xSxS2_ik1)
    x, ctx_1024, mask_Bx1xSxS2_ff0, mask_Bx1xSxS2_ik1 = _rec_inputs()

    def _L0_xattn_setup():
        import jax, jax.numpy as jnp
        import numpy as np
        HIDDEN = 128
        HEADS = 16
        N, T1, T2 = (2, 256, 256)

        def _split_heads(x):
            n, t, e = x.shape
            return x.reshape(n, t, HEADS, e // HEADS).transpose(0, 2, 1, 3)
        key = jax.random.key(seed)
        k1, k2, k3, k4 = jax.random.split(key, 4)
        q = jax.random.normal(k1, (N, T1, HIDDEN), dtype=jnp.float32)
        encoder_k = jax.random.normal(k2, (N, T2, HIDDEN), dtype=jnp.float32)
        encoder_v = jax.random.normal(k3, (N, T2, HIDDEN), dtype=jnp.float32)
        encoder_attention_mask = jnp.zeros((N, 1, T2, T2), dtype=jnp.float32)
        wo_w = jax.random.normal(k4, (HIDDEN, HIDDEN), dtype=jnp.float32) * (1.0 / np.sqrt(HIDDEN))
        wo_b = jnp.zeros((HIDDEN,), dtype=jnp.float32)
        return {'q': q, 'encoder_k': encoder_k, 'encoder_v': encoder_v, 'encoder_attention_mask': encoder_attention_mask, 'wo_w': wo_w, 'wo_b': wo_b}
    _L0_xattn_all = _L0_xattn_setup()
    _L0_xattn_in = {k: v for k, v in _L0_xattn_all.items() if k in ('wo_w', 'wo_b')}
    del _L0_xattn_all

    def _L0_ffn_setup():
        import jax, jax.numpy as jnp
        import numpy as np
        D = 128
        H = 512
        O = 128
        E = 8
        K = 2
        key = jax.random.key(seed)
        ks = jax.random.split(key, 8)
        B, S = (2, 256)
        x = jax.random.normal(ks[0], (B, S, D), dtype=jnp.float32)
        s = 0.02
        Wr = jax.random.normal(ks[1], (D, E), dtype=jnp.float32) * s
        br = jnp.zeros((E,), dtype=jnp.float32)
        W1 = jax.random.normal(ks[2], (E, D, H), dtype=jnp.float32) * s
        b1 = jnp.zeros((E, H), dtype=jnp.float32)
        W2 = jax.random.normal(ks[3], (E, H, O), dtype=jnp.float32) * s
        b2 = jnp.zeros((E, O), dtype=jnp.float32)
        return {'x': x, 'Wr': Wr, 'br': br, 'W1': W1, 'b1': b1, 'W2': W2, 'b2': b2}
    _L0_ffn_all = _L0_ffn_setup()
    _L0_ffn_in = {k: v for k, v in _L0_ffn_all.items() if k in ('Wr', 'br', 'W1', 'b1', 'W2', 'b2')}
    del _L0_ffn_all

    def _L1_xattn_setup():
        import jax, jax.numpy as jnp
        import numpy as np
        DIM = 128
        HEADS = 16
        HEAD_DIM = DIM // HEADS
        key = jax.random.key(seed)
        ks = jax.random.split(key, 12)
        B, Tq, Tk = (2, 256, 256)
        inp = {'query': jax.random.normal(ks[0], (B, Tq, DIM), jnp.float32), 'key': jax.random.normal(ks[1], (B, Tk, DIM), jnp.float32), 'value': jax.random.normal(ks[2], (B, Tk, DIM), jnp.float32), 'mask': jax.random.randint(ks[3], (B, 1, Tq, Tk), 0, 2, jnp.int32), 'wq': jax.random.uniform(ks[4], (DIM, DIM), jnp.float32, -1.0, 1.0) * np.sqrt(6.0 / (2 * DIM)), 'wk': jax.random.uniform(ks[5], (DIM, DIM), jnp.float32, -1.0, 1.0) * np.sqrt(6.0 / (2 * DIM)), 'wv': jax.random.uniform(ks[6], (DIM, DIM), jnp.float32, -1.0, 1.0) * np.sqrt(6.0 / (2 * DIM)), 'wo': jax.random.uniform(ks[7], (DIM, DIM), jnp.float32, -1.0, 1.0) * np.sqrt(6.0 / (2 * DIM)), 'bq': jnp.zeros((DIM,), jnp.float32), 'bk': jnp.zeros((DIM,), jnp.float32), 'bv': jnp.zeros((DIM,), jnp.float32), 'bo': jnp.zeros((DIM,), jnp.float32)}
        return inp
    _L1_xattn_all = _L1_xattn_setup()
    _L1_xattn_in = {k: v for k, v in _L1_xattn_all.items() if k in ('wq', 'wk', 'wv', 'wo', 'bq', 'bk', 'bv', 'bo')}
    del _L1_xattn_all

    def _L1_ffn_setup():
        import jax, jax.numpy as jnp
        import numpy as np
        QMAX = 127.0

        def _ste_round(v):
            return v + jax.lax.stop_gradient(jnp.round(v) - v)

        def _act_fake_quant(x, clip_factor):
            scale = jax.nn.sigmoid(clip_factor) * jnp.max(jnp.abs(x)) / QMAX
            return jnp.clip(_ste_round(x / scale), -QMAX - 1.0, QMAX) * scale

        def _weight_fake_quant(w):
            scale = jnp.max(jnp.abs(w), axis=1, keepdims=True) / QMAX
            return jnp.clip(_ste_round(w / scale), -QMAX - 1.0, QMAX) * scale
        key = jax.random.key(seed)
        k1, k2, k3, k4 = jax.random.split(key, 4)
        B, S, H, I = (8, 1024, 128, 352)
        return {'x': jax.random.normal(k1, (B, S, H), dtype=jnp.float32), 'clip_x': jnp.full((1,), 4.0, dtype=jnp.float32), 'clip_down': jnp.full((1,), 4.0, dtype=jnp.float32), 'w_gate': jax.random.normal(k2, (I, H), dtype=jnp.float32) * 0.02, 'w_up': jax.random.normal(k3, (I, H), dtype=jnp.float32) * 0.02, 'w_down': jax.random.normal(k4, (H, I), dtype=jnp.float32) * 0.02}
    _L1_ffn_all = _L1_ffn_setup()
    _L1_ffn_in = {k: v for k, v in _L1_ffn_all.items() if k in ('clip_x', 'clip_down', 'w_gate', 'w_up', 'w_down')}
    del _L1_ffn_all

    def _L2_xattn_setup():
        import jax, jax.numpy as jnp
        import numpy as np
        D_MODEL = 128
        NUM_HEADS = 16
        D_K = D_MODEL // NUM_HEADS
        key = jax.random.key(seed)
        ks = jax.random.split(key, 11)
        B, S = (4, 256)
        s = 1.0 / np.sqrt(D_MODEL)
        return {'Q': jax.random.normal(ks[0], (B, S, D_MODEL), jnp.float32), 'K': jax.random.normal(ks[1], (B, S, D_MODEL), jnp.float32), 'V': jax.random.normal(ks[2], (B, S, D_MODEL), jnp.float32), 'Wq': jax.random.normal(ks[3], (D_MODEL, D_MODEL), jnp.float32) * s, 'bq': jnp.zeros((D_MODEL,), jnp.float32), 'Wk': jax.random.normal(ks[4], (D_MODEL, D_MODEL), jnp.float32) * s, 'bk': jnp.zeros((D_MODEL,), jnp.float32), 'Wv': jax.random.normal(ks[5], (D_MODEL, D_MODEL), jnp.float32) * s, 'bv': jnp.zeros((D_MODEL,), jnp.float32), 'Wo': jax.random.normal(ks[6], (D_MODEL, D_MODEL), jnp.float32) * s, 'bo': jnp.zeros((D_MODEL,), jnp.float32)}
    _L2_xattn_all = _L2_xattn_setup()
    _L2_xattn_in = {k: v for k, v in _L2_xattn_all.items() if k in ('Wq', 'bq', 'Wk', 'bk', 'Wv', 'bv', 'Wo', 'bo')}
    del _L2_xattn_all

    def _L2_ffn_setup():
        import jax, jax.numpy as jnp
        import numpy as np
        D_MODEL = 128
        NUM_SLOTS = 64
        TOP_K = 8
        B, T = (4, 512)

        def _forward(x, slot_init, slot_scale, w1, b1, w2, b2, gru_wih, gru_whh, gru_bih, gru_bhh, wv, bv, wo, bo, tau):
            Bn, Tn, D = x.shape
            Sn = slot_init.shape[0]
            S = jnp.broadcast_to((slot_init * slot_scale)[None], (Bn, Sn, D)).astype(x.dtype)
            slot_mean = S.mean(axis=1, keepdims=True)
            ctx = jnp.concatenate([x, jnp.broadcast_to(slot_mean, x.shape)], axis=-1)
            h = jax.nn.gelu(ctx @ w1.T + b1, approximate=False)
            route_logits = (h @ w2.T + b2) / (jnp.abs(tau) + 0.1)
            topk_vals, topk_idx = jax.lax.top_k(route_logits, TOP_K)
            topk_w = jax.nn.softmax(topk_vals, axis=-1)
            alpha = jnp.sum(topk_w[..., None] * jax.nn.one_hot(topk_idx, Sn, dtype=x.dtype), axis=-2)
            slot_input = jnp.einsum('bts,btd->bsd', alpha, x)
            slot_wsum = alpha.sum(axis=1) + 1e-08
            gi = (slot_input / slot_wsum[..., None]).reshape(Bn * Sn, D)
            hs = S.reshape(Bn * Sn, D)
            gx = gi @ gru_wih.T + gru_bih
            gh = hs @ gru_whh.T + gru_bhh
            xr, xz, xn = jnp.split(gx, 3, axis=-1)
            hr, hz, hn = jnp.split(gh, 3, axis=-1)
            r = jax.nn.sigmoid(xr + hr)
            z = jax.nn.sigmoid(xz + hz)
            n = jnp.tanh(xn + r * hn)
            h_new = (1.0 - z) * n + z * hs
            S_new = h_new.reshape(Bn, Sn, D)
            slot_values = S_new @ wv.T + bv
            out = jnp.einsum('bts,bsd->btd', alpha, slot_values)
            return out @ wo.T + bo
        key = jax.random.key(seed)
        ks = jax.random.split(key, 16)
        D, S = (D_MODEL, NUM_SLOTS)
        H = D // 2
        sc = lambda fan_in: 1.0 / np.sqrt(fan_in)
        inp = {'x': jax.random.normal(ks[0], (B, T, D), dtype=jnp.float32), 'slot_init': jax.random.normal(ks[1], (S, D), dtype=jnp.float32) * 0.1, 'slot_scale': jnp.ones((S, 1), dtype=jnp.float32), 'w1': jax.random.normal(ks[2], (H, 2 * D), dtype=jnp.float32) * sc(2 * D), 'b1': jnp.zeros((H,), dtype=jnp.float32), 'w2': jax.random.normal(ks[3], (S, H), dtype=jnp.float32) * sc(H), 'b2': jnp.zeros((S,), dtype=jnp.float32), 'gru_wih': jax.random.normal(ks[4], (3 * D, D), dtype=jnp.float32) * sc(D), 'gru_whh': jax.random.normal(ks[5], (3 * D, D), dtype=jnp.float32) * sc(D), 'gru_bih': jnp.zeros((3 * D,), dtype=jnp.float32), 'gru_bhh': jnp.zeros((3 * D,), dtype=jnp.float32), 'wv': jax.random.normal(ks[6], (D, D), dtype=jnp.float32) * sc(D), 'bv': jnp.zeros((D,), dtype=jnp.float32), 'wo': jax.random.normal(ks[7], (D, D), dtype=jnp.float32) * sc(D), 'bo': jnp.zeros((D,), dtype=jnp.float32), 'tau': jnp.ones((1,), dtype=jnp.float32)}
        return inp
    _L2_ffn_all = _L2_ffn_setup()
    _L2_ffn_in = {k: v for k, v in _L2_ffn_all.items() if k in ('slot_init', 'slot_scale', 'w1', 'b1', 'w2', 'b2', 'gru_wih', 'gru_whh', 'gru_bih', 'gru_bhh', 'wv', 'bv', 'wo', 'bo', 'tau')}
    del _L2_ffn_all

    def _L3_xattn_setup():
        import jax, jax.numpy as jnp
        import numpy as np
        B, NQ, NKV = (2, 256, 256)
        DIM, CTX_DIM = (128, 128)
        HEADS, DIM_HEAD = (16, 64)
        INNER = HEADS * DIM_HEAD
        SCALE = DIM_HEAD ** (-0.5)
        key = jax.random.key(seed)
        ks = jax.random.split(key, 6)
        x = jax.random.normal(ks[0], (B, NQ, DIM), dtype=jnp.float32)
        context = jax.random.normal(ks[1], (B, NKV, CTX_DIM), dtype=jnp.float32)
        Wq = jax.random.normal(ks[2], (DIM, INNER), dtype=jnp.float32) / np.sqrt(DIM)
        Wkv = jax.random.normal(ks[3], (CTX_DIM, 2 * INNER), dtype=jnp.float32) / np.sqrt(CTX_DIM)
        Wout = jax.random.normal(ks[4], (INNER, DIM), dtype=jnp.float32) / np.sqrt(INNER)
        bout = jax.random.normal(ks[5], (DIM,), dtype=jnp.float32) * 0.01
        return {'x': x, 'context': context, 'Wq': Wq, 'Wkv': Wkv, 'Wout': Wout, 'bout': bout}
    _L3_xattn_all = _L3_xattn_setup()
    _L3_xattn_in = {k: v for k, v in _L3_xattn_all.items() if k in ('Wq', 'Wkv', 'Wout', 'bout')}
    del _L3_xattn_all

    def _L3_ffn_setup():
        import jax, jax.numpy as jnp
        import numpy as np
        D_MODEL = 128
        HIDDEN = 256
        N_EXPERTS = 8
        TOP_K = 2
        key = jax.random.key(seed)
        ks = jax.random.split(key, 9)
        s = 0.02
        x = jax.random.normal(ks[0], (4, 256, D_MODEL), dtype=jnp.float32)
        sw1 = jax.random.normal(ks[1], (D_MODEL, HIDDEN), dtype=jnp.float32) * s
        sw2 = jax.random.normal(ks[2], (D_MODEL, HIDDEN), dtype=jnp.float32) * s
        sw3 = jax.random.normal(ks[3], (HIDDEN, D_MODEL), dtype=jnp.float32) * s
        ew1 = jax.random.normal(ks[4], (N_EXPERTS, D_MODEL, HIDDEN), dtype=jnp.float32) * s
        ew2 = jax.random.normal(ks[5], (N_EXPERTS, D_MODEL, HIDDEN), dtype=jnp.float32) * s
        ew3 = jax.random.normal(ks[6], (N_EXPERTS, HIDDEN, D_MODEL), dtype=jnp.float32) * s
        rw = jax.random.normal(ks[7], (D_MODEL, N_EXPERTS), dtype=jnp.float32) * s
        rb = jax.random.normal(ks[8], (N_EXPERTS,), dtype=jnp.float32) * s
        return {'x': x, 'sw1': sw1, 'sw2': sw2, 'sw3': sw3, 'ew1': ew1, 'ew2': ew2, 'ew3': ew3, 'rw': rw, 'rb': rb}
    _L3_ffn_all = _L3_ffn_setup()
    _L3_ffn_in = {k: v for k, v in _L3_ffn_all.items() if k in ('sw1', 'sw2', 'sw3', 'ew1', 'ew2', 'ew3', 'rw', 'rb')}
    del _L3_ffn_all
    return {'x': x, 'ctx_1024': ctx_1024, 'mask_Bx1xSxS2_ff0': mask_Bx1xSxS2_ff0, 'mask_Bx1xSxS2_ik1': mask_Bx1xSxS2_ik1, 'L0_xattn_wo_w': _L0_xattn_in['wo_w'], 'L0_xattn_wo_b': _L0_xattn_in['wo_b'], 'L0_ffn_Wr': _L0_ffn_in['Wr'], 'L0_ffn_br': _L0_ffn_in['br'], 'L0_ffn_W1': _L0_ffn_in['W1'], 'L0_ffn_b1': _L0_ffn_in['b1'], 'L0_ffn_W2': _L0_ffn_in['W2'], 'L0_ffn_b2': _L0_ffn_in['b2'], 'L1_xattn_wq': _L1_xattn_in['wq'], 'L1_xattn_wk': _L1_xattn_in['wk'], 'L1_xattn_wv': _L1_xattn_in['wv'], 'L1_xattn_wo': _L1_xattn_in['wo'], 'L1_xattn_bq': _L1_xattn_in['bq'], 'L1_xattn_bk': _L1_xattn_in['bk'], 'L1_xattn_bv': _L1_xattn_in['bv'], 'L1_xattn_bo': _L1_xattn_in['bo'], 'L1_ffn_clip_x': _L1_ffn_in['clip_x'], 'L1_ffn_clip_down': _L1_ffn_in['clip_down'], 'L1_ffn_w_gate': _L1_ffn_in['w_gate'], 'L1_ffn_w_up': _L1_ffn_in['w_up'], 'L1_ffn_w_down': _L1_ffn_in['w_down'], 'L2_xattn_Wq': _L2_xattn_in['Wq'], 'L2_xattn_bq': _L2_xattn_in['bq'], 'L2_xattn_Wk': _L2_xattn_in['Wk'], 'L2_xattn_bk': _L2_xattn_in['bk'], 'L2_xattn_Wv': _L2_xattn_in['Wv'], 'L2_xattn_bv': _L2_xattn_in['bv'], 'L2_xattn_Wo': _L2_xattn_in['Wo'], 'L2_xattn_bo': _L2_xattn_in['bo'], 'L2_ffn_slot_init': _L2_ffn_in['slot_init'], 'L2_ffn_slot_scale': _L2_ffn_in['slot_scale'], 'L2_ffn_w1': _L2_ffn_in['w1'], 'L2_ffn_b1': _L2_ffn_in['b1'], 'L2_ffn_w2': _L2_ffn_in['w2'], 'L2_ffn_b2': _L2_ffn_in['b2'], 'L2_ffn_gru_wih': _L2_ffn_in['gru_wih'], 'L2_ffn_gru_whh': _L2_ffn_in['gru_whh'], 'L2_ffn_gru_bih': _L2_ffn_in['gru_bih'], 'L2_ffn_gru_bhh': _L2_ffn_in['gru_bhh'], 'L2_ffn_wv': _L2_ffn_in['wv'], 'L2_ffn_bv': _L2_ffn_in['bv'], 'L2_ffn_wo': _L2_ffn_in['wo'], 'L2_ffn_bo': _L2_ffn_in['bo'], 'L2_ffn_tau': _L2_ffn_in['tau'], 'L3_xattn_Wq': _L3_xattn_in['Wq'], 'L3_xattn_Wkv': _L3_xattn_in['Wkv'], 'L3_xattn_Wout': _L3_xattn_in['Wout'], 'L3_xattn_bout': _L3_xattn_in['bout'], 'L3_ffn_sw1': _L3_ffn_in['sw1'], 'L3_ffn_sw2': _L3_ffn_in['sw2'], 'L3_ffn_sw3': _L3_ffn_in['sw3'], 'L3_ffn_ew1': _L3_ffn_in['ew1'], 'L3_ffn_ew2': _L3_ffn_in['ew2'], 'L3_ffn_ew3': _L3_ffn_in['ew3'], 'L3_ffn_rw': _L3_ffn_in['rw'], 'L3_ffn_rb': _L3_ffn_in['rb']}

def reference(x, ctx_1024, mask_Bx1xSxS2_ff0, mask_Bx1xSxS2_ik1, L0_xattn_wo_w, L0_xattn_wo_b, L0_ffn_Wr, L0_ffn_br, L0_ffn_W1, L0_ffn_b1, L0_ffn_W2, L0_ffn_b2, L1_xattn_wq, L1_xattn_wk, L1_xattn_wv, L1_xattn_wo, L1_xattn_bq, L1_xattn_bk, L1_xattn_bv, L1_xattn_bo, L1_ffn_clip_x, L1_ffn_clip_down, L1_ffn_w_gate, L1_ffn_w_up, L1_ffn_w_down, L2_xattn_Wq, L2_xattn_bq, L2_xattn_Wk, L2_xattn_bk, L2_xattn_Wv, L2_xattn_bv, L2_xattn_Wo, L2_xattn_bo, L2_ffn_slot_init, L2_ffn_slot_scale, L2_ffn_w1, L2_ffn_b1, L2_ffn_w2, L2_ffn_b2, L2_ffn_gru_wih, L2_ffn_gru_whh, L2_ffn_gru_bih, L2_ffn_gru_bhh, L2_ffn_wv, L2_ffn_bv, L2_ffn_wo, L2_ffn_bo, L2_ffn_tau, L3_xattn_Wq, L3_xattn_Wkv, L3_xattn_Wout, L3_xattn_bout, L3_ffn_sw1, L3_ffn_sw2, L3_ffn_sw3, L3_ffn_ew1, L3_ffn_ew2, L3_ffn_ew3, L3_ffn_rw, L3_ffn_rb):
    import jax
    import jax.numpy as jnp

    def _L0_xattn_ref(q, encoder_k, encoder_v, encoder_attention_mask, wo_w, wo_b):
        import jax, jax.numpy as jnp
        import numpy as np
        HIDDEN = 128
        HEADS = 16
        N, T1, T2 = (2, 256, 256)

        def _split_heads(x):
            n, t, e = x.shape
            return x.reshape(n, t, HEADS, e // HEADS).transpose(0, 2, 1, 3)
        qh = _split_heads(q)
        kh = _split_heads(encoder_k)
        vh = _split_heads(encoder_v)
        scores = jnp.einsum('bhqd,bhkd->bhqk', qh, kh) + encoder_attention_mask
        weights = jax.nn.softmax(scores, axis=-1)
        ctx = jnp.einsum('bhqk,bhkd->bhqd', weights, vh)
        ctx = ctx.transpose(0, 2, 1, 3).reshape(q.shape[0], q.shape[1], -1)
        return jax.nn.relu(ctx @ wo_w.T + wo_b)

    def _L0_ffn_ref(x, Wr, br, W1, b1, W2, b2):
        import jax, jax.numpy as jnp
        import numpy as np
        D = 128
        H = 512
        O = 128
        E = 8
        K = 2
        B, S, _ = x.shape
        T = B * S
        xf = x.reshape(T, D)
        logits = xf @ Wr + br
        topk_logits, topk_idx = jax.lax.top_k(logits, K)
        gates = jax.nn.softmax(topk_logits, axis=1)
        dense_gates = jnp.zeros((T, E), dtype=logits.dtype).at[jnp.arange(T)[:, None], topk_idx].set(gates)
        h = jax.nn.relu(jnp.einsum('td,edh->teh', xf, W1) + b1)
        y = jnp.einsum('teh,eho->teo', h, W2) + b2
        out = jnp.einsum('te,teo->to', dense_gates, y)
        return out.reshape(B, S, O)

    def _L1_xattn_ref(query, key, value, mask, wq, wk, wv, wo, bq, bk, bv, bo):
        import jax, jax.numpy as jnp
        import numpy as np
        DIM = 128
        HEADS = 16
        HEAD_DIM = DIM // HEADS
        B, Tq, C = query.shape
        Tk = key.shape[1]
        scale = 1.0 / np.sqrt(HEAD_DIM)
        q = (query @ wq.T + bq).reshape(B, Tq, HEADS, HEAD_DIM).transpose(0, 2, 1, 3)
        k = (key @ wk.T + bk).reshape(B, Tk, HEADS, HEAD_DIM).transpose(0, 2, 1, 3)
        v = (value @ wv.T + bv).reshape(B, Tk, HEADS, HEAD_DIM).transpose(0, 2, 1, 3)
        scores = jnp.einsum('bhqd,bhkd->bhqk', q, k) * scale
        scores = jnp.clip(scores, -100.0, 100.0)
        scores = jnp.where(mask == 0, -jnp.inf, scores)
        attn = jax.nn.softmax(scores, axis=-1)
        out = jnp.einsum('bhqk,bhkd->bhqd', attn, v)
        out = out.transpose(0, 2, 1, 3).reshape(B, Tq, HEADS * HEAD_DIM)
        return out @ wo.T + bo

    def _L1_ffn_ref(x, clip_x, clip_down, w_gate, w_up, w_down):
        import jax, jax.numpy as jnp
        import numpy as np
        QMAX = 127.0

        def _ste_round(v):
            return v + jax.lax.stop_gradient(jnp.round(v) - v)

        def _act_fake_quant(x, clip_factor):
            scale = jax.nn.sigmoid(clip_factor) * jnp.max(jnp.abs(x)) / QMAX
            return jnp.clip(_ste_round(x / scale), -QMAX - 1.0, QMAX) * scale

        def _weight_fake_quant(w):
            scale = jnp.max(jnp.abs(w), axis=1, keepdims=True) / QMAX
            return jnp.clip(_ste_round(w / scale), -QMAX - 1.0, QMAX) * scale
        xq = _act_fake_quant(x, clip_x[0])
        gate = jnp.einsum('bsh,ih->bsi', xq, _weight_fake_quant(w_gate))
        up = jnp.einsum('bsh,ih->bsi', xq, _weight_fake_quant(w_up))
        h = _act_fake_quant(jax.nn.silu(gate) * up, clip_down[0])
        return jnp.einsum('bsi,hi->bsh', h, _weight_fake_quant(w_down))

    def _L2_xattn_ref(Q, K, V, Wq, bq, Wk, bk, Wv, bv, Wo, bo):
        import jax, jax.numpy as jnp
        import numpy as np
        D_MODEL = 128
        NUM_HEADS = 16
        D_K = D_MODEL // NUM_HEADS
        B, S, _ = Q.shape
        H, dk = (NUM_HEADS, D_K)
        q = (Q @ Wq + bq).reshape(B, S, H, dk).transpose(0, 2, 1, 3)
        k = (K @ Wk + bk).reshape(B, S, H, dk).transpose(0, 2, 1, 3)
        v = (V @ Wv + bv).reshape(B, S, H, dk).transpose(0, 2, 1, 3)
        scores = jnp.einsum('bhqd,bhkd->bhqk', q, k) / jnp.sqrt(jnp.float32(dk))
        attn = jax.nn.softmax(scores, axis=-1)
        ctx = jnp.einsum('bhqk,bhkd->bhqd', attn, v)
        ctx = ctx.transpose(0, 2, 1, 3).reshape(B, S, H * dk)
        return ctx @ Wo + bo

    def _L2_ffn_ref(x, slot_init, slot_scale, w1, b1, w2, b2, gru_wih, gru_whh, gru_bih, gru_bhh, wv, bv, wo, bo, tau):
        import jax, jax.numpy as jnp
        import numpy as np
        D_MODEL = 128
        NUM_SLOTS = 64
        TOP_K = 8
        B, T = (4, 512)

        def _forward(x, slot_init, slot_scale, w1, b1, w2, b2, gru_wih, gru_whh, gru_bih, gru_bhh, wv, bv, wo, bo, tau):
            Bn, Tn, D = x.shape
            Sn = slot_init.shape[0]
            S = jnp.broadcast_to((slot_init * slot_scale)[None], (Bn, Sn, D)).astype(x.dtype)
            slot_mean = S.mean(axis=1, keepdims=True)
            ctx = jnp.concatenate([x, jnp.broadcast_to(slot_mean, x.shape)], axis=-1)
            h = jax.nn.gelu(ctx @ w1.T + b1, approximate=False)
            route_logits = (h @ w2.T + b2) / (jnp.abs(tau) + 0.1)
            topk_vals, topk_idx = jax.lax.top_k(route_logits, TOP_K)
            topk_w = jax.nn.softmax(topk_vals, axis=-1)
            alpha = jnp.sum(topk_w[..., None] * jax.nn.one_hot(topk_idx, Sn, dtype=x.dtype), axis=-2)
            slot_input = jnp.einsum('bts,btd->bsd', alpha, x)
            slot_wsum = alpha.sum(axis=1) + 1e-08
            gi = (slot_input / slot_wsum[..., None]).reshape(Bn * Sn, D)
            hs = S.reshape(Bn * Sn, D)
            gx = gi @ gru_wih.T + gru_bih
            gh = hs @ gru_whh.T + gru_bhh
            xr, xz, xn = jnp.split(gx, 3, axis=-1)
            hr, hz, hn = jnp.split(gh, 3, axis=-1)
            r = jax.nn.sigmoid(xr + hr)
            z = jax.nn.sigmoid(xz + hz)
            n = jnp.tanh(xn + r * hn)
            h_new = (1.0 - z) * n + z * hs
            S_new = h_new.reshape(Bn, Sn, D)
            slot_values = S_new @ wv.T + bv
            out = jnp.einsum('bts,bsd->btd', alpha, slot_values)
            return out @ wo.T + bo
        return _forward(x, slot_init, slot_scale, w1, b1, w2, b2, gru_wih, gru_whh, gru_bih, gru_bhh, wv, bv, wo, bo, tau)

    def _L3_xattn_ref(x, context, Wq, Wkv, Wout, bout):
        import jax, jax.numpy as jnp
        import numpy as np
        B, NQ, NKV = (2, 256, 256)
        DIM, CTX_DIM = (128, 128)
        HEADS, DIM_HEAD = (16, 64)
        INNER = HEADS * DIM_HEAD
        SCALE = DIM_HEAD ** (-0.5)
        q = x @ Wq
        kv = context @ Wkv
        k, v = jnp.split(kv, 2, axis=-1)

        def split_heads(t):
            return t.reshape(t.shape[0], t.shape[1], HEADS, DIM_HEAD).transpose(0, 2, 1, 3)
        q, k, v = (split_heads(q), split_heads(k), split_heads(v))
        dots = jnp.einsum('bhqd,bhkd->bhqk', q, k) * SCALE
        attn = jax.nn.softmax(dots, axis=-1)
        out = jnp.einsum('bhqk,bhkd->bhqd', attn, v)
        out = out.transpose(0, 2, 1, 3).reshape(out.shape[0], out.shape[2], INNER)
        return out @ Wout + bout

    def _L3_ffn_ref(x, sw1, sw2, sw3, ew1, ew2, ew3, rw, rb):
        import jax, jax.numpy as jnp
        import numpy as np
        D_MODEL = 128
        HIDDEN = 256
        N_EXPERTS = 8
        TOP_K = 2
        shared = jnp.einsum('bth,hd->btd', jax.nn.silu(jnp.einsum('btd,dh->bth', x, sw1)) * jnp.einsum('btd,dh->bth', x, sw2), sw3)
        probs = jax.nn.softmax(jnp.einsum('btd,de->bte', x, rw) + rb, axis=-1)
        w, idx = jax.lax.top_k(probs, TOP_K)
        w = w / jnp.sum(w, axis=-1, keepdims=True)
        gates = jnp.sum(w[..., None] * jax.nn.one_hot(idx, N_EXPERTS, dtype=x.dtype), axis=-2)
        h = jax.nn.silu(jnp.einsum('btd,edh->beth', x, ew1)) * jnp.einsum('btd,edh->beth', x, ew2)
        eout = jnp.einsum('beth,ehd->betd', h, ew3)
        routed = jnp.einsum('betd,bte->btd', eout, gates)
        return shared + routed
    x = x + _L0_xattn_ref(_layernorm(x, axis=-1), ctx_1024, ctx_1024, mask_Bx1xSxS2_ff0, L0_xattn_wo_w, L0_xattn_wo_b)
    x = x + _L0_ffn_ref(_layernorm(x, axis=-1), L0_ffn_Wr, L0_ffn_br, L0_ffn_W1, L0_ffn_b1, L0_ffn_W2, L0_ffn_b2)
    x = x + _L1_xattn_ref(_layernorm(x, axis=-1), ctx_1024, ctx_1024, mask_Bx1xSxS2_ik1, L1_xattn_wq, L1_xattn_wk, L1_xattn_wv, L1_xattn_wo, L1_xattn_bq, L1_xattn_bk, L1_xattn_bv, L1_xattn_bo)
    x = x + _L1_ffn_ref(_layernorm(x, axis=-1), L1_ffn_clip_x, L1_ffn_clip_down, L1_ffn_w_gate, L1_ffn_w_up, L1_ffn_w_down)
    x = x + _L2_xattn_ref(_layernorm(x, axis=-1), ctx_1024, ctx_1024, L2_xattn_Wq, L2_xattn_bq, L2_xattn_Wk, L2_xattn_bk, L2_xattn_Wv, L2_xattn_bv, L2_xattn_Wo, L2_xattn_bo)
    x = x + _L2_ffn_ref(_layernorm(x, axis=-1), L2_ffn_slot_init, L2_ffn_slot_scale, L2_ffn_w1, L2_ffn_b1, L2_ffn_w2, L2_ffn_b2, L2_ffn_gru_wih, L2_ffn_gru_whh, L2_ffn_gru_bih, L2_ffn_gru_bhh, L2_ffn_wv, L2_ffn_bv, L2_ffn_wo, L2_ffn_bo, L2_ffn_tau)
    x = x + _L3_xattn_ref(_layernorm(x, axis=-1), ctx_1024, L3_xattn_Wq, L3_xattn_Wkv, L3_xattn_Wout, L3_xattn_bout)
    x = x + _L3_ffn_ref(_layernorm(x, axis=-1), L3_ffn_sw1, L3_ffn_sw2, L3_ffn_sw3, L3_ffn_ew1, L3_ffn_ew2, L3_ffn_ew3, L3_ffn_rw, L3_ffn_rb)
    return x

_drawn_inputs = setup_inputs


def setup_inputs(seed=0):
    import zlib

    import numpy as np

    out = dict(_drawn_inputs(seed))
    spreads = {'L0_xattn_wo_b': (0.0, 0.1),
     'L0_ffn_br': (0.0, 0.1),
     'L0_ffn_b1': (0.0, 0.536),
     'L0_ffn_b2': (0.0, 0.1),
     'L1_xattn_bq': (0.0, 0.503),
     'L1_xattn_bk': (0.0, 2.0),
     'L1_xattn_bv': (0.0, 0.1),
     'L1_xattn_bo': (0.0, 0.1),
     'L2_xattn_bq': (0.0, 0.491),
     'L2_xattn_bk': (0.0, 2.0),
     'L2_xattn_bv': (0.0, 0.1),
     'L2_xattn_bo': (0.0, 0.1),
     'L2_ffn_slot_scale': (1.0, 0.6),
     'L2_ffn_b1': (0.0, 0.629),
     'L2_ffn_b2': (0.0, 0.552),
     'L2_ffn_gru_bih': (0.0, 0.32),
     'L2_ffn_gru_bhh': (0.0, 1.488),
     'L2_ffn_bv': (0.0, 0.1),
     'L2_ffn_bo': (0.0, 0.1)}
    factors = {'L1_ffn_w_gate': 8.0,
     'L1_ffn_w_up': 7.961,
     'L1_ffn_w_down': 8.0,
     'L2_ffn_slot_init': 3.769,
     'L2_ffn_gru_whh': 8.0,
     'L3_xattn_bout': 7.702,
     'L3_ffn_sw1': 8.0,
     'L3_ffn_sw2': 8.0,
     'L3_ffn_sw3': 8.0,
     'L3_ffn_ew1': 8.0,
     'L3_ffn_ew2': 8.0,
     'L3_ffn_ew3': 8.0,
     'L3_ffn_rw': 8.0,
     'L3_ffn_rb': 8.0}
    for name, (base, spread) in spreads.items():
        noise = np.random.default_rng([zlib.crc32(name.encode()), seed]).standard_normal(out[name].shape)
        drawn = base * np.exp(spread * noise) if base else spread * noise
        out[name] = jnp.asarray(drawn.astype(out[name].dtype))
    for name, factor in factors.items():
        out[name] = (out[name] * factor).astype(out[name].dtype)
    return out
```

```python
from contextlib import ExitStack

import concourse.bass as bass
import numpy as np
from concourse import mybir

F32 = mybir.dt.float32
BF16 = mybir.dt.bfloat16
F16 = mybir.dt.float16
I32 = mybir.dt.int32
ALU = mybir.AluOpType
ACT = mybir.ActivationFunctionType
AX = mybir.AxisListType.X
RMAX = bass.bass_isa.ReduceOp.max

P = 128
B, S, D = 32, 128, 128
G = 4
NG = B // G
T = G * S
H = 16
DH = D // H
DH3 = 64
IC3 = H * DH3 // P
BLK = 8
NU = G * H // BLK
E0, HID0 = 8, 512
C0 = HID0 // P
E3, HID3 = 8, 256
C3 = HID3 // P
FF1 = 352
CH1 = [(0, 128), (128, 128), (256, 96)]
NC1 = len(CH1)
SLOTS, TOPS, HR = 64, 8, 64
EPS = 1e-5
MAGIC = 1.5 * 2.0 ** 23
QMAX = 127.0
NEG = -1.0e30
PSCALE = 2.0 ** 14

W_COLS = [("ident", 128), ("wo0", 128), ("wr0", E0), ("b1_0", E0 * C0), ("b2_0", 128),
          ("wq1", 128), ("wk1", 128), ("wv1", 128), ("wo1", 128), ("bq1", 1), ("bk1", 1),
          ("wq2", 128), ("wk2", 128), ("wv2", 128), ("wo2", 128), ("bq2", 1), ("bk2", 1),
          ("w1x", HR), ("w1m", HR), ("w2s", SLOTS), ("b1s", 1), ("wih", 3 * D), ("whh", 3 * D),
          ("wvs", 128), ("wos", 128), ("slot", 128), ("slot_scale", 1), ("rw3", E3),
          ("hm", 4), ("hms", 4), ("below", E0 * E0)]
R_COLS = [("br0", E0), ("wo_b0", D), ("bv1", D), ("bo1", D), ("bv2", D), ("bo2", D), ("b2s", SLOTS),
          ("bih", 3 * D), ("bhh", 3 * D), ("bvs", D), ("bos", D), ("bout3", D), ("rb3", E3),
          ("clip_x", 1), ("clip_down", 1), ("tau", 1)]


def places(cols):
    at, out = 0, {}
    for name, n in cols:
        out[name] = (at, n)
        at += n
    return out, at


W_AT, W_N = places(W_COLS)
R_AT, R_N = places(R_COLS)
BIG0 = 2 * E0 * HID0
BIG3 = 4 * IC3 * D + 3 * (E3 + 1) * HID3
NE3 = E3 + 1


def build(nc, x_d, ctx_d, ctxT_d, mask0_d, mask1_d, w_d, r_d, big0_d, big3_d, wg_d, wu_d, wd_d, out_d):
    with ExitStack() as stack:
        def sb(name, shape, dt=F32):
            return stack.enter_context(nc.sbuf_tensor(name, shape, dt))

        def sem(name):
            return stack.enter_context(nc.semaphore(name))

        x_all = sb("x_all", [P, B, D])
        h_all = sb("h_all", [P, NG * NC1, T])
        big = sb("big", [P, max(BIG0, BIG3)])
        w = sb("w", [P, W_N])
        rows = sb("rows", [P, R_N])
        wgq = sb("wgq", [P, FF1], BF16)
        wuq = sb("wuq", [P, FF1], BF16)
        wdq = sb("wdq", [P, NC1, D], BF16)
        gsc = sb("gsc", [P, NC1])
        usc = sb("usc", [P, NC1])
        dscB = sb("dscB", [P, D])
        identb = sb("identb", [P, P], BF16)
        ones = sb("ones", [P, P])
        half = sb("half", [P, G])
        sc = sb("sc", [P, 16])
        hmax = sb("hmax", [P, NG * NC1])
        ymax = sb("ymax", [P, NG])
        crz = sb("crz", [P, 2 * D])
        hn_c = sb("hn_c", [P, D])
        hs = sb("hs", [P, D])
        hsT = sb("hsT", [P, P])
        smean = sb("smean", [P, 1])
        c1 = sb("c1", [P, 1])
        xg = sb("xg", [P, G, D])
        spare = sb("spare", [P, 2, T])
        ctxT = sb("ctxT", [P, T])
        mask1i = sb("mask1i", [P, G, S], I32)
        y = sb("y", [P, G, D])
        yT = sb("yT", [P, T])
        qT = sb("qT", [P, T])
        qm = sb("qm", [P, 4, T])
        kT = sb("kT", [P, T])
        r0 = sb("r0", [P, G, D])
        va = sb("va", [P, G, H, 3, DH + 1], BF16)
        pb = sb("pb", [P, 2, BLK * S])
        pt = sb("pt", [P, 2, BLK * S])
        ctx = spare[:, 0, :].rearrange("p (b d) -> p b d", b=G)
        mask0 = spare[:, 1, :].rearrange("p (b k) -> p b k", b=G)
        u3 = spare
        mask1 = mask1i[:, :, :].bitcast(F32)
        pth = pt[:, :, :].bitcast(F16)
        on = sb("on", [P, BLK, DH + 1])
        rc = sb("rc", [P, BLK])
        nm = sb("nm", [P, 2, BLK])
        o = sb("o", [P, G, D])
        oT = sb("oT", [P, T])
        hT = sb("hT", [P, 8, T])
        st = sb("st", [P, G, 6])
        mv = sb("mv", [P, G, 2])
        ve = sb("ve", [P, G])
        rs = sb("rs", [P, G])
        lg = sb("lg", [P, G, E0])
        cmp_a = sb("cmp_a", [P, G, E0 * E0])
        cmp_b = sb("cmp_b", [P, G, E0 * E0])
        sel = sb("sel", [P, G, E0])
        gate = sb("gate", [P, G, E0])
        gs = sb("gs", [P, 4 * G])
        gateT = sb("gateT", [E0, T])
        ps = stack.enter_context(nc.psum_tensor("ps", [P, 8, 512], F32))

        def W(name, p=P):
            a, n = W_AT[name]
            return w[0:p, a:a + n]

        def R(name):
            a, n = R_AT[name]
            return rows[:, a:a + n]

        def row_bcast(name, n):
            return R(name).unsqueeze(1).to_broadcast([P, n, R_AT[name][1]])

        def tiles(k, n=D):
            return ps[:, k, 0:G * n].rearrange("p (b n) -> p b n", b=G)

        ident = W("ident")
        w1_0 = big[:, 0:E0 * HID0].rearrange("p (e c m) -> p e c m", e=E0, c=C0)
        w2_0 = big[:, E0 * HID0:BIG0].rearrange("p (e c m) -> p e c m", e=E0, c=C0)
        q3_w, k3_w, v3_w, o3_w = (big[:, i * IC3 * D:(i + 1) * IC3 * D].rearrange("p (c m) -> p c m", c=IC3)
                                  for i in range(4))
        f3 = big[:, 4 * IC3 * D:BIG3].rearrange("p (w e c m) -> p w e c m", w=3, e=NE3, c=C3)

        small_loaded = sem("small_loaded")
        large_loaded = sem("large_loaded")
        out_stored = sem("out_stored")
        setup_v = sem("setup_v")
        w_rounded = sem("w_rounded")
        w_turned = sem("w_turned")
        diag_ready = sem("diag_ready")
        scales_psum = sem("scales_psum")
        slots_ready = sem("slots_ready")
        slots_psum = sem("slots_psum")
        setup_g = sem("setup_g")
        counted = []

        def isem(name):
            s = sem(name)
            counted.append(s)
            return s

        group_loaded = isem("group_loaded")
        group_loaded2 = isem("group_loaded2")
        x_ready = isem("x_ready")
        ln_stats = isem("ln_stats")
        ln_mean = isem("ln_mean")
        ln_var = isem("ln_var")
        ln_rstd = isem("ln_rstd")
        y_ready = isem("y_ready")
        yT_psum = isem("yT_psum")
        yT_ready = isem("yT_ready")
        x_kept = isem("x_kept")
        x_copied = isem("x_copied")
        hq_ready = isem("hq_ready")
        down_psum = isem("down_psum")
        steps = isem("steps")

        def attention_sems(n):
            names = ["q_psum", "k_psum", "v_psum", "q_col", "k_col", "v_row", "v_hi", "v_rest", "v_mid", "v_ready",
                     "q_ready", "scores", "masked", "maxed", "exps", "transposed", "p_hi", "p_lo", "pv",
                     "o_read", "o_recip", "normed", "oT_psum", "oT_ready", "out_psum", "bias_added",
                     "chunk_added"]
            return {name: isem(f"{name}_{n}") for name in names}

        att_a = attention_sems("a")
        att_b = attention_sems("b")
        moe = {name: isem(f"moe_{name}") for name in
               ["logits", "logit_row", "shifted", "gate_exp", "gates", "gateT_psum", "gateT", "hid_psum",
                "hid_act", "hid_dve", "expert", "combined", "b2_psum", "silu"]}
        slot = {name: isem(f"slot_{name}") for name in
                ["hid_psum", "hid", "logits", "shifted", "exps", "alpha", "in_psum", "in_ready", "wsum", "aT_psum",
                 "aT", "gates_psum", "rz_in", "rz", "n_in", "n", "new", "newT_psum", "newT", "val_psum", "val",
                 "oT_psum", "oT", "out_psum", "bias_added"]}

        def linker(v, semaphore):
            count = [0]

            def link(m):
                count[0] += 1
                m.then_inc(semaphore, 1)
                v.wait_ge(semaphore, count[0])
            return link

        def layernorm_dve(v, n, out):
            v.wait_ge(x_ready, n)
            for b in range(G):
                m = v.bn_stats(st[:, b, :], xg[:, b, :])
            m.then_inc(ln_stats, 1)
            v.wait_ge(ln_stats, n)
            for b in range(G):
                m = v.bn_aggr(mv[:, b, :], st[:, b, :])
            m.then_inc(ln_mean, 1)
            v.wait_ge(ln_mean, n)
            v.tensor_scalar(ve[:, :], mv[:, :, 1], EPS, None, ALU.add).then_inc(ln_var, 1)
            v.wait_ge(ln_rstd, n)
            for b in range(G):
                m = v.tensor_scalar(out(b), xg[:, b, :], mv[:, b, 0:1], rs[:, b:b + 1], ALU.subtract, ALU.mult)
            m.then_inc(y_ready, 1)

        def layernorm_pool(g, n):
            g.wait_ge(ln_var, n)
            g.tensor_tensor(rs[:, :], ve[:, :], half[:, :], ALU.pow).then_inc(ln_rstd, 1)

        def transpose_y_pe(pe, n):
            pe.wait_ge(y_ready, n)
            for b in range(G):
                m = pe.transpose(ps[:, 7, b * P:(b + 1) * P], y[:, b, :], ident)
            m.then_inc(yT_psum, 1)

        def copy_yT_act(a, n, out):
            a.wait_ge(yT_psum, n)
            a.activation(out, ps[:, 7, :], ACT.Copy).then_inc(yT_ready, 1)

        def attention_pe(pe, s, n, k_in, wq, wk, wv, wo):
            if wq is not None:
                if n > 1:
                    pe.wait_ge(x_ready, n)
                pe.matmul(ps[:, 5, :], wk, ctxT[:, :], start=True, stop=True).then_inc(s["k_psum"], 1)
                for b in range(G):
                    m = pe.matmul(ps[:, 4, b * D:(b + 1) * D], ctxT[:, b * S:(b + 1) * S], wv, start=True, stop=True)
                m.then_inc(s["v_psum"], 1)
            transpose_y_pe(pe, n)
            if wq is not None:
                pe.wait_ge(yT_ready, n)
                pe.matmul(ps[:, 6, :], wq, yT[:, :], start=True, stop=True).then_inc(s["q_psum"], 1)
                pe.wait_ge(s["k_col"], 1)
                pe.wait_ge(s["v_row"], 1)
            pe.wait_ge(s["q_ready"], 1)
            scores_used = s["exps"] if not s["has_mask"] else s["masked"]
            for step in range(NU + 2):
                if step < NU:
                    u = step
                    b, c = divmod(u, 2)
                    if u >= 2:
                        pe.wait_ge(scores_used, u - 1)
                    for k in range(BLK):
                        a, j = divmod(k, 4)
                        g = 2 * c + a
                        m = pe.matmul(ps[:, 2 * (u % 2) + a, j * S:(j + 1) * S],
                                      qm[32 * g:32 * g + 32, j, b * S:(b + 1) * S],
                                      k_in[32 * g:32 * g + 32, b * S:(b + 1) * S], start=True, stop=True)
                    m.then_inc(s["scores"], 1)
                if 0 <= step - 1 < NU:
                    u = step - 1
                    pe.wait_ge(s["exps"], u + 1)
                    if u >= 1:
                        pe.wait_ge(s["p_lo"], u)
                    for k in range(BLK):
                        m = pe.transpose(ps[:, 4 + k // 4, (k % 4) * S:(k % 4 + 1) * S],
                                         pb[:, u % 2, k * S:(k + 1) * S], ident)
                    m.then_inc(s["transposed"], 1)
                if step >= 2:
                    u = step - 2
                    b, c = divmod(u, 2)
                    if u == 0:
                        pe.wait_ge(s["v_ready"], 1)
                    pe.wait_ge(s["p_lo"], u + 1)
                    if u >= 1:
                        pe.wait_ge(s["o_read"], u)
                    for k in range(BLK):
                        for part in range(2):
                            m = pe.matmul(ps[:, 6, k * 27:(k + 1) * 27],
                                          pth[:, u % 2, part * BLK * S + k * S:part * BLK * S + (k + 1) * S],
                                          va[:, b, BLK * c + k, :, :].rearrange("p t d -> p (t d)"),
                                          start=(part == 0), stop=(part == 1))
                    m.then_inc(s["pv"], 1)
            pe.wait_ge(s["normed"], NU)
            for b in range(G):
                m = pe.transpose(ps[:, 7, b * P:(b + 1) * P], o[:, b, :], ident)
            m.then_inc(s["oT_psum"], 1)
            pe.wait_ge(s["oT_ready"], 1)
            for b in range(G):
                m = pe.matmul(ps[:, 7, b * D:(b + 1) * D], oT[:, b * S:(b + 1) * S], wo, start=True, stop=True)
            m.then_inc(s["out_psum"], 1)

        def attention_act(a, s, n, bq, bk, v_src):
            if bk is not None:
                a.wait_ge(s["k_psum"], 1)
                a.activation(kT[:, :], ps[:, 5, :], ACT.Identity, bias=bk).then_inc(s["k_col"], 1)
                a.wait_ge(s["v_row"], 1)
            heads = v_src[:, :, :].rearrange("p b (h d) -> p (b h) d", h=H)
            rest = r0[:, :, :].rearrange("p b (h d) -> p (b h) d", h=H)
            parts = va[:, :, :, :, :].rearrange("p b h t d -> p (b h) t d")
            a.activation(parts[:, :, 0, 0:DH], heads, ACT.Copy).then_inc(s["v_hi"], 1)
            a.wait_ge(s["v_rest"], 1)
            a.activation(parts[:, :, 1, 0:DH], rest, ACT.Copy).then_inc(s["v_mid"], 1)
            if bq is None:
                copy_yT_act(a, n, qT[:, :])
            else:
                copy_yT_act(a, n, yT[:, :])
                a.wait_ge(s["q_psum"], 1)
                a.activation(qT[:, :], ps[:, 6, :], ACT.Identity, bias=bq).then_inc(s["q_col"], 1)
            for step in range(NU + 1):
                if step < NU:
                    u = step
                    a.wait_ge(s["maxed"], u + 1)
                    if u >= 2:
                        a.wait_ge(s["transposed"], u - 1)
                    src = pb[:, u % 2, :] if s["has_mask"] else ps[:, 2 * (u % 2):2 * (u % 2) + 2, :].rearrange(
                        "p a k -> p (a k)")
                    for k in range(BLK):
                        m = a.activation(pb[:, u % 2, k * S:(k + 1) * S], src[:, k * S:(k + 1) * S], ACT.Exp,
                                         bias=nm[:, u % 2, k:k + 1])
                    m.then_inc(s["exps"], 1)
                if step >= 1:
                    u = step - 1
                    a.wait_ge(s["transposed"], u + 1)
                    if u >= 2:
                        a.wait_ge(s["pv"], u - 1)
                    a.activation(pth[:, u % 2, 0:BLK * S], ps[:, 4:6, :].rearrange("p a k -> p (a k)"), ACT.Copy,
                                 scale=PSCALE).then_inc(s["p_hi"], 1)
            a.wait_ge(s["oT_psum"], 1)
            a.activation(oT[:, :], ps[:, 7, :], ACT.Copy).then_inc(s["oT_ready"], 1)

        def values_pool(g, s, v_src):
            heads = v_src[:, :, :].rearrange("p b (h d) -> p (b h) d", h=H)
            rest = r0[:, :, :].rearrange("p b (h d) -> p (b h) d", h=H)
            parts = va[:, :, :, :, :].rearrange("p b h t d -> p (b h) t d")
            g.wait_ge(s["v_hi"], 1)
            g.tensor_tensor(rest, heads, parts[:, :, 0, 0:DH], ALU.subtract).then_inc(s["v_rest"], 1)
            g.wait_ge(s["v_mid"], 1)
            g.tensor_tensor(parts[:, :, 2, 0:DH], rest, parts[:, :, 1, 0:DH], ALU.subtract).then_inc(s["v_ready"], 1)

        def attention_dve(v, s, n, bias_v, mask_op, heads_mask):
            if bias_v is not None:
                v.wait_ge(s["v_psum"], 1)
                v.tensor_tensor(o[:, :, :], tiles(4), row_bcast(bias_v, G), ALU.add).then_inc(s["v_row"], 1)
            layernorm_dve(v, n, lambda b: y[:, b, :])
            v.wait_ge(s["q_col"], 1) if bias_v is not None else v.wait_ge(yT_ready, n)
            for j in range(4):
                m = v.tensor_scalar(qm[:, j, :], qT[:, :], heads_mask[:, j:j + 1], None, ALU.mult)
            m.then_inc(s["q_ready"], 1)
            for step in range(NU + 2):
                if step < NU:
                    u = step
                    b = u // 2
                    sc_ps = ps[:, 2 * (u % 2):2 * (u % 2) + 2, :].rearrange("p a (j k) -> p (a j) k", k=S)
                    v.wait_ge(s["scores"], u + 1)
                    if mask_op is not None:
                        if u >= 2:
                            v.wait_ge(s["transposed"], u - 1)
                        buf = pb[:, u % 2, :].rearrange("p (j k) -> p j k", k=S)
                        mask_op(v, buf, sc_ps, b).then_inc(s["masked"], 1)
                        v.wait_ge(s["masked"], u + 1)
                        sc_ps = buf
                    if u >= 2:
                        v.wait_ge(s["exps"], u - 1)
                    v.tensor_reduce(nm[:, u % 2, :], sc_ps, AX, ALU.max, negate=True).then_inc(s["maxed"], 1)
                if 0 <= step - 1 < NU:
                    u = step - 1
                    v.wait_ge(s["p_hi"], u + 1)
                    v.scalar_tensor_tensor(pth[:, u % 2, BLK * S:2 * BLK * S], ps[:, 4:6, :].rearrange("p a k -> p (a k)"),
                                           PSCALE, pth[:, u % 2, 0:BLK * S], ALU.mult,
                                           ALU.subtract).then_inc(s["p_lo"], 1)
                if step >= 2:
                    u = step - 2
                    b, c = divmod(u, 2)
                    v.wait_ge(s["pv"], u + 1)
                    if u >= 1:
                        v.wait_ge(s["normed"], u)
                    v.tensor_reduce(on[:, :, :], ps[:, 6, 0:BLK * 27].rearrange("p (k t d) -> p k d t", k=BLK, t=3), AX,
                                    ALU.add).then_inc(s["o_read"], 1)
                    v.wait_ge(s["o_read"], u + 1)
                    v.reciprocal(rc[:, :], on[:, :, DH]).then_inc(s["o_recip"], 1)
                    v.wait_ge(s["o_recip"], u + 1)
                    if u == 0 and bias_v is not None:
                        v.wait_ge(s["v_ready"], 1)
                    v.tensor_tensor(o[:, b, c * 64:(c + 1) * 64].rearrange("p (k d) -> p k d", d=DH), on[:, :, 0:DH],
                                    rc[:, :].unsqueeze(2).to_broadcast([P, BLK, DH]), ALU.mult).then_inc(s["normed"], 1)
            v.wait_ge(s["out_psum"], 1)

        def add_bias_pool(g, n, bias):
            g.wait_ge(y_ready, n)
            return g.tensor_tensor(xg[:, :, :], xg[:, :, :], row_bcast(bias, G), ALU.add)

        def router_pe(pe, wr):
            for b in range(G):
                m = pe.matmul(ps[:, 6, b * E0:(b + 1) * E0], yT[:, b * S:(b + 1) * S], wr, start=True, stop=True)
            m.then_inc(moe["logits"], 1)

        def router_dve(v, link, bias):
            v.wait_ge(moe["logits"], 1)
            link(v.tensor_tensor(lg[:, :, :], tiles(6, E0), row_bcast(bias, G), ALU.add))
            other = lg[:, :, :].unsqueeze(2).to_broadcast([P, G, E0, E0])
            own = lg[:, :, :].unsqueeze(3).to_broadcast([P, G, E0, E0])
            ca = cmp_a[:, :, :].rearrange("p b (e f) -> p b e f", e=E0)
            cb = cmp_b[:, :, :].rearrange("p b (e f) -> p b e f", e=E0)
            v.tensor_tensor(ca, other, own, ALU.is_gt)
            v.tensor_reduce(gs[:, 0:G], lg[:, :, :], AX, ALU.max)
            link(v.tensor_tensor(cb, other, own, ALU.is_equal))
            link(v.tensor_tensor(cmp_b[:, :, :], cmp_b[:, :, :],
                                 W("below").unsqueeze(1).to_broadcast([P, G, E0 * E0]), ALU.mult))
            v.tensor_tensor(lg[:, :, :], lg[:, :, :], gs[:, 0:G].unsqueeze(2).to_broadcast([P, G, E0]),
                            ALU.subtract).then_inc(moe["shifted"], 1)
            link(v.tensor_tensor(cmp_a[:, :, :], cmp_a[:, :, :], cmp_b[:, :, :], ALU.add))
            link(v.tensor_reduce(sel[:, :, :], ca, AX, ALU.add))
            link(v.tensor_scalar(sel[:, :, :], sel[:, :, :], 2.0, None, ALU.is_lt))
            v.wait_ge(moe["gate_exp"], 1)
            link(v.tensor_tensor(gate[:, :, :], gate[:, :, :], sel[:, :, :], ALU.mult))
            link(v.tensor_reduce(gs[:, G:2 * G], gate[:, :, :], AX, ALU.add))
            link(v.reciprocal(gs[:, 2 * G:3 * G], gs[:, G:2 * G]))
            v.tensor_tensor(gate[:, :, :], gate[:, :, :], gs[:, 2 * G:3 * G].unsqueeze(2).to_broadcast([P, G, E0]),
                            ALU.mult).then_inc(moe["gates"], 1)
            v.wait_ge(moe["gates"], 1)

        def router_act(a):
            a.wait_ge(moe["shifted"], 1)
            a.activation(gate[:, :, :], lg[:, :, :], ACT.Exp).then_inc(moe["gate_exp"], 1)

        def combine_dve(v, e, gated):
            v.wait_ge(moe["expert"], e + 1)
            if e:
                v.wait_ge(moe["combined"], e)
            for b in range(G):
                m = v.scalar_tensor_tensor(xg[:, b, :], ps[:, 4 + e % 2, b * D:(b + 1) * D],
                                           gate[:, b, e:e + 1] if gated else 1.0, xg[:, b, :], ALU.mult, ALU.add)
            m.then_inc(moe["combined"], 1)

        n_small, n_large = 9, 2
        with nc.Block() as block:
            @block.sync
            def _(sp):
                sp.dma_start(w[:, :], w_d).then_inc(small_loaded, 16)
                sp.dma_start(rows[:, :], r_d.partition_broadcast(P)).then_inc(small_loaded, 16)
                for k, src in enumerate((wg_d, wu_d)):
                    for c, (at, m) in enumerate(CH1):
                        sp.dma_start(hT[0:m, 3 * k + c, 0:D], src[at:at + m, :]).then_inc(small_loaded, 16)
                sp.dma_start(hT[:, 6, 0:FF1], wd_d).then_inc(small_loaded, 16)
                sp.dma_start(x_all[:, :, :], x_d.rearrange("b s d -> s b d")).then_inc(large_loaded, 16)
                sp.dma_start(big[:, 0:BIG0], big0_d).then_inc(large_loaded, 16)
                sp.wait_ge(large_loaded, 16 * n_large)

            @block.gpsimd
            def _(g):
                g.memset(ones[:, :], 1.0)
                g.memset(half[:, :], -0.5)
                g.memset(hmax[:, :], 0.0)
                g.memset(va[:, :, :, :, :], 0.0).then_inc(setup_g, 1)
                g.wait_ge(setup_g, 1)
                g.memset(va[:, :, :, 0, DH:DH + 1], 1.0).then_inc(setup_g, 1)

            @block.vector
            def _(v):
                link = linker(v, setup_v)
                v.memset(gsc[:, :], 0.0)
                v.memset(usc[:, :], 0.0)
                v.wait_ge(small_loaded, 16 * n_small)
                v.tensor_copy(identb[:, :], ident).then_inc(w_rounded, 1)
                for t in range(7):
                    m, n = (P, FF1) if t == 6 else (CH1[t % 3][1], D)
                    src = hT[0:m, t, 0:n]
                    scale = usc[0:m, t - 3:t - 2] if 3 <= t < 6 else (gsc[0:m, t:t + 1] if t < 3 else sc[0:m, 0:1])
                    link(v.tensor_reduce(sc[0:m, 1:2], src, AX, ALU.max, apply_absolute_value=True))
                    link(v.tensor_scalar(scale, sc[0:m, 1:2], 1.0 / QMAX, None, ALU.mult))
                    link(v.reciprocal(sc[0:m, 2:3], scale))
                    link(v.tensor_scalar(src, src, sc[0:m, 2:3], MAGIC, ALU.mult, ALU.add))
                    link(v.tensor_scalar(src, src, MAGIC, None, ALU.subtract))
                    v.tensor_scalar(pt[0:m, t % 2, 0:192].bitcast(BF16)[:, 0:n], src, QMAX, -QMAX - 1.0,
                                    ALU.min, ALU.max).then_inc(w_rounded, 1)
                    v.wait_ge(w_turned, t + 1)
                    pw = ps[:, t, 0:256].bitcast(BF16)
                    if t < 3:
                        v.tensor_copy(wgq[:, CH1[t][0]:CH1[t][0] + m], pw[:, 0:m])
                    elif t < 6:
                        v.tensor_copy(wuq[:, CH1[t - 3][0]:CH1[t - 3][0] + m], pw[:, 0:m])
                    else:
                        for c, (at, mc) in enumerate(CH1):
                            v.tensor_copy(wdq[0:mc, c, :], pw[0:mc, c * P:(c + 1) * P])
                v.tensor_scalar(hT[:, 7, 0:P], ident, sc[:, 0:1], None, ALU.mult).then_inc(diag_ready, 1)
                v.wait_ge(scales_psum, 1)
                v.tensor_copy(dscB[:, :], ps[:, 7, 0:P])
                link(v.tensor_scalar(sc[:, 4:5], R("tau"), -1.0, None, ALU.mult))
                link(v.tensor_tensor(sc[:, 4:5], sc[:, 4:5], R("tau"), ALU.max))
                link(v.tensor_scalar(sc[:, 4:5], sc[:, 4:5], 0.1, None, ALU.add))
                v.reciprocal(sc[:, 5:6], sc[:, 4:5])
                v.tensor_scalar(hs[:, :], W("slot"), W("slot_scale"), None, ALU.mult).then_inc(slots_ready, 1)
                v.wait_ge(slots_psum, 1)
                v.tensor_copy(hsT[:, :], ps[:, 1, 0:P])
                v.tensor_scalar(smean[:, :], ps[:, 2, 0:1], 1.0 / SLOTS, None, ALU.mult).then_inc(slots_ready, 1)
                v.wait_ge(slots_psum, 2)
                v.tensor_tensor(c1[0:HR, :], ps[0:HR, 3, 0:1], W("b1s", HR), ALU.add)
                link(v.tensor_tensor(crz[:, :], ps[:, 4, 0:2 * D], R("bhh")[:, 0:2 * D], ALU.add))
                v.tensor_tensor(crz[:, :], crz[:, :], R("bih")[:, 0:2 * D], ALU.add)
                v.tensor_tensor(hn_c[:, :], ps[:, 4, 2 * D:3 * D], R("bhh")[:, 2 * D:3 * D], ALU.add)

            @block.tensor
            def _(pe):
                for t in range(7):
                    pe.wait_ge(w_rounded, 1 + t + 1)
                    m = P if t == 6 else CH1[t % 3][1]
                    pw = ps[:, t, 0:256].bitcast(BF16)
                    src = pt[0:m, t % 2, 0:192].bitcast(BF16)
                    if t < 6:
                        i = pe.transpose(pw[:, 0:m], src[:, 0:D], identb[0:m, 0:m])
                    else:
                        for c, (at, mc) in enumerate(CH1):
                            i = pe.transpose(pw[0:mc, c * P:(c + 1) * P], src[:, at:at + mc], identb[:, :])
                    i.then_inc(w_turned, 1)
                pe.wait_ge(setup_g, 1)
                pe.wait_ge(diag_ready, 1)
                pe.matmul(ps[:, 7, 0:P], ones[:, :], hT[:, 7, 0:P], start=True, stop=True).then_inc(scales_psum, 1)
                pe.wait_ge(slots_ready, 1)
                pe.transpose(ps[:, 1, 0:P], hs[:, :], ident)
                pe.matmul(ps[:, 2, 0:1], hs[0:SLOTS, :], ones[0:SLOTS, 0:1], start=True, stop=True)\
                    .then_inc(slots_psum, 1)
                pe.wait_ge(slots_ready, 2)
                pe.matmul(ps[0:HR, 3, 0:1], W("w1m"), smean[:, :], start=True, stop=True)
                pe.matmul(ps[:, 4, 0:3 * D], hsT[:, :], W("whh"), start=True, stop=True).then_inc(slots_psum, 1)

            @block.scalar
            def _(a):
                a.wait_ge(small_loaded, 16 * n_small)
                a.activation(sc[:, 6:7], R("clip_x"), ACT.Sigmoid)
                a.activation(sc[:, 7:8], R("clip_down"), ACT.Sigmoid)

        first, last = counted[0].num, counted[-1].num
        assert [s.num for s in counted] == list(range(first, last + 1))

        def next_iteration():
            nc.gpsimd.sem_clear(range(first, last + 1))
            nc.all_engine_barrier()

        def mask0_add(v, out, scores, b):
            return v.tensor_tensor(out, scores, mask0[:, b, :].unsqueeze(1).to_broadcast([P, BLK, S]), ALU.add)

        def mask1_clip(v, out, scores, b):
            return v.scalar_tensor_tensor(out, scores, -100.0, mask1[:, b, :].unsqueeze(1).to_broadcast([P, BLK, S]),
                                          ALU.max, ALU.min)

        s0, s1 = dict(att_a, has_mask=True), dict(att_b, has_mask=True)
        ctx_rows = ctx_d.rearrange("b s d -> s b d")
        mask0_rows = mask0_d.rearrange("b s d -> s b d")
        mask1_rows = mask1_d.rearrange("b s d -> s b d")

        with nc.Fori(0, NG) as i:
            with nc.Block() as block:
                @block.sync
                def _(sp):
                    sp.dma_start(ctxT[:, :], ctxT_d[:, bass.ts(i, T)]).then_inc(group_loaded, 16)
                    sp.dma_start(ctx[:, :, :], ctx_rows[:, bass.ts(i, G), :]).then_inc(group_loaded, 16)
                    sp.dma_start(mask0[:, :, :], mask0_rows[:, bass.ts(i, G), :]).then_inc(group_loaded, 16)
                    sp.dma_start(mask1i[:, :, :], mask1_rows[:, bass.ts(i, G), :]).then_inc(group_loaded2, 16)
                    sp.wait_ge(group_loaded, 48)
                    sp.wait_ge(group_loaded2, 16)

                @block.tensor
                def _(pe):
                    pe.wait_ge(group_loaded, 48)
                    attention_pe(pe, s0, 1, ctxT, None, None, None, W("wo0"))
                    transpose_y_pe(pe, 2)
                    pe.wait_ge(yT_ready, 2)
                    router_pe(pe, W("wr0"))

                    def hidden(e):
                        for c in range(C0):
                            k = e * C0 + c
                            if k >= 4:
                                pe.wait_ge(moe["hid_act" if k % 2 == 0 else "hid_dve"], (k - 4) // 2 + 1)
                            pe.matmul(ps[:, k % 4, :], w1_0[:, e, c, :], yT[:, :], start=True, stop=True)\
                                .then_inc(moe["hid_psum"], 1)

                    def expert(e):
                        pe.wait_ge(moe["hid_act"], 2 * (e + 1))
                        pe.wait_ge(moe["hid_dve"], 2 * (e + 1))
                        if e >= 2:
                            pe.wait_ge(moe["combined"], e - 1)
                        for b in range(G):
                            for c in range(C0):
                                m = pe.matmul(ps[:, 4 + e % 2, b * D:(b + 1) * D],
                                              hT[:, (e * C0 + c) % 8, b * S:(b + 1) * S], w2_0[:, e, c, :],
                                              start=(c == 0), stop=(c == C0 - 1))
                        m.then_inc(moe["expert"], 1)

                    hidden(0)
                    for e in range(E0):
                        if e + 1 < E0:
                            hidden(e + 1)
                        if e == 0:
                            pe.wait_ge(moe["gates"], 1)
                            for b in range(G):
                                m = pe.transpose(ps[0:E0, 7, b * S:(b + 1) * S], gate[:, b, :], ident)
                            m.then_inc(moe["gateT_psum"], 1)
                        if e == 1:
                            pe.wait_ge(moe["gateT"], 1)
                            for b in range(G):
                                m = pe.matmul(ps[:, 7, b * D:(b + 1) * D], gateT[:, b * S:(b + 1) * S], W("b2_0", E0),
                                              start=True, stop=True)
                            m.then_inc(moe["b2_psum"], 1)
                        expert(e)
                    attention_pe(pe, s1, 3, kT, W("wq1"), W("wk1"), W("wv1"), W("wo1"))

                @block.scalar
                def _(a):
                    a.activation(xg[:, :, :], x_all[:, bass.ts(i, G), :], ACT.Copy).then_inc(x_ready, 1)
                    a.wait_ge(group_loaded, 48)
                    attention_act(a, s0, 1, None, None, ctx)
                    copy_yT_act(a, 2, yT[:, :])
                    router_act(a)
                    for k in range(0, E0 * C0, 2):
                        a.wait_ge(moe["hid_psum"], k + 1)
                        if k >= 8:
                            a.wait_ge(moe["expert"], (k - 8) // C0 + 1)
                        a.activation(hT[:, k % 8, :], ps[:, k % 4, :], ACT.Relu,
                                     bias=W("b1_0")[:, k:k + 1]).then_inc(moe["hid_act"], 1)
                    attention_act(a, s1, 3, W("bq1"), W("bk1"), o)
                    a.wait_ge(x_ready, 4)
                    a.activation(x_all[:, bass.ts(i, G), :], xg[:, :, :], ACT.Copy)

                @block.gpsimd
                def _(g):
                    g.wait_ge(group_loaded, 48)
                    values_pool(g, s0, ctx)
                    layernorm_pool(g, 1)
                    layernorm_pool(g, 2)
                    values_pool(g, s1, o)
                    layernorm_pool(g, 3)
                    add_bias_pool(g, 3, "bo1").then_inc(s1["bias_added"], 1)
                    layernorm_pool(g, 4)

                @block.vector
                def _(v):
                    link = linker(v, steps)
                    v.wait_ge(group_loaded, 48)
                    attention_dve(v, s0, 1, None, mask0_add, W("hm"))
                    v.tensor_tensor(r0[:, :, :], tiles(7), row_bcast("wo_b0", G), ALU.add).then_inc(s0["v_row"], 1)
                    v.wait_ge(s0["v_row"], 1)
                    v.scalar_tensor_tensor(xg[:, :, :], r0[:, :, :], 0.0, xg[:, :, :], ALU.max, ALU.add)\
                        .then_inc(x_ready, 1)
                    layernorm_dve(v, 2, lambda b: y[:, b, :])
                    router_dve(v, link, "br0")

                    def hidden(e):
                        for k in range(e * C0 + 1, (e + 1) * C0, 2):
                            v.wait_ge(moe["hid_psum"], k + 1)
                            if k >= 8:
                                v.wait_ge(moe["expert"], (k - 8) // C0 + 1)
                            v.tensor_scalar(hT[:, k % 8, :], ps[:, k % 4, :], W("b1_0")[:, k:k + 1], 0.0, ALU.add,
                                            ALU.max).then_inc(moe["hid_dve"], 1)

                    hidden(0)
                    for e in range(E0):
                        if e + 1 < E0:
                            hidden(e + 1)
                        if e == 0:
                            v.wait_ge(moe["gateT_psum"], 1)
                            v.tensor_copy(gateT[:, :], ps[0:E0, 7, :]).then_inc(moe["gateT"], 1)
                        combine_dve(v, e, True)
                    v.wait_ge(moe["b2_psum"], 1)
                    v.wait_ge(moe["combined"], E0)
                    v.tensor_tensor(xg[:, :, :], tiles(7), xg[:, :, :], ALU.add).then_inc(x_ready, 1)
                    v.wait_ge(group_loaded2, 16)
                    link(v.tensor_scalar(mask1[:, :, :], mask1i[:, :, :], 0.0, NEG, ALU.is_equal, ALU.mult))
                    link(v.tensor_scalar(mask1[:, :, :], mask1[:, :, :], 100.0, None, ALU.add))
                    attention_dve(v, s1, 3, "bv1", mask1_clip, W("hms"))
                    v.wait_ge(s1["bias_added"], 1)
                    v.tensor_tensor(xg[:, :, :], tiles(7), xg[:, :, :], ALU.add).then_inc(x_ready, 1)
                    layernorm_dve(v, 4, lambda b: y[:, b, :])
                    v.wait_ge(y_ready, 4)
                    v.tensor_copy(h_all[:, bass.ds(i * NC1, 1), :], y[:, :, :].rearrange("p b d -> p (b d)").unsqueeze(1))
                    v.tensor_reduce(ymax[:, bass.ds(i, 1)], y[:, :, :].rearrange("p b d -> p (b d)"), AX, ALU.max,
                                    apply_absolute_value=True)

            next_iteration()

        with nc.Block() as block:
            @block.vector
            def _(v):
                v.tensor_reduce(sc[:, 8:9], ymax[:, :], AX, ALU.max).then_inc(steps, 1)
                v.wait_ge(setup_g, 3)
                v.tensor_scalar(sc[:, 10:11], sc[:, 9:10], 1.0 / QMAX, sc[:, 6:7], ALU.mult, ALU.mult).then_inc(steps, 1)
                v.wait_ge(steps, 2)
                v.reciprocal(sc[:, 11:12], sc[:, 10:11])
                v.tensor_scalar(gsc[:, :], gsc[:, :], sc[:, 10:11], None, ALU.mult)
                v.tensor_scalar(usc[:, :], usc[:, :], sc[:, 10:11], None, ALU.mult).then_inc(steps, 1)
                v.wait_ge(steps, 3)

            @block.gpsimd
            def _(g):
                g.wait_ge(steps, 1)
                g.partition_all_reduce(sc[:, 9:10], sc[:, 8:9], P, RMAX).then_inc(setup_g, 1)

            @block.sync
            def _(sp):
                sp.dma_start(big[:, 0:BIG3], big3_d).then_inc(large_loaded, 16)

        next_iteration()

        def quantise(v, link, out, src, tmp, rscale):
            link(v.tensor_scalar(tmp, src, rscale, QMAX, ALU.mult, ALU.min))
            link(v.tensor_scalar(tmp, tmp, -QMAX - 1.0, MAGIC, ALU.max, ALU.add))
            return v.tensor_scalar(out, tmp, MAGIC, None, ALU.subtract)

        xq = pt[:, 0, 0:256].bitcast(BF16).rearrange("p (b d) -> p b d", b=G)
        xqT = pt[:, 1, 0:256].bitcast(BF16)
        with nc.Fori(0, NG) as i:
            with nc.Block() as block:
                @block.tensor
                def _(pe):
                    pe.wait_ge(y_ready, 1)
                    t_out = ps[:, 7, 0:256].bitcast(BF16)
                    for b in range(G):
                        m = pe.transpose(t_out[:, b * P:(b + 1) * P], xq[:, b, :], identb[:, :])
                    m.then_inc(yT_psum, 1)
                    pe.wait_ge(yT_ready, 1)
                    for c, (at, m) in enumerate(CH1):
                        pe.matmul(ps[0:m, c, :], wgq[:, at:at + m], xqT, start=True, stop=True)
                        pe.matmul(ps[0:m, 3 + c, :], wuq[:, at:at + m], xqT, start=True, stop=True)\
                            .then_inc(moe["hid_psum"], 1)

                @block.scalar
                def _(a):
                    a.wait_ge(yT_psum, 1)
                    a.activation(xqT, ps[:, 7, 0:256].bitcast(BF16), ACT.Copy).then_inc(yT_ready, 1)
                    for c, (at, m) in enumerate(CH1):
                        a.wait_ge(moe["hid_psum"], c + 1)
                        a.activation(hT[0:m, c, :], ps[0:m, c, :], ACT.Silu, scale=gsc[0:m, c:c + 1])\
                            .then_inc(moe["silu"], 1)

                @block.vector
                def _(v):
                    link = linker(v, steps)
                    quantise(v, link, xq.rearrange("p b d -> p (b d)").unsqueeze(1), h_all[:, bass.ds(i * NC1, 1), :],
                             y[:, :, :].rearrange("p b d -> p (b d)").unsqueeze(1), sc[:, 11:12]).then_inc(y_ready, 1)
                    for c, (at, m) in enumerate(CH1):
                        v.wait_ge(moe["silu"], c + 1)
                        v.scalar_tensor_tensor(hT[0:m, 4 + c, :], ps[0:m, 3 + c, :], usc[0:m, c:c + 1], hT[0:m, c, :],
                                               ALU.mult, ALU.mult).then_inc(moe["hid_dve"], 1)
                        v.wait_ge(moe["hid_dve"], c + 1)
                        v.tensor_copy(h_all[0:m, bass.ds(i * NC1 + c, 1), :], hT[0:m, 4 + c, :].unsqueeze(1))
                        v.tensor_reduce(hmax[0:m, bass.ds(i * NC1 + c, 1)], hT[0:m, 4 + c, :], AX, ALU.max,
                                        apply_absolute_value=True)

            next_iteration()

        with nc.Block() as block:
            @block.vector
            def _(v):
                v.tensor_reduce(sc[:, 8:9], hmax[:, :], AX, ALU.max).then_inc(steps, 1)
                v.wait_ge(setup_g, 4)
                v.tensor_scalar(sc[:, 10:11], sc[:, 9:10], 1.0 / QMAX, sc[:, 7:8], ALU.mult, ALU.mult).then_inc(steps, 1)
                v.wait_ge(steps, 2)
                v.reciprocal(sc[:, 11:12], sc[:, 10:11])
                v.tensor_scalar(dscB[:, :], dscB[:, :], sc[:, 10:11], None, ALU.mult).then_inc(steps, 1)
                v.wait_ge(steps, 3)

            @block.gpsimd
            def _(g):
                g.wait_ge(steps, 1)
                g.partition_all_reduce(sc[:, 9:10], sc[:, 8:9], P, RMAX).then_inc(setup_g, 1)

            @block.sync
            def _(sp):
                sp.wait_ge(large_loaded, 16 * (n_large + 1))

        next_iteration()

        s2 = dict(att_a, has_mask=False)
        s3 = att_b
        hq = pt[:, 0, 0:768].bitcast(BF16).rearrange("p (c t) -> p c t", c=NC1)
        gT = hT[0:HR, 0, :]
        slg = hT[:, 1, 0:G * SLOTS].rearrange("p (b s) -> p b s", b=G)
        srep = hT[:, 1, G * SLOTS:2 * G * SLOTS].rearrange("p (b s) -> p b s", b=G)
        alpha = hT[:, 2, 0:G * SLOTS].rearrange("p (b s) -> p b s", b=G)
        stop8 = hT[:, 2, 256:256 + G * 8].rearrange("p (b s) -> p b s", b=G)
        srow = hT[:, 2, 288:304]
        siT = hT[:, 3, 0:256]
        aT = hT[:, 3, 256:512].rearrange("p (q t) -> p q t", q=2)
        rz = hT[:, 4, :].rearrange("p (q n) -> p q n", q=2)
        xn = hT[:, 5, 0:256].rearrange("p (q n) -> p q n", q=2)
        hnew = hT[:, 5, 256:512].rearrange("p (q n) -> p q n", q=2)
        hnT = hT[:, 6, 0:256]
        sval = hT[:, 6, 256:512].rearrange("p (q n) -> p q n", q=2)
        outT = hT[:, 7, :]
        q3 = qm[:, 0:2, :]
        k3 = qm[:, 2:4, :]
        v3 = hT[:, 0:2, :]
        o3 = hT[:, 2:4, :]
        oT3 = hT[:, 4:6, :]
        sums = hT[:, 6, 0:2 * BLK].rearrange("p (u k) -> p u k", u=2)
        rc3 = hT[:, 6, 16:16 + BLK]

        with nc.Fori(0, NG) as i:
            with nc.Block() as block:
                @block.sync
                def _(sp):
                    sp.dma_start(ctxT[:, :], ctxT_d[:, bass.ts(i, T)]).then_inc(group_loaded, 16)
                    sp.wait_ge(group_loaded, 16)
                    sp.wait_ge(x_kept, 1)
                    sp.dma_start(out_d.rearrange("b s d -> s b d")[:, bass.ts(i, G), :],
                                 x_all[:, bass.ts(i, G), :]).then_inc(out_stored, 16)

                @block.tensor
                def _(pe):
                    pe.wait_ge(hq_ready, 1)
                    for b in range(G):
                        for c, (at, m) in enumerate(CH1):
                            j = pe.matmul(ps[:, 7, b * D:(b + 1) * D], hq[0:m, c, b * S:(b + 1) * S], wdq[0:m, c, :],
                                          start=(c == 0), stop=(c == NC1 - 1))
                    j.then_inc(down_psum, 1)
                    pe.wait_ge(group_loaded, 16)
                    attention_pe(pe, s2, 1, kT, W("wq2"), W("wk2"), W("wv2"), W("wo2"))
                    transpose_y_pe(pe, 2)
                    pe.wait_ge(yT_ready, 2)
                    pe.matmul(ps[0:HR, 0, :], W("w1x"), yT[:, :], start=True, stop=True).then_inc(slot["hid_psum"], 1)
                    pe.wait_ge(slot["hid"], 1)
                    for b in range(G):
                        m = pe.matmul(ps[:, 1, b * SLOTS:(b + 1) * SLOTS], gT[:, b * S:(b + 1) * S], W("w2s", HR),
                                      start=True, stop=True)
                    m.then_inc(slot["logits"], 1)
                    pe.wait_ge(slot["alpha"], 1)
                    for b in range(G):
                        m = pe.matmul(ps[:, 2, b * SLOTS:(b + 1) * SLOTS], y[:, b, :], alpha[:, b, :], start=True,
                                      stop=True)
                    m.then_inc(slot["in_psum"], 1)
                    for b in range(G):
                        q, a = divmod(b, 2)
                        m = pe.matmul(ps[64 * a:64 * a + 64, 3, q:q + 1], alpha[:, b, :], ones[:, 0:1], start=True,
                                      stop=True)
                    m.then_inc(slot["wsum"], 1)
                    for q in range(2):
                        m = pe.transpose(ps[:, 4, q * P:(q + 1) * P],
                                         alpha[:, 2 * q:2 * q + 2, :].rearrange("p b s -> p (b s)"), ident)
                    m.then_inc(slot["aT_psum"], 1)
                    pe.wait_ge(slot["in_ready"], 1)
                    for q in range(2):
                        m = pe.matmul(ps[:, 5 + q, 0:3 * D], siT[:, q * P:(q + 1) * P], W("wih"), start=True, stop=True)
                    m.then_inc(slot["gates_psum"], 1)
                    pe.wait_ge(slot["new"], 1)
                    for q in range(2):
                        m = pe.transpose(ps[:, 0, q * P:(q + 1) * P], hnew[:, q, :], ident)
                    m.then_inc(slot["newT_psum"], 1)
                    pe.wait_ge(slot["newT"], 1)
                    for q in range(2):
                        m = pe.matmul(ps[:, 1, q * D:(q + 1) * D], hnT[:, q * P:(q + 1) * P], W("wvs"), start=True,
                                      stop=True)
                    m.then_inc(slot["val_psum"], 1)
                    pe.wait_ge(slot["val"], 1)
                    pe.wait_ge(slot["aT"], 1)
                    for b in range(G):
                        q, a = divmod(b, 2)
                        m = pe.matmul(ps[:, 2 + a, q * S:(q + 1) * S], sval[64 * a:64 * a + 64, q, :],
                                      aT[64 * a:64 * a + 64, q, :], start=True, stop=True)
                    m.then_inc(slot["oT_psum"], 1)
                    pe.wait_ge(slot["oT"], 1)
                    for b in range(G):
                        m = pe.matmul(ps[:, 7, b * D:(b + 1) * D], outT[:, b * S:(b + 1) * S], W("wos"), start=True,
                                      stop=True)
                    m.then_inc(slot["out_psum"], 1)
                    transpose_y_pe(pe, 3)
                    pe.wait_ge(yT_ready, 3)

                    def project_q(c):
                        pe.matmul(ps[:, 7, :], q3_w[:, c, :], yT[:, :], start=True, stop=True).then_inc(s3["q_psum"], 1)

                    def project_k(c):
                        pe.wait_ge(s3["q_col"], c + 1)
                        pe.matmul(ps[:, 7, :], k3_w[:, c, :], ctxT[:, :], start=True, stop=True)\
                            .then_inc(s3["k_psum"], 1)

                    def project_v(c):
                        pe.wait_ge(s3["k_col"], c + 1)
                        for b in range(G):
                            m = pe.matmul(ps[:, 7, b * D:(b + 1) * D], ctxT[:, b * S:(b + 1) * S], v3_w[:, c, :],
                                          start=True, stop=True)
                        m.then_inc(s3["v_psum"], 1)

                    def scores(u, a):
                        for b in range(G):
                            m = pe.matmul(ps[:, 2 * (u % 2) + a, b * S:(b + 1) * S],
                                          q3[64 * a:64 * a + 64, u % 2, b * S:(b + 1) * S],
                                          k3[64 * a:64 * a + 64, u % 2, b * S:(b + 1) * S], start=True, stop=True)
                        if a:
                            m.then_inc(s3["scores"], 1)

                    def values(u, a):
                        for b in range(G):
                            k = G * a + b
                            m = pe.matmul(ps[:, 6, k * DH3:(k + 1) * DH3], pt[:, u % 2, k * S:(k + 1) * S],
                                          v3[:, u % 2, b * D + a * DH3:b * D + (a + 1) * DH3], start=True, stop=True)
                        if a:
                            m.then_inc(s3["pv"], 1)

                    project_q(0)
                    project_k(0)
                    project_v(0)
                    for step in range(IC3 + 3):
                        has_s, has_t, has_o, has_out = step < IC3, 0 < step <= IC3, 2 <= step < IC3 + 2, step >= 3
                        has_p = step + 1 < IC3
                        if has_s:
                            if step == 0:
                                pe.wait_ge(s3["k_col"], 1)
                            if step >= 2:
                                pe.wait_ge(s3["exps"], step - 1)
                            scores(step, 0)
                        if has_out:
                            u = step - 3
                            pe.wait_ge(s3["oT_ready"], u + 1)
                            for b in range(G):
                                m = pe.matmul(ps[:, 7, b * D:(b + 1) * D], oT3[:, u % 2, b * S:(b + 1) * S],
                                              o3_w[:, u, :], start=True, stop=True)
                            m.then_inc(s3["out_psum"], 1)
                        if has_s:
                            scores(step, 1)
                        if has_p:
                            if has_out:
                                pe.wait_ge(s3["chunk_added"], step - 2)
                            else:
                                pe.wait_ge(s3["v_row"], step + 1)
                            project_q(step + 1)
                        if has_t:
                            u = step - 1
                            pe.wait_ge(s3["exps"], u + 1)
                            if u >= 1:
                                pe.wait_ge(s3["p_hi"], u)
                                pe.wait_ge(s3["p_lo"], u)
                            for k in range(BLK):
                                m = pe.transpose(ps[:, 4 + k // 4, (k % 4) * S:(k % 4 + 1) * S],
                                                 pb[:, u % 2, k * S:(k + 1) * S], ident)
                                if k % 4 == 3:
                                    m.then_inc(s3["transposed"], 1)
                        if has_p:
                            project_k(step + 1)
                        if has_t:
                            u = step - 1
                            pe.wait_ge(s3["v_row"], u + 1)
                            pe.wait_ge(s3["p_hi"], u + 1)
                            if u >= 1:
                                pe.wait_ge(s3["normed"], u)
                            values(u, 0)
                        if has_p:
                            project_v(step + 1)
                        if has_t:
                            pe.wait_ge(s3["p_lo"], u + 1)
                            values(u, 1)
                        if has_o:
                            u = step - 2
                            pe.wait_ge(s3["normed"], u + 1)
                            if has_p:
                                pe.wait_ge(s3["v_row"], step + 2)
                            elif has_out:
                                pe.wait_ge(s3["chunk_added"], step - 2)
                            for b in range(G):
                                m = pe.transpose(ps[:, 7, b * P:(b + 1) * P], o3[:, u % 2, b * D:(b + 1) * D], ident)
                            m.then_inc(s3["oT_psum"], 1)
                    transpose_y_pe(pe, 4)
                    pe.wait_ge(yT_ready, 4)
                    router_pe(pe, W("rw3"))

                    def hidden(e):
                        for c in range(C3):
                            k = e * C3 + c
                            if k >= 2:
                                pe.wait_ge(moe["hid_dve"], k - 1)
                            pe.matmul(ps[:, 2 * (k % 2), :], f3[:, 0, e, c, :], yT[:, :], start=True, stop=True)
                            pe.matmul(ps[:, 2 * (k % 2) + 1, :], f3[:, 1, e, c, :], yT[:, :], start=True,
                                      stop=True).then_inc(moe["hid_psum"], 1)

                    hidden(0)
                    for e in range(NE3):
                        if e + 1 < NE3:
                            hidden(e + 1)
                        pe.wait_ge(moe["hid_dve"], C3 * (e + 1))
                        if e >= 2:
                            pe.wait_ge(moe["combined"], e - 1)
                        for b in range(G):
                            for c in range(C3):
                                m = pe.matmul(ps[:, 4 + e % 2, b * D:(b + 1) * D],
                                              hT[:, (e * C3 + c) % 8, b * S:(b + 1) * S], f3[:, 2, e, c, :],
                                              start=(c == 0), stop=(c == C3 - 1))
                        m.then_inc(moe["expert"], 1)

                @block.scalar
                def _(a):
                    a.activation(xg[:, :, :], x_all[:, bass.ts(i, G), :], ACT.Copy).then_inc(x_copied, 1)
                    attention_act(a, s2, 1, W("bq2"), W("bk2"), o)
                    copy_yT_act(a, 2, yT[:, :])
                    a.wait_ge(slot["hid_psum"], 1)
                    a.activation(gT, ps[0:HR, 0, :], ACT.Gelu, bias=c1[0:HR, :]).then_inc(slot["hid"], 1)
                    a.wait_ge(slot["shifted"], 1)
                    a.activation(slg, slg, ACT.Exp).then_inc(slot["exps"], 1)
                    a.wait_ge(slot["in_psum"], 1)
                    a.activation(siT, ps[:, 2, 0:256], ACT.Copy).then_inc(slot["in_ready"], 1)
                    a.wait_ge(slot["aT_psum"], 1)
                    a.activation(aT, ps[:, 4, 0:256].rearrange("p (q t) -> p q t", q=2), ACT.Copy)\
                        .then_inc(slot["aT"], 1)
                    a.wait_ge(slot["rz_in"], 1)
                    a.activation(rz, rz, ACT.Sigmoid).then_inc(slot["rz"], 1)
                    a.wait_ge(slot["n_in"], 1)
                    a.activation(xn, xn, ACT.Tanh).then_inc(slot["n"], 1)
                    a.wait_ge(slot["newT_psum"], 1)
                    a.activation(hnT, ps[:, 0, 0:256], ACT.Copy).then_inc(slot["newT"], 1)
                    a.wait_ge(slot["oT_psum"], 1)
                    a.activation(outT.rearrange("p (q a t) -> p a q t", q=2, a=2),
                                 ps[:, 2:4, 0:2 * S].rearrange("p a (q t) -> p a q t", q=2), ACT.Copy)\
                        .then_inc(slot["oT"], 1)
                    copy_yT_act(a, 3, yT[:, :])

                    def project_q(c):
                        a.wait_ge(s3["q_psum"], c + 1)
                        a.activation(q3[:, c % 2, :], ps[:, 7, :], ACT.Copy, scale=DH3 ** -0.5).then_inc(s3["q_col"], 1)

                    def project_v(c):
                        a.wait_ge(s3["v_psum"], c + 1)
                        if c >= 2:
                            a.wait_ge(s3["pv"], c - 1)
                        a.activation(v3[:, c % 2, :], ps[:, 7, :], ACT.Copy).then_inc(s3["v_row"], 1)

                    project_q(0)
                    project_v(0)
                    for step in range(IC3 + 2):
                        if step + 1 < IC3:
                            project_q(step + 1)
                        if 0 < step <= IC3:
                            u = step - 1
                            a.wait_ge(s3["transposed"], 2 * u + 1)
                            if u >= 2:
                                a.wait_ge(s3["pv"], u - 1)
                            a.activation(pt[:, u % 2, 0:512], ps[:, 4, :], ACT.Copy).then_inc(s3["p_hi"], 1)
                        if step < IC3:
                            u = step
                            a.wait_ge(s3["maxed"], u + 1)
                            if u >= 2:
                                a.wait_ge(s3["transposed"], 2 * (u - 1))
                                a.wait_ge(s3["o_recip"], u - 1)
                            src = ps[:, 2 * (u % 2):2 * (u % 2) + 2, :].rearrange("p a k -> p (a k)")
                            for k in range(BLK):
                                m = a.activation(pb[:, u % 2, k * S:(k + 1) * S], src[:, k * S:(k + 1) * S], ACT.Exp,
                                                 bias=nm[:, u % 2, k:k + 1], accum_out=sums[:, u % 2, k:k + 1])
                            m.then_inc(s3["exps"], 1)
                        if step + 1 < IC3:
                            project_v(step + 1)
                        if step >= 2:
                            u = step - 2
                            a.wait_ge(s3["oT_psum"], u + 1)
                            if u >= 2:
                                a.wait_ge(s3["out_psum"], u - 1)
                            a.activation(oT3[:, u % 2, :], ps[:, 7, :], ACT.Copy).then_inc(s3["oT_ready"], 1)
                    copy_yT_act(a, 4, yT[:, :])
                    router_act(a)
                    for k in range(NE3 * C3):
                        a.wait_ge(moe["hid_psum"], k + 1)
                        if k >= 2:
                            a.wait_ge(moe["hid_dve"], k - 1)
                        a.activation(u3[:, k % 2, :], ps[:, 2 * (k % 2), :], ACT.Silu).then_inc(moe["silu"], 1)
                    a.wait_ge(moe["combined"], NE3)
                    a.activation(x_all[:, bass.ts(i, G), :], xg[:, :, :], ACT.Copy).then_inc(x_kept, 1)

                @block.gpsimd
                def _(g):
                    values_pool(g, s2, o)
                    layernorm_pool(g, 1)
                    add_bias_pool(g, 1, "bo2").then_inc(s2["bias_added"], 1)
                    layernorm_pool(g, 2)
                    add_bias_pool(g, 2, "bos").then_inc(slot["bias_added"], 1)
                    layernorm_pool(g, 3)
                    add_bias_pool(g, 3, "bout3").then_inc(s3["bias_added"], 1)
                    layernorm_pool(g, 4)

                @block.vector
                def _(v):
                    link = linker(v, steps)
                    for m, c0, c1_ in ((P, 0, NC1 - 1), (CH1[-1][1], NC1 - 1, NC1)):
                        j = quantise(v, link, hq[0:m, c0:c1_, :], h_all[0:m, bass.ds(i * NC1 + c0, c1_ - c0), :],
                                     hT[0:m, c0:c1_, :], sc[0:m, 11:12])
                    j.then_inc(hq_ready, 1)
                    v.wait_ge(down_psum, 1)
                    link(v.tensor_tensor(r0[:, :, :], tiles(7), dscB[:, :].unsqueeze(1).to_broadcast([P, G, D]),
                                         ALU.mult))
                    v.wait_ge(x_copied, 1)
                    v.tensor_tensor(xg[:, :, :], xg[:, :, :], r0[:, :, :], ALU.add).then_inc(x_ready, 1)
                    attention_dve(v, s2, 1, "bv2", None, W("hms"))
                    v.wait_ge(s2["bias_added"], 1)
                    v.tensor_tensor(xg[:, :, :], tiles(7), xg[:, :, :], ALU.add).then_inc(x_ready, 1)
                    layernorm_dve(v, 2, lambda b: y[:, b, :])
                    v.wait_ge(slot["logits"], 1)
                    link(v.tensor_tensor(slg, tiles(1, SLOTS), row_bcast("b2s", G), ALU.add))
                    link(v.tensor_scalar(slg, slg, sc[:, 5:6], None, ALU.mult))
                    for b in range(G):
                        j = v.max(stop8[:, b, :], slg[:, b, :])
                    link(j)
                    for b in range(G):
                        j = v.match_replace(srep[:, b, :], stop8[:, b, :], slg[:, b, :], NEG)
                    link(j)
                    v.tensor_tensor(srep, srep, slg, ALU.not_equal)
                    v.tensor_tensor(slg, slg, stop8[:, :, 0:1].to_broadcast([P, G, SLOTS]), ALU.subtract)\
                        .then_inc(slot["shifted"], 1)
                    v.wait_ge(slot["exps"], 1)
                    link(v.tensor_tensor(alpha, slg, srep, ALU.mult))
                    link(v.tensor_reduce(srow[:, 0:G], alpha, AX, ALU.add))
                    link(v.reciprocal(srow[:, G:2 * G], srow[:, 0:G]))
                    v.tensor_tensor(alpha, alpha, srow[:, G:2 * G].unsqueeze(2).to_broadcast([P, G, SLOTS]),
                                    ALU.mult).then_inc(slot["alpha"], 1)
                    v.wait_ge(slot["wsum"], 1)
                    link(v.tensor_scalar(srow[:, 8:10], ps[:, 3, 0:2], 1e-8, None, ALU.add))
                    link(v.reciprocal(srow[:, 10:12], srow[:, 8:10]))
                    v.wait_ge(slot["gates_psum"], 1)
                    for q in range(2):
                        j = v.scalar_tensor_tensor(rz[:, q, :], ps[:, 5 + q, 0:2 * D], srow[:, 10 + q:11 + q],
                                                   crz[:, :], ALU.mult, ALU.add)
                    j.then_inc(slot["rz_in"], 1)
                    for q in range(2):
                        v.scalar_tensor_tensor(xn[:, q, :], ps[:, 5 + q, 2 * D:3 * D], srow[:, 10 + q:11 + q],
                                               R("bih")[:, 2 * D:3 * D], ALU.mult, ALU.add)
                    v.wait_ge(slot["rz"], 1)
                    both = [P, 2, D]
                    link(v.tensor_tensor(rz[:, :, 0:D], rz[:, :, 0:D], hn_c[:, :].unsqueeze(1).to_broadcast(both),
                                         ALU.mult))
                    v.tensor_tensor(xn, xn, rz[:, :, 0:D], ALU.add).then_inc(slot["n_in"], 1)
                    v.wait_ge(slot["n"], 1)
                    link(v.tensor_tensor(hnew, hs[:, :].unsqueeze(1).to_broadcast(both), xn, ALU.subtract))
                    link(v.tensor_tensor(hnew, hnew, rz[:, :, D:2 * D], ALU.mult))
                    v.tensor_tensor(hnew, hnew, xn, ALU.add).then_inc(slot["new"], 1)
                    v.wait_ge(slot["val_psum"], 1)
                    v.tensor_tensor(sval, ps[:, 1, 0:2 * D].rearrange("p (q d) -> p q d", q=2), row_bcast("bvs", 2),
                                    ALU.add).then_inc(slot["val"], 1)
                    v.wait_ge(slot["out_psum"], 1)
                    v.wait_ge(slot["bias_added"], 1)
                    v.tensor_tensor(xg[:, :, :], tiles(7), xg[:, :, :], ALU.add).then_inc(x_ready, 1)
                    layernorm_dve(v, 3, lambda b: y[:, b, :])

                    def project_k(c):
                        v.wait_ge(s3["k_psum"], c + 1)
                        v.tensor_copy(k3[:, c % 2, :], ps[:, 7, :]).then_inc(s3["k_col"], 1)

                    project_k(0)
                    for step in range(IC3 + 3):
                        if step >= 3:
                            u = step - 3
                            v.wait_ge(s3["out_psum"], u + 1)
                            v.wait_ge(s3["chunk_added"], u) if u else v.wait_ge(s3["bias_added"], 1)
                            j = v.tensor_tensor(xg[:, :, :], tiles(7), xg[:, :, :], ALU.add)
                            j.then_inc(s3["chunk_added"] if u < IC3 - 1 else x_ready, 1)
                        if step < IC3:
                            u = step
                            v.wait_ge(s3["scores"], u + 1)
                            if u >= 2:
                                v.wait_ge(s3["exps"], u - 1)
                            v.tensor_reduce(nm[:, u % 2, :], ps[:, 2 * (u % 2):2 * (u % 2) + 2, :].rearrange(
                                "p a (j k) -> p (a j) k", k=S), AX, ALU.max, negate=True).then_inc(s3["maxed"], 1)
                        if 0 < step <= IC3:
                            u = step - 1
                            v.wait_ge(s3["transposed"], 2 * u + 2)
                            if u >= 2:
                                v.wait_ge(s3["pv"], u - 1)
                            v.tensor_copy(pt[:, u % 2, 512:1024], ps[:, 5, :]).then_inc(s3["p_lo"], 1)
                        if step + 1 < IC3:
                            project_k(step + 1)
                        if 0 < step <= IC3:
                            v.wait_ge(s3["exps"], u + 1)
                            if u >= 1:
                                v.wait_ge(s3["normed"], u)
                            v.reciprocal(rc3, sums[:, u % 2, :]).then_inc(s3["o_recip"], 1)
                            v.wait_ge(s3["o_recip"], u + 1)
                            v.wait_ge(s3["pv"], u + 1)
                            if u >= 2:
                                v.wait_ge(s3["oT_psum"], u - 1)
                            v.tensor_tensor(o3[:, u % 2, :].rearrange("p (b a c) -> p a b c", b=G, a=2),
                                            ps[:, 6, :].rearrange("p (a b c) -> p a b c", a=2, b=G),
                                            rc3.rearrange("p (a b) -> p a b", a=2).unsqueeze(3)
                                            .to_broadcast([P, 2, G, DH3]), ALU.mult).then_inc(s3["normed"], 1)
                    layernorm_dve(v, 4, lambda b: y[:, b, :])
                    router_dve(v, link, "rb3")

                    def hidden(e):
                        for k in range(e * C3, (e + 1) * C3):
                            v.wait_ge(moe["silu"], k + 1)
                            if k >= 8:
                                v.wait_ge(moe["expert"], (k - 8) // C3 + 1)
                            v.tensor_tensor(hT[:, k % 8, :], ps[:, 2 * (k % 2) + 1, :], u3[:, k % 2, :], ALU.mult)\
                                .then_inc(moe["hid_dve"], 1)

                    hidden(0)
                    for e in range(NE3):
                        if e + 1 < NE3:
                            hidden(e + 1)
                        combine_dve(v, e, e < E3)

            next_iteration()

        with nc.Block() as block:
            @block.sync
            def _(sp):
                sp.wait_ge(out_stored, 16 * NG)


def pack(parts, names, height):
    return np.concatenate([np.asarray(parts[name], np.float32).reshape(height, -1) for name, _ in names], axis=1)


def kernel(**inputs):
    import concourse.bacc as bacc
    from concourse.bass_utils import run_bass_kernel_spmd

    a = {k: np.asarray(v) for k, v in inputs.items()}

    def col(v):
        return v.reshape(-1, 1)

    def pad(v):
        return np.concatenate([v, np.zeros((P - v.shape[0], v.shape[1]), v.dtype)], axis=0)

    h_of = np.arange(P) // DH % 4
    head = (h_of[:, None] == np.arange(4)[None, :]).astype(np.float32)
    below = np.tile((np.arange(E0)[None, :] < np.arange(E0)[:, None]).astype(np.float32).reshape(1, -1), (P, 1))
    parts = {
        "ident": np.eye(P, dtype=np.float32), "wo0": a["L0_xattn_wo_w"].T, "wr0": a["L0_ffn_Wr"],
        "b1_0": a["L0_ffn_b1"].reshape(E0 * C0, P).T, "b2_0": pad(a["L0_ffn_b2"]),
        "wq1": a["L1_xattn_wq"].T, "wk1": a["L1_xattn_wk"].T, "wv1": a["L1_xattn_wv"].T, "wo1": a["L1_xattn_wo"].T,
        "bq1": col(a["L1_xattn_bq"]), "bk1": col(a["L1_xattn_bk"]),
        "wq2": a["L2_xattn_Wq"], "wk2": a["L2_xattn_Wk"], "wv2": a["L2_xattn_Wv"], "wo2": a["L2_xattn_Wo"],
        "bq2": col(a["L2_xattn_bq"]), "bk2": col(a["L2_xattn_bk"]),
        "w1x": a["L2_ffn_w1"][:, :D].T, "w1m": a["L2_ffn_w1"][:, D:].T, "w2s": pad(a["L2_ffn_w2"].T),
        "b1s": pad(col(a["L2_ffn_b1"])), "wih": a["L2_ffn_gru_wih"].T, "whh": a["L2_ffn_gru_whh"].T,
        "wvs": a["L2_ffn_wv"].T, "wos": a["L2_ffn_wo"].T,
        "slot": np.tile(a["L2_ffn_slot_init"], (2, 1)), "slot_scale": np.tile(a["L2_ffn_slot_scale"], (2, 1)),
        "rw3": a["L3_ffn_rw"], "hm": head, "hms": head * np.float32(DH ** -0.5), "below": below,
    }
    rows = {
        "br0": a["L0_ffn_br"], "wo_b0": a["L0_xattn_wo_b"], "bv1": a["L1_xattn_bv"], "bo1": a["L1_xattn_bo"],
        "bv2": a["L2_xattn_bv"], "bo2": a["L2_xattn_bo"], "b2s": a["L2_ffn_b2"], "bih": a["L2_ffn_gru_bih"],
        "bhh": a["L2_ffn_gru_bhh"], "bvs": a["L2_ffn_bv"], "bos": a["L2_ffn_bo"], "bout3": a["L3_xattn_bout"],
        "rb3": a["L3_ffn_rb"], "clip_x": a["L1_ffn_clip_x"], "clip_down": a["L1_ffn_clip_down"],
        "tau": a["L2_ffn_tau"],
    }

    def down(v, chunks):
        return v.reshape(v.shape[0], chunks, P, v.shape[2]).transpose(2, 0, 1, 3).reshape(P, -1)

    def across(v):
        return v.transpose(1, 0, 2).reshape(P, -1)

    inner = IC3 * P
    e_in1 = np.concatenate([a["L3_ffn_ew1"], a["L3_ffn_sw1"][None]])
    e_in2 = np.concatenate([a["L3_ffn_ew2"], a["L3_ffn_sw2"][None]])
    e_out = np.concatenate([a["L3_ffn_ew3"], a["L3_ffn_sw3"][None]])
    arrays = {
        "x": a["x"], "ctx": a["ctx_1024"], "ctxT": a["ctx_1024"].reshape(B * S, D).T,
        "mask0": a["mask_Bx1xSxS2_ff0"].reshape(B, S, S), "mask1": a["mask_Bx1xSxS2_ik1"].reshape(B, S, S),
        "w": pack(parts, W_COLS, P), "rows": pack(rows, R_COLS, 1).reshape(-1),
        "big0": np.concatenate([across(a["L0_ffn_W1"]), down(a["L0_ffn_W2"], C0)], axis=1),
        "big3": np.concatenate([a["L3_xattn_Wq"], a["L3_xattn_Wkv"][:, :inner], a["L3_xattn_Wkv"][:, inner:],
                                down(a["L3_xattn_Wout"][None], IC3), across(e_in1), across(e_in2),
                                down(e_out, C3)], axis=1),
        "wg": a["L1_ffn_w_gate"], "wu": a["L1_ffn_w_up"], "wd": a["L1_ffn_w_down"],
    }
    arrays = {k: np.ascontiguousarray(v) for k, v in arrays.items()}
    nc = bacc.Bacc("TRN2", target_bir_lowering=False, num_devices=1)
    args = [nc.dram_tensor(f"in_{k}", v.shape, mybir.dt.from_np(v.dtype), kind="ExternalInput").ap()
            for k, v in arrays.items()]
    out = nc.dram_tensor("out", (B, S, D), F32, kind="ExternalOutput").ap()
    build(nc, *args, out)
    r = run_bass_kernel_spmd(nc, [{f"in_{k}": v for k, v in arrays.items()}], core_ids=[0])
    return r.results[0]["out"]
```

```python
from contextlib import ExitStack

import concourse.bass as bass
import numpy as np
from concourse import mybir

F32 = mybir.dt.float32
BF16 = mybir.dt.bfloat16
F16 = mybir.dt.float16
I32 = mybir.dt.int32
ALU = mybir.AluOpType
ACT = mybir.ActivationFunctionType
AX = mybir.AxisListType.X
RMAX = bass.bass_isa.ReduceOp.max

P = 128
B, S, D = 32, 128, 128
G = 4
NG = B // G
T = G * S
H = 16
DH = D // H
DH3 = 64
IC3 = H * DH3 // P
BLK = 8
NU = G * H // BLK
E0, HID0 = 8, 512
C0 = HID0 // P
E3, HID3 = 8, 256
C3 = HID3 // P
FF1 = 352
CH1 = [(0, 128), (128, 128), (256, 96)]
NC1 = len(CH1)
SLOTS, TOPS, HR = 64, 8, 64
EPS = 1e-5
MAGIC = 1.5 * 2.0 ** 23
QMAX = 127.0
NEG = -1.0e30
PSCALE = 2.0 ** 14

W_COLS = [("ident", 128), ("wo0", 128), ("wr0", E0), ("b1_0", E0 * C0), ("b2_0", 128),
          ("wq1", 128), ("wk1", 128), ("wv1", 128), ("wo1", 128), ("bq1", 1), ("bk1", 1),
          ("wq2", 128), ("wk2", 128), ("wv2", 128), ("wo2", 128), ("bq2", 1), ("bk2", 1),
          ("w1x", HR), ("w1m", HR), ("w2s", SLOTS), ("b1s", 1), ("wih", 3 * D), ("whh", 3 * D),
          ("wvs", 128), ("wos", 128), ("slot", 128), ("slot_scale", 1), ("rw3", E3),
          ("hm", 4), ("hms", 4), ("below", E0 * E0)]
R_COLS = [("br0", E0), ("wo_b0", D), ("bv1", D), ("bo1", D), ("bv2", D), ("bo2", D), ("b2s", SLOTS),
          ("bih", 3 * D), ("bhh", 3 * D), ("bvs", D), ("bos", D), ("bout3", D), ("rb3", E3),
          ("clip_x", 1), ("clip_down", 1), ("tau", 1)]


def places(cols):
    at, out = 0, {}
    for name, n in cols:
        out[name] = (at, n)
        at += n
    return out, at


W_AT, W_N = places(W_COLS)
R_AT, R_N = places(R_COLS)
BIG0 = 2 * E0 * HID0
BIG3 = 4 * IC3 * D + 3 * (E3 + 1) * HID3
NE3 = E3 + 1


def build(nc, x_d, ctx_d, ctxT_d, mask0_d, mask1_d, w_d, r_d, big0_d, big3_d, wg_d, wu_d, wd_d, out_d):
    with ExitStack() as stack:
        def sb(name, shape, dt=F32):
            return stack.enter_context(nc.sbuf_tensor(name, shape, dt))

        def sem(name):
            return stack.enter_context(nc.semaphore(name))

        x_all = sb("x_all", [P, B, D])
        h_all = sb("h_all", [P, NG * NC1, T])
        big = sb("big", [P, max(BIG0, BIG3)])
        w = sb("w", [P, W_N])
        rows = sb("rows", [P, R_N])
        wgq = sb("wgq", [P, FF1], BF16)
        wuq = sb("wuq", [P, FF1], BF16)
        wdq = sb("wdq", [P, NC1, D], BF16)
        gsc = sb("gsc", [P, NC1])
        usc = sb("usc", [P, NC1])
        dscB = sb("dscB", [P, D])
        identb = sb("identb", [P, P], BF16)
        ones = sb("ones", [P, P])
        half = sb("half", [P, G])
        sc = sb("sc", [P, 16])
        hmax = sb("hmax", [P, NG * NC1])
        ymax = sb("ymax", [P, NG])
        crz = sb("crz", [P, 2 * D])
        hn_c = sb("hn_c", [P, D])
        hs = sb("hs", [P, D])
        hsT = sb("hsT", [P, P])
        smean = sb("smean", [P, 1])
        c1 = sb("c1", [P, 1])
        xg = sb("xg", [P, G, D])
        xm = sb("xm", [P, G, D])
        yTm = sb("yTm", [P, T])
        spare = sb("spare", [P, 2, T])
        ctxT = sb("ctxT", [P, T])
        mask1i = sb("mask1i", [P, G, S], I32)
        y = sb("y", [P, G, D])
        yT = sb("yT", [P, T])
        qT = sb("qT", [P, T])
        qm = sb("qm", [P, 4, T])
        kT = sb("kT", [P, T])
        r0 = sb("r0", [P, G, D])
        va = sb("va", [P, G, H, 3, DH + 1], BF16)
        pb = sb("pb", [P, 2, BLK * S])
        pt = sb("pt", [P, 2, BLK * S])
        ctx = spare[:, 0, :].rearrange("p (b d) -> p b d", b=G)
        mask0 = spare[:, 1, :].rearrange("p (b k) -> p b k", b=G)
        u3 = spare
        mask1 = mask1i[:, :, :].bitcast(F32)
        pth = pt[:, :, :].bitcast(F16)
        on = sb("on", [P, BLK, DH + 1])
        rc = sb("rc", [P, BLK])
        nm = sb("nm", [P, 2, BLK])
        o = sb("o", [P, G, D])
        oT = sb("oT", [P, T])
        hT = sb("hT", [P, 8, T])
        lg = sb("lg", [P, G, E0])
        cmp_a = sb("cmp_a", [P, G, E0 * E0])
        cmp_b = sb("cmp_b", [P, G, E0 * E0])
        sel = sb("sel", [P, G, E0])
        gate = sb("gate", [P, G, E0])
        gs = sb("gs", [P, 4 * G])
        ps = stack.enter_context(nc.psum_tensor("ps", [P, 8, 512], F32))

        def W(name, p=P):
            a, n = W_AT[name]
            return w[0:p, a:a + n]

        def R(name):
            a, n = R_AT[name]
            return rows[:, a:a + n]

        def row_bcast(name, n):
            return R(name).unsqueeze(1).to_broadcast([P, n, R_AT[name][1]])

        def tiles(k, n=D):
            return ps[:, k, 0:G * n].rearrange("p (b n) -> p b n", b=G)

        ident = W("ident")
        w1_0 = big[:, 0:E0 * HID0].rearrange("p (e c m) -> p e c m", e=E0, c=C0)
        w2_0 = big[:, E0 * HID0:BIG0].rearrange("p (e c m) -> p e c m", e=E0, c=C0)
        q3_w, k3_w, v3_w, o3_w = (big[:, i * IC3 * D:(i + 1) * IC3 * D].rearrange("p (c m) -> p c m", c=IC3)
                                  for i in range(4))
        f3 = big[:, 4 * IC3 * D:BIG3].rearrange("p (w e c m) -> p w e c m", w=3, e=NE3, c=C3)

        small_loaded = sem("small_loaded")
        large_loaded = sem("large_loaded")
        out_stored = sem("out_stored")
        setup_v = sem("setup_v")
        w_rounded = sem("w_rounded")
        w_turned = sem("w_turned")
        diag_ready = sem("diag_ready")
        scales_psum = sem("scales_psum")
        slots_ready = sem("slots_ready")
        slots_psum = sem("slots_psum")
        setup_g = sem("setup_g")
        counted = []

        def isem(name):
            s = sem(name)
            counted.append(s)
            return s

        group_loaded = isem("group_loaded")
        group_loaded2 = isem("group_loaded2")

        class Stream:
            def __init__(self, name, x, y, yT):
                self.x, self.y, self.yT = x, y, yT
                self.x_ready = isem(f"x_ready_{name}")
                self.ln_stats = isem(f"ln_stats_{name}")
                self.ln_mean = isem(f"ln_mean_{name}")
                self.ln_var = isem(f"ln_var_{name}")
                self.ln_rstd = isem(f"ln_rstd_{name}")
                self.y_ready = isem(f"y_ready_{name}")
                self.yT_psum = isem(f"yT_psum_{name}")
                self.yT_ready = isem(f"yT_ready_{name}")
                self.st = sb(f"st_{name}", [P, G, 6])
                self.mv = sb(f"mv_{name}", [P, G, 2])
                self.ve = sb(f"ve_{name}", [P, G])
                self.rs = sb(f"rs_{name}", [P, G])

        front = Stream("front", xg, y, yT)
        gateT = yTm[0:E0, :]
        expert_y = hT[:, 7, :].rearrange("p (b d) -> p b d", b=G)
        experts = Stream("experts", xm, expert_y, yTm)
        x_kept = isem("x_kept")
        x_copied = isem("x_copied")
        hq_ready = isem("hq_ready")
        down_psum = isem("down_psum")
        steps = isem("steps")
        router_steps = isem("router_steps")

        def attention_sems(n):
            names = ["q_psum", "k_psum", "v_psum", "q_col", "k_col", "v_row", "v_hi", "v_rest", "v_mid", "v_ready",
                     "q_ready", "scores", "masked", "maxed", "exps", "transposed", "p_hi", "p_lo", "pv",
                     "o_read", "o_recip", "normed", "oT_psum", "oT_ready", "out_psum", "bias_added",
                     "chunk_added"]
            return {name: isem(f"{name}_{n}") for name in names}

        att_a = attention_sems("a")
        att_b = attention_sems("b")
        moe = {name: isem(f"moe_{name}") for name in
               ["logits", "logit_row", "shifted", "gate_exp", "gates", "gateT_psum", "gateT", "hid_psum",
                "hid_act", "hid_dve", "expert", "combined", "b2_psum", "silu"]}
        slot = {name: isem(f"slot_{name}") for name in
                ["hid_psum", "hid", "logits", "shifted", "exps", "alpha", "in_psum", "in_ready", "wsum", "aT_psum",
                 "aT", "gates_psum", "rz_in", "rz", "n_in", "n", "new", "newT_psum", "newT", "val_psum", "val",
                 "oT_psum", "oT", "out_psum", "bias_added"]}

        def linker(v, semaphore):
            count = [0]

            def link(m):
                count[0] += 1
                m.then_inc(semaphore, 1)
                v.wait_ge(semaphore, count[0])
            return link

        def layernorm_stats_dve(v, f, n):
            v.wait_ge(f.x_ready, n)
            for b in range(G):
                m = v.bn_stats(f.st[:, b, :], f.x[:, b, :])
            m.then_inc(f.ln_stats, 1)
            v.wait_ge(f.ln_stats, n)
            for b in range(G):
                m = v.bn_aggr(f.mv[:, b, :], f.st[:, b, :])
            m.then_inc(f.ln_mean, 1)
            v.wait_ge(f.ln_mean, n)
            v.tensor_scalar(f.ve[:, :], f.mv[:, :, 1], EPS, None, ALU.add).then_inc(f.ln_var, 1)

        def layernorm_pool(g, f, n):
            g.wait_ge(f.ln_var, n)
            g.tensor_tensor(f.rs[:, :], f.ve[:, :], half[:, :], ALU.pow).then_inc(f.ln_rstd, 1)

        def layernorm_apply_dve(v, f, n):
            v.wait_ge(f.ln_rstd, n)
            for b in range(G):
                m = v.tensor_scalar(f.y[:, b, :], f.x[:, b, :], f.mv[:, b, 0:1], f.rs[:, b:b + 1], ALU.subtract,
                                    ALU.mult)
            m.then_inc(f.y_ready, 1)

        def layernorm_dve(v, f, n):
            layernorm_stats_dve(v, f, n)
            layernorm_apply_dve(v, f, n)

        def transpose_y_pe(pe, f, n, bank):
            pe.wait_ge(f.y_ready, n)
            for b in range(G):
                m = pe.transpose(ps[:, bank, b * P:(b + 1) * P], f.y[:, b, :], ident)
            m.then_inc(f.yT_psum, 1)

        def copy_yT_act(a, f, n, bank, out):
            a.wait_ge(f.yT_psum, n)
            a.activation(out, ps[:, bank, :], ACT.Copy).then_inc(f.yT_ready, 1)

        def no_work(part, t):
            pass

        def project_kv_pe(pe, s, wk, wv):
            pe.matmul(ps[:, 2, :], wk, ctxT[:, :], start=True, stop=True).then_inc(s["k_psum"], 1)
            for b in range(G):
                m = pe.matmul(ps[:, 3, b * D:(b + 1) * D], ctxT[:, b * S:(b + 1) * S], wv, start=True, stop=True)
            m.then_inc(s["v_psum"], 1)

        def attention_pe(pe, s, f, n, k_in, wq, between):
            if wq is not None:
                pe.wait_ge(f.yT_ready, n)
                pe.matmul(ps[:, 0, :], wq, f.yT[:, :], start=True, stop=True).then_inc(s["q_psum"], 1)
                pe.wait_ge(s["k_col"], 1)
                pe.wait_ge(s["v_row"], 1)
            pe.wait_ge(s["q_ready"], 1)
            scores_used = s["exps"] if not s["has_mask"] else s["masked"]
            per_unit = 1 if s["has_mask"] else 2
            double = s["score_banks"][0] != s["score_banks"][1]
            for t in range(NU + 2):
                if t < NU:
                    b, c = divmod(t, 2)
                    before = t - 2 if double else t - 1
                    if before >= 0:
                        pe.wait_ge(scores_used, per_unit * (before + 1))
                    for k in range(BLK):
                        a, j = divmod(k, 4)
                        g = 2 * c + a
                        m = pe.matmul(ps[:, s["score_banks"][t % 2] + a, j * S:(j + 1) * S],
                                      qm[32 * g:32 * g + 32, j, b * S:(b + 1) * S],
                                      k_in[32 * g:32 * g + 32, b * S:(b + 1) * S], start=True, stop=True)
                    m.then_inc(s["scores"], 1)
                between(0, t)
                if 0 <= t - 1 < NU:
                    u = t - 1
                    if u >= 1:
                        pe.wait_ge(s["p_lo"], u)
                    for k in range(BLK):
                        if k % 4 == 0:
                            pe.wait_ge(s["exps"], 2 * u + 1 + k // 4)
                        m = pe.transpose(ps[:, 2 + k // 4, (k % 4) * S:(k % 4 + 1) * S],
                                         pb[:, u % 2, k * S:(k + 1) * S], ident)
                    m.then_inc(s["transposed"], 1)
                between(1, t)
                if t >= 2:
                    u = t - 2
                    b, c = divmod(u, 2)
                    if u == 0:
                        pe.wait_ge(s["v_ready"], 1)
                        if s["misc"] == 4:
                            pe.wait_ge(f.yT_ready, n)
                    pe.wait_ge(s["p_lo"], u + 1)
                    if u >= 1:
                        pe.wait_ge(s["o_read"], u)
                    for k in range(BLK):
                        for part in range(2):
                            m = pe.matmul(ps[:, 4, k * 27:(k + 1) * 27],
                                          pth[:, u % 2, part * BLK * S + k * S:part * BLK * S + (k + 1) * S],
                                          va[:, b, BLK * c + k, :, :].rearrange("p t d -> p (t d)"),
                                          start=(part == 0), stop=(part == 1))
                    m.then_inc(s["pv"], 1)
                between(2, t)

        def attention_out_pe(pe, s, wo):
            bank = s["misc"]
            pe.wait_ge(s["normed"], NU)
            for b in range(G):
                m = pe.transpose(ps[:, bank, b * P:(b + 1) * P], o[:, b, :], ident)
            m.then_inc(s["oT_psum"], 1)
            pe.wait_ge(s["oT_ready"], 1)
            for b in range(G):
                m = pe.matmul(ps[:, bank, b * D:(b + 1) * D], oT[:, b * S:(b + 1) * S], wo, start=True, stop=True)
            m.then_inc(s["out_psum"], 1)

        def keys_act(a, s, bk):
            a.wait_ge(s["k_psum"], 1)
            a.activation(kT[:, :], ps[:, 2, :], ACT.Identity, bias=bk).then_inc(s["k_col"], 1)

        def values_act(a, s, v_src):
            heads = v_src[:, :, :].rearrange("p b (h d) -> p (b h) d", h=H)
            rest = r0[:, :, :].rearrange("p b (h d) -> p (b h) d", h=H)
            parts = va[:, :, :, :, :].rearrange("p b h t d -> p (b h) t d")
            a.activation(parts[:, :, 0, 0:DH], heads, ACT.Copy).then_inc(s["v_hi"], 1)
            a.wait_ge(s["v_rest"], 1)
            a.activation(parts[:, :, 1, 0:DH], rest, ACT.Copy).then_inc(s["v_mid"], 1)

        def queries_act(a, s, f, n, bq):
            if bq is None:
                copy_yT_act(a, f, n, s["misc"], qT[:, :])
            else:
                copy_yT_act(a, f, n, s["misc"], f.yT[:, :])
                a.wait_ge(s["q_psum"], 1)
                a.activation(qT[:, :], ps[:, 0, :], ACT.Identity, bias=bq).then_inc(s["q_col"], 1)

        def attention_act(a, s, between):
            for t in range(NU + 2):
                between(0, t)
                if 1 <= t <= NU:
                    u = t - 1
                    a.wait_ge(s["transposed"], u + 1)
                    if u >= 2:
                        a.wait_ge(s["pv"], u - 1)
                    a.activation(pth[:, u % 2, 0:BLK * S], ps[:, 2:4, :].rearrange("p a k -> p (a k)"), ACT.Copy,
                                 scale=PSCALE).then_inc(s["p_hi"], 1)
                if t < NU:
                    u = t
                    a.wait_ge(s["maxed"], u + 1)
                    at = s["score_banks"][u % 2]
                    src = pb[:, u % 2, :] if s["has_mask"] else ps[:, at:at + 2, :].rearrange("p a k -> p (a k)")
                    for k in range(BLK):
                        m = a.activation(pb[:, u % 2, k * S:(k + 1) * S], src[:, k * S:(k + 1) * S], ACT.Exp,
                                         bias=nm[:, u % 2, k:k + 1])
                        if k % 4 == 3:
                            m.then_inc(s["exps"], 1)
                between(1, t)

        def attention_out_act(a, s):
            a.wait_ge(s["oT_psum"], 1)
            a.activation(oT[:, :], ps[:, s["misc"], :], ACT.Copy).then_inc(s["oT_ready"], 1)

        def values_pool(g, s, v_src):
            heads = v_src[:, :, :].rearrange("p b (h d) -> p (b h) d", h=H)
            rest = r0[:, :, :].rearrange("p b (h d) -> p (b h) d", h=H)
            parts = va[:, :, :, :, :].rearrange("p b h t d -> p (b h) t d")
            g.wait_ge(s["v_hi"], 1)
            g.tensor_tensor(rest, heads, parts[:, :, 0, 0:DH], ALU.subtract).then_inc(s["v_rest"], 1)
            g.wait_ge(s["v_mid"], 1)
            g.tensor_tensor(parts[:, :, 2, 0:DH], rest, parts[:, :, 1, 0:DH], ALU.subtract).then_inc(s["v_ready"], 1)

        def values_dve(v, s, bias_v):
            v.wait_ge(s["v_psum"], 1)
            v.tensor_tensor(o[:, :, :], tiles(3), row_bcast(bias_v, G), ALU.add).then_inc(s["v_row"], 1)

        def queries_dve(v, s, q_there, n, heads_mask):
            v.wait_ge(q_there, n)
            for j in range(4):
                m = v.tensor_scalar(qm[:, j, :], qT[:, :], heads_mask[:, j:j + 1], None, ALU.mult)
            m.then_inc(s["q_ready"], 1)

        def attention_dve(v, s, mask_op, o_was_values, between):
            for t in range(NU + 2):
                between(0, t)
                if t < NU:
                    u = t
                    b = u // 2
                    at = s["score_banks"][u % 2]
                    sc_ps = ps[:, at:at + 2, :].rearrange("p a (j k) -> p (a j) k", k=S)
                    v.wait_ge(s["scores"], u + 1)
                    if mask_op is not None:
                        if u >= 2:
                            v.wait_ge(s["transposed"], u - 1)
                        buf = pb[:, u % 2, :].rearrange("p (j k) -> p j k", k=S)
                        mask_op(v, buf, sc_ps, b).then_inc(s["masked"], 1)
                        v.wait_ge(s["masked"], u + 1)
                        sc_ps = buf
                    if u >= 2:
                        v.wait_ge(s["exps"], 2 * (u - 1))
                    v.tensor_reduce(nm[:, u % 2, :], sc_ps, AX, ALU.max, negate=True).then_inc(s["maxed"], 1)
                between(1, t)
                if 0 <= t - 1 < NU:
                    u = t - 1
                    v.wait_ge(s["p_hi"], u + 1)
                    v.scalar_tensor_tensor(pth[:, u % 2, BLK * S:2 * BLK * S], ps[:, 2:4, :].rearrange("p a k -> p (a k)"),
                                           PSCALE, pth[:, u % 2, 0:BLK * S], ALU.mult,
                                           ALU.subtract).then_inc(s["p_lo"], 1)
                between(2, t)
                if t >= 2:
                    u = t - 2
                    b, c = divmod(u, 2)
                    v.wait_ge(s["pv"], u + 1)
                    if u >= 1:
                        v.wait_ge(s["normed"], u)
                    v.tensor_reduce(on[:, :, :], ps[:, 4, 0:BLK * 27].rearrange("p (k t d) -> p k d t", k=BLK, t=3), AX,
                                    ALU.add).then_inc(s["o_read"], 1)
                    v.wait_ge(s["o_read"], u + 1)
                    v.reciprocal(rc[:, :], on[:, :, DH]).then_inc(s["o_recip"], 1)
                    v.wait_ge(s["o_recip"], u + 1)
                    if u == 0 and o_was_values:
                        v.wait_ge(s["v_ready"], 1)
                    v.tensor_tensor(o[:, b, c * 64:(c + 1) * 64].rearrange("p (k d) -> p k d", d=DH), on[:, :, 0:DH],
                                    rc[:, :].unsqueeze(2).to_broadcast([P, BLK, DH]), ALU.mult).then_inc(s["normed"], 1)

        def add_bias_pool(g, f, n, bias):
            g.wait_ge(f.y_ready, n)
            return g.tensor_tensor(f.x[:, :, :], f.x[:, :, :], row_bcast(bias, G), ALU.add)

        def router_pe(pe, wr):
            for b in range(G):
                m = pe.matmul(ps[:, 7, b * E0:(b + 1) * E0], yTm[:, b * S:(b + 1) * S], wr, start=True, stop=True)
            m.then_inc(moe["logits"], 1)

        def router_dve(v, link, bias):
            v.wait_ge(moe["logits"], 1)
            link(v.tensor_tensor(lg[:, :, :], tiles(7, E0), row_bcast(bias, G), ALU.add))
            other = lg[:, :, :].unsqueeze(2).to_broadcast([P, G, E0, E0])
            own = lg[:, :, :].unsqueeze(3).to_broadcast([P, G, E0, E0])
            ca = cmp_a[:, :, :].rearrange("p b (e f) -> p b e f", e=E0)
            cb = cmp_b[:, :, :].rearrange("p b (e f) -> p b e f", e=E0)
            v.tensor_tensor(ca, other, own, ALU.is_gt)
            v.tensor_reduce(gs[:, 0:G], lg[:, :, :], AX, ALU.max)
            link(v.tensor_tensor(cb, other, own, ALU.is_equal))
            link(v.tensor_tensor(cmp_b[:, :, :], cmp_b[:, :, :],
                                 W("below").unsqueeze(1).to_broadcast([P, G, E0 * E0]), ALU.mult))
            v.tensor_tensor(lg[:, :, :], lg[:, :, :], gs[:, 0:G].unsqueeze(2).to_broadcast([P, G, E0]),
                            ALU.subtract).then_inc(moe["shifted"], 1)
            link(v.tensor_tensor(cmp_a[:, :, :], cmp_a[:, :, :], cmp_b[:, :, :], ALU.add))
            link(v.tensor_reduce(sel[:, :, :], ca, AX, ALU.add))
            link(v.tensor_scalar(sel[:, :, :], sel[:, :, :], 2.0, None, ALU.is_lt))
            v.wait_ge(moe["gate_exp"], 1)
            link(v.tensor_tensor(gate[:, :, :], gate[:, :, :], sel[:, :, :], ALU.mult))
            link(v.tensor_reduce(gs[:, G:2 * G], gate[:, :, :], AX, ALU.add))
            link(v.reciprocal(gs[:, 2 * G:3 * G], gs[:, G:2 * G]))
            v.tensor_tensor(gate[:, :, :], gate[:, :, :], gs[:, 2 * G:3 * G].unsqueeze(2).to_broadcast([P, G, E0]),
                            ALU.mult).then_inc(moe["gates"], 1)
            v.wait_ge(moe["gates"], 1)

        def router_act(a):
            a.wait_ge(moe["shifted"], 1)
            a.activation(gate[:, :, :], lg[:, :, :], ACT.Exp).then_inc(moe["gate_exp"], 1)

        def expert_pe(pe, e, chunks, w_out):
            if e == 0:
                pe.wait_ge(moe["shifted"], 1)
            else:
                pe.wait_ge(moe["combined"], e)
            for b in range(G):
                for c in range(chunks):
                    m = pe.matmul(ps[:, 7, b * D:(b + 1) * D], hT[:, (e * chunks + c) % 8, b * S:(b + 1) * S],
                                  w_out[:, e, c, :], start=(c == 0), stop=(c == chunks - 1))
            m.then_inc(moe["expert"], 1)

        def combine_dve(v, e, gated):
            v.wait_ge(moe["expert"], e + 1)
            if e:
                v.wait_ge(moe["combined"], e)
            for b in range(G):
                m = v.scalar_tensor_tensor(xm[:, b, :], ps[:, 7, b * D:(b + 1) * D],
                                           gate[:, b, e:e + 1] if gated else 1.0, xm[:, b, :], ALU.mult, ALU.add)
            m.then_inc(moe["combined"], 1)

        def experts0_pe(pe, part, t):
            if part < 2 and t < E0:
                for c in (2 * part, 2 * part + 1):
                    k = t * C0 + c
                    if k >= 2:
                        pe.wait_ge(moe["hid_act" if k % 2 == 0 else "hid_dve"], k // 2)
                    pe.matmul(ps[:, 5 + k % 2, :], w1_0[:, t, c, :], yTm[:, :], start=True, stop=True)\
                        .then_inc(moe["hid_psum"], 1)
            if part == 2 and 1 <= t <= E0:
                pe.wait_ge(moe["hid_act"], 2 * t)
                pe.wait_ge(moe["hid_dve"], 2 * t)
                expert_pe(pe, t - 1, C0, w2_0)
            if part == 0 and t == E0:
                pe.wait_ge(moe["hid_act"], 2 * E0)
                for b in range(G):
                    m = pe.transpose(ps[0:E0, 5, b * S:(b + 1) * S], gate[:, b, :], ident)
                m.then_inc(moe["gateT_psum"], 1)
            if part == 1 and t == E0:
                pe.wait_ge(moe["gateT"], 1)
                pe.wait_ge(moe["hid_dve"], 2 * E0)
                for b in range(G):
                    m = pe.matmul(ps[:, 6, b * D:(b + 1) * D], gateT[:, b * S:(b + 1) * S], W("b2_0", E0),
                                  start=True, stop=True)
                m.then_inc(moe["b2_psum"], 1)

        def experts0_act(a, part, t):
            if t < E0:
                k = t * C0 + 2 * part
                a.wait_ge(moe["hid_psum"], k + 1)
                if k >= 8:
                    a.wait_ge(moe["expert"], (k - 8) // C0 + 1)
                a.activation(hT[:, k % 8, :], ps[:, 5, :], ACT.Relu, bias=W("b1_0")[:, k:k + 1])\
                    .then_inc(moe["hid_act"], 1)
            if t == 0 and part == 0:
                router_act(a)

        def experts0_dve(v, link, part, t):
            if part >= 1 and t < E0:
                k = t * C0 + 2 * part - 1
                v.wait_ge(moe["hid_psum"], k + 1)
                if k >= 8:
                    v.wait_ge(moe["expert"], (k - 8) // C0 + 1)
                v.tensor_scalar(hT[:, k % 8, :], ps[:, 6, :], W("b1_0")[:, k:k + 1], 0.0, ALU.add, ALU.max)\
                    .then_inc(moe["hid_dve"], 1)
            if part == 0 and t == 0:
                router_dve(v, link, "br0")
            if part == 1 and t == E0:
                v.wait_ge(moe["gateT_psum"], 1)
                v.tensor_copy(gateT[:, :], ps[0:E0, 5, :]).then_inc(moe["gateT"], 1)
            if part == 0 and 2 <= t <= E0 + 1:
                combine_dve(v, t - 2, True)

        n_small, n_large = 9, 2
        with nc.Block() as block:
            @block.sync
            def _(sp):
                sp.dma_start(w[:, :], w_d).then_inc(small_loaded, 16)
                sp.dma_start(rows[:, :], r_d.partition_broadcast(P)).then_inc(small_loaded, 16)
                for k, src in enumerate((wg_d, wu_d)):
                    for c, (at, m) in enumerate(CH1):
                        sp.dma_start(hT[0:m, 3 * k + c, 0:D], src[at:at + m, :]).then_inc(small_loaded, 16)
                sp.dma_start(hT[:, 6, 0:FF1], wd_d).then_inc(small_loaded, 16)
                sp.dma_start(x_all[:, :, :], x_d.rearrange("b s d -> s b d")).then_inc(large_loaded, 16)
                sp.dma_start(big[:, 0:BIG0], big0_d).then_inc(large_loaded, 16)
                sp.wait_ge(large_loaded, 16 * n_large)

            @block.gpsimd
            def _(g):
                g.memset(ones[:, :], 1.0)
                g.memset(half[:, :], -0.5)
                g.memset(hmax[:, :], 0.0)
                g.memset(va[:, :, :, :, :], 0.0).then_inc(setup_g, 1)
                g.wait_ge(setup_g, 1)
                g.memset(va[:, :, :, 0, DH:DH + 1], 1.0).then_inc(setup_g, 1)

            @block.vector
            def _(v):
                link = linker(v, setup_v)
                v.memset(gsc[:, :], 0.0)
                v.memset(usc[:, :], 0.0)
                v.wait_ge(small_loaded, 16 * n_small)
                v.tensor_copy(identb[:, :], ident).then_inc(w_rounded, 1)
                for t in range(7):
                    m, n = (P, FF1) if t == 6 else (CH1[t % 3][1], D)
                    src = hT[0:m, t, 0:n]
                    scale = usc[0:m, t - 3:t - 2] if 3 <= t < 6 else (gsc[0:m, t:t + 1] if t < 3 else sc[0:m, 0:1])
                    link(v.tensor_reduce(sc[0:m, 1:2], src, AX, ALU.max, apply_absolute_value=True))
                    link(v.tensor_scalar(scale, sc[0:m, 1:2], 1.0 / QMAX, None, ALU.mult))
                    link(v.reciprocal(sc[0:m, 2:3], scale))
                    link(v.tensor_scalar(src, src, sc[0:m, 2:3], MAGIC, ALU.mult, ALU.add))
                    link(v.tensor_scalar(src, src, MAGIC, None, ALU.subtract))
                    v.tensor_scalar(pt[0:m, t % 2, 0:192].bitcast(BF16)[:, 0:n], src, QMAX, -QMAX - 1.0,
                                    ALU.min, ALU.max).then_inc(w_rounded, 1)
                    v.wait_ge(w_turned, t + 1)
                    pw = ps[:, t, 0:256].bitcast(BF16)
                    if t < 3:
                        v.tensor_copy(wgq[:, CH1[t][0]:CH1[t][0] + m], pw[:, 0:m])
                    elif t < 6:
                        v.tensor_copy(wuq[:, CH1[t - 3][0]:CH1[t - 3][0] + m], pw[:, 0:m])
                    else:
                        for c, (at, mc) in enumerate(CH1):
                            v.tensor_copy(wdq[0:mc, c, :], pw[0:mc, c * P:(c + 1) * P])
                v.tensor_scalar(hT[:, 7, 0:P], ident, sc[:, 0:1], None, ALU.mult).then_inc(diag_ready, 1)
                v.wait_ge(scales_psum, 1)
                v.tensor_copy(dscB[:, :], ps[:, 7, 0:P])
                link(v.tensor_scalar(sc[:, 4:5], R("tau"), -1.0, None, ALU.mult))
                link(v.tensor_tensor(sc[:, 4:5], sc[:, 4:5], R("tau"), ALU.max))
                link(v.tensor_scalar(sc[:, 4:5], sc[:, 4:5], 0.1, None, ALU.add))
                v.reciprocal(sc[:, 5:6], sc[:, 4:5])
                v.tensor_scalar(hs[:, :], W("slot"), W("slot_scale"), None, ALU.mult).then_inc(slots_ready, 1)
                v.wait_ge(slots_psum, 1)
                v.tensor_copy(hsT[:, :], ps[:, 1, 0:P])
                v.tensor_scalar(smean[:, :], ps[:, 2, 0:1], 1.0 / SLOTS, None, ALU.mult).then_inc(slots_ready, 1)
                v.wait_ge(slots_psum, 2)
                v.tensor_tensor(c1[0:HR, :], ps[0:HR, 3, 0:1], W("b1s", HR), ALU.add)
                link(v.tensor_tensor(crz[:, :], ps[:, 4, 0:2 * D], R("bhh")[:, 0:2 * D], ALU.add))
                v.tensor_tensor(crz[:, :], crz[:, :], R("bih")[:, 0:2 * D], ALU.add)
                v.tensor_tensor(hn_c[:, :], ps[:, 4, 2 * D:3 * D], R("bhh")[:, 2 * D:3 * D], ALU.add)

            @block.tensor
            def _(pe):
                for t in range(7):
                    pe.wait_ge(w_rounded, 1 + t + 1)
                    m = P if t == 6 else CH1[t % 3][1]
                    pw = ps[:, t, 0:256].bitcast(BF16)
                    src = pt[0:m, t % 2, 0:192].bitcast(BF16)
                    if t < 6:
                        i = pe.transpose(pw[:, 0:m], src[:, 0:D], identb[0:m, 0:m])
                    else:
                        for c, (at, mc) in enumerate(CH1):
                            i = pe.transpose(pw[0:mc, c * P:(c + 1) * P], src[:, at:at + mc], identb[:, :])
                    i.then_inc(w_turned, 1)
                pe.wait_ge(setup_g, 1)
                pe.wait_ge(diag_ready, 1)
                pe.matmul(ps[:, 7, 0:P], ones[:, :], hT[:, 7, 0:P], start=True, stop=True).then_inc(scales_psum, 1)
                pe.wait_ge(slots_ready, 1)
                pe.transpose(ps[:, 1, 0:P], hs[:, :], ident)
                pe.matmul(ps[:, 2, 0:1], hs[0:SLOTS, :], ones[0:SLOTS, 0:1], start=True, stop=True)\
                    .then_inc(slots_psum, 1)
                pe.wait_ge(slots_ready, 2)
                pe.matmul(ps[0:HR, 3, 0:1], W("w1m"), smean[:, :], start=True, stop=True)
                pe.matmul(ps[:, 4, 0:3 * D], hsT[:, :], W("whh"), start=True, stop=True).then_inc(slots_psum, 1)

            @block.scalar
            def _(a):
                a.wait_ge(small_loaded, 16 * n_small)
                a.activation(sc[:, 6:7], R("clip_x"), ACT.Sigmoid)
                a.activation(sc[:, 7:8], R("clip_down"), ACT.Sigmoid)

        first, last = counted[0].num, counted[-1].num
        assert [s.num for s in counted] == list(range(first, last + 1))

        def next_iteration():
            nc.gpsimd.sem_clear(range(first, last + 1))
            nc.all_engine_barrier()

        def mask0_add(v, out, scores, b):
            return v.tensor_tensor(out, scores, mask0[:, b, :].unsqueeze(1).to_broadcast([P, BLK, S]), ALU.add)

        def mask1_clip(v, out, scores, b):
            return v.scalar_tensor_tensor(out, scores, -100.0, mask1[:, b, :].unsqueeze(1).to_broadcast([P, BLK, S]),
                                          ALU.max, ALU.min)

        beside_experts = dict(score_banks=(0, 0), misc=4)
        alone = dict(score_banks=(0, 5), misc=7)
        s0, s1 = dict(att_a, has_mask=True, **beside_experts), dict(att_b, has_mask=True, **alone)
        ctx_rows = ctx_d.rearrange("b s d -> s b d")
        mask0_rows = mask0_d.rearrange("b s d -> s b d")
        mask1_rows = mask1_d.rearrange("b s d -> s b d")

        def x_group(g):
            return x_all[:, bass.ds(g * G, G), :]

        def iteration_a(gf, gm):
            with nc.Block() as block:
                @block.sync
                def _(sp):
                    if gf is not None:
                        sp.dma_start(ctxT[:, :], ctxT_d[:, bass.ds(gf * T, T)]).then_inc(group_loaded, 16)
                        sp.dma_start(ctx[:, :, :], ctx_rows[:, bass.ds(gf * G, G), :]).then_inc(group_loaded, 16)
                        sp.dma_start(mask0[:, :, :], mask0_rows[:, bass.ds(gf * G, G), :]).then_inc(group_loaded, 16)
                        sp.wait_ge(group_loaded, 48)
                    if gm is not None:
                        sp.dma_start(mask1i[:, :, :], mask1_rows[:, bass.ds(gm * G, G), :]).then_inc(group_loaded2, 16)
                        if gf is not None:
                            sp.wait_ge(s0["scores"], NU)
                        sp.dma_start(ctxT[:, :], ctxT_d[:, bass.ds(gm * T, T)]).then_inc(group_loaded2, 16)
                        sp.wait_ge(group_loaded2, 32)

                @block.tensor
                def _(pe):
                    if gm is not None:
                        transpose_y_pe(pe, experts, 1, 7)
                    if gf is not None:
                        transpose_y_pe(pe, front, 1, 4)
                    if gm is not None:
                        pe.wait_ge(experts.yT_ready, 1)
                        router_pe(pe, W("wr0"))
                    between = no_work if gm is None else lambda part, t: experts0_pe(pe, part, t)
                    if gf is not None:
                        pe.wait_ge(group_loaded, 48)
                        attention_pe(pe, s0, front, 1, ctxT, None, between)
                    else:
                        for t in range(E0 + 1):
                            for part in range(3):
                                between(part, t)
                    if gm is not None:
                        pe.wait_ge(group_loaded2, 32)
                        project_kv_pe(pe, s1, W("wk1"), W("wv1"))
                    if gf is not None:
                        attention_out_pe(pe, s0, W("wo0"))
                    if gm is not None:
                        transpose_y_pe(pe, experts, 2, 7)
                        if gf is not None:
                            pe.wait_ge(front.x_ready, 2)
                        attention_pe(pe, s1, experts, 2, kT, W("wq1"), no_work)
                        attention_out_pe(pe, s1, W("wo1"))

                @block.scalar
                def _(a):
                    if gm is not None:
                        a.activation(xm[:, :, :], x_group(gm), ACT.Copy).then_inc(experts.x_ready, 1)
                    if gf is not None:
                        a.activation(xg[:, :, :], x_group(gf), ACT.Copy).then_inc(front.x_ready, 1)
                        a.wait_ge(group_loaded, 48)
                        values_act(a, s0, ctx)
                    if gm is not None:
                        copy_yT_act(a, experts, 1, 7, yTm[:, :])
                    if gf is not None:
                        queries_act(a, s0, front, 1, None)
                    between = no_work if gm is None else lambda part, t: experts0_act(a, part, t)
                    if gf is not None:
                        attention_act(a, s0, between)
                    else:
                        for t in range(E0):
                            for part in range(2):
                                between(part, t)
                    if gm is not None:
                        keys_act(a, s1, W("bk1"))
                    if gf is not None:
                        attention_out_act(a, s0)
                    if gm is not None:
                        a.wait_ge(s1["v_row"], 1)
                        values_act(a, s1, o)
                        queries_act(a, s1, experts, 2, W("bq1"))
                    if gf is not None:
                        a.wait_ge(front.x_ready, 2)
                        a.activation(x_group(gf), xg[:, :, :], ACT.Copy)
                    if gm is not None:
                        attention_act(a, s1, no_work)
                        attention_out_act(a, s1)
                        a.wait_ge(experts.x_ready, 3)
                        a.activation(x_group(gm), xm[:, :, :], ACT.Copy)

                @block.gpsimd
                def _(g):
                    if gm is not None:
                        layernorm_pool(g, experts, 1)
                    if gf is not None:
                        layernorm_pool(g, front, 1)
                        values_pool(g, s0, ctx)
                    if gm is not None:
                        layernorm_pool(g, experts, 2)
                        values_pool(g, s1, o)
                        add_bias_pool(g, experts, 2, "bo1").then_inc(s1["bias_added"], 1)
                        layernorm_pool(g, experts, 3)

                @block.vector
                def _(v):
                    if gm is not None:
                        layernorm_stats_dve(v, experts, 1)
                    if gf is not None:
                        layernorm_stats_dve(v, front, 1)
                    if gm is not None:
                        layernorm_apply_dve(v, experts, 1)
                    if gf is not None:
                        layernorm_apply_dve(v, front, 1)
                        queries_dve(v, s0, front.yT_ready, 1, W("hm"))
                    link = linker(v, router_steps)
                    between = no_work if gm is None else lambda part, t: experts0_dve(v, link, part, t)
                    if gf is not None:
                        v.wait_ge(group_loaded, 48)
                        attention_dve(v, s0, mask0_add, False, between)
                    else:
                        for t in range(E0 + 2):
                            for part in range(3):
                                between(part, t)
                    if gm is not None:
                        v.wait_ge(moe["b2_psum"], 1)
                        v.wait_ge(moe["combined"], E0)
                        v.tensor_tensor(xm[:, :, :], tiles(6), xm[:, :, :], ALU.add).then_inc(experts.x_ready, 1)
                        layernorm_dve(v, experts, 2)
                    if gf is not None:
                        v.wait_ge(s0["out_psum"], 1)
                        v.tensor_tensor(r0[:, :, :], tiles(4), row_bcast("wo_b0", G), ALU.add).then_inc(s0["v_row"], 1)
                        v.wait_ge(s0["v_row"], 1)
                        v.scalar_tensor_tensor(xg[:, :, :], r0[:, :, :], 0.0, xg[:, :, :], ALU.max, ALU.add)\
                            .then_inc(front.x_ready, 1)
                    if gm is not None:
                        if gf is not None:
                            v.wait_ge(s0["oT_psum"], 1)
                            v.wait_ge(front.x_ready, 2)
                        values_dve(v, s1, "bv1")
                        link = linker(v, steps)
                        v.wait_ge(group_loaded2, 32)
                        link(v.tensor_scalar(mask1[:, :, :], mask1i[:, :, :], 0.0, NEG, ALU.is_equal, ALU.mult))
                        link(v.tensor_scalar(mask1[:, :, :], mask1[:, :, :], 100.0, None, ALU.add))
                        queries_dve(v, s1, s1["q_col"], 1, W("hms"))
                        attention_dve(v, s1, mask1_clip, True, no_work)
                        v.wait_ge(s1["bias_added"], 1)
                        v.wait_ge(s1["out_psum"], 1)
                        v.tensor_tensor(xm[:, :, :], tiles(7), xm[:, :, :], ALU.add).then_inc(experts.x_ready, 1)
                        layernorm_dve(v, experts, 3)
                        v.wait_ge(experts.y_ready, 3)
                        y3 = expert_y.rearrange("p b d -> p (b d)")
                        v.tensor_copy(h_all[:, bass.ds(gm * NC1, 1), :], y3.unsqueeze(1))
                        v.tensor_reduce(ymax[:, bass.ds(gm, 1)], y3, AX, ALU.max, apply_absolute_value=True)

            next_iteration()

        iteration_a(0, None)
        with nc.Fori(1, NG) as i:
            iteration_a(i, i - 1)
        iteration_a(None, NG - 1)

        with nc.Block() as block:
            @block.vector
            def _(v):
                v.tensor_reduce(sc[:, 8:9], ymax[:, :], AX, ALU.max).then_inc(steps, 1)
                v.wait_ge(setup_g, 3)
                v.tensor_scalar(sc[:, 10:11], sc[:, 9:10], 1.0 / QMAX, sc[:, 6:7], ALU.mult, ALU.mult).then_inc(steps, 1)
                v.wait_ge(steps, 2)
                v.reciprocal(sc[:, 11:12], sc[:, 10:11])
                v.tensor_scalar(gsc[:, :], gsc[:, :], sc[:, 10:11], None, ALU.mult)
                v.tensor_scalar(usc[:, :], usc[:, :], sc[:, 10:11], None, ALU.mult).then_inc(steps, 1)
                v.wait_ge(steps, 3)

            @block.gpsimd
            def _(g):
                g.wait_ge(steps, 1)
                g.partition_all_reduce(sc[:, 9:10], sc[:, 8:9], P, RMAX).then_inc(setup_g, 1)

            @block.sync
            def _(sp):
                sp.dma_start(big[:, 0:BIG3], big3_d).then_inc(large_loaded, 16)

        next_iteration()

        def quantise(v, link, out, src, tmp, rscale):
            link(v.tensor_scalar(tmp, src, rscale, QMAX, ALU.mult, ALU.min))
            link(v.tensor_scalar(tmp, tmp, -QMAX - 1.0, MAGIC, ALU.max, ALU.add))
            return v.tensor_scalar(out, tmp, MAGIC, None, ALU.subtract)

        xq = pt[:, 0, 0:256].bitcast(BF16).rearrange("p (b d) -> p b d", b=G)
        xqT = pt[:, 1, 0:256].bitcast(BF16)
        with nc.Fori(0, NG) as i:
            with nc.Block() as block:
                @block.tensor
                def _(pe):
                    pe.wait_ge(front.y_ready, 1)
                    t_out = ps[:, 7, 0:256].bitcast(BF16)
                    for b in range(G):
                        m = pe.transpose(t_out[:, b * P:(b + 1) * P], xq[:, b, :], identb[:, :])
                    m.then_inc(front.yT_psum, 1)
                    pe.wait_ge(front.yT_ready, 1)
                    for c, (at, m) in enumerate(CH1):
                        pe.matmul(ps[0:m, c, :], wgq[:, at:at + m], xqT, start=True, stop=True)
                        pe.matmul(ps[0:m, 3 + c, :], wuq[:, at:at + m], xqT, start=True, stop=True)\
                            .then_inc(moe["hid_psum"], 1)

                @block.scalar
                def _(a):
                    a.wait_ge(front.yT_psum, 1)
                    a.activation(xqT, ps[:, 7, 0:256].bitcast(BF16), ACT.Copy).then_inc(front.yT_ready, 1)
                    for c, (at, m) in enumerate(CH1):
                        a.wait_ge(moe["hid_psum"], c + 1)
                        a.activation(hT[0:m, c, :], ps[0:m, c, :], ACT.Silu, scale=gsc[0:m, c:c + 1])\
                            .then_inc(moe["silu"], 1)

                @block.vector
                def _(v):
                    link = linker(v, steps)
                    quantise(v, link, xq.rearrange("p b d -> p (b d)").unsqueeze(1), h_all[:, bass.ds(i * NC1, 1), :],
                             y[:, :, :].rearrange("p b d -> p (b d)").unsqueeze(1), sc[:, 11:12]).then_inc(front.y_ready, 1)
                    for c, (at, m) in enumerate(CH1):
                        v.wait_ge(moe["silu"], c + 1)
                        v.scalar_tensor_tensor(hT[0:m, 4 + c, :], ps[0:m, 3 + c, :], usc[0:m, c:c + 1], hT[0:m, c, :],
                                               ALU.mult, ALU.mult).then_inc(moe["hid_dve"], 1)
                        v.wait_ge(moe["hid_dve"], c + 1)
                        v.tensor_copy(h_all[0:m, bass.ds(i * NC1 + c, 1), :], hT[0:m, 4 + c, :].unsqueeze(1))
                        v.tensor_reduce(hmax[0:m, bass.ds(i * NC1 + c, 1)], hT[0:m, 4 + c, :], AX, ALU.max,
                                        apply_absolute_value=True)

            next_iteration()

        with nc.Block() as block:
            @block.vector
            def _(v):
                v.tensor_reduce(sc[:, 8:9], hmax[:, :], AX, ALU.max).then_inc(steps, 1)
                v.wait_ge(setup_g, 4)
                v.tensor_scalar(sc[:, 10:11], sc[:, 9:10], 1.0 / QMAX, sc[:, 7:8], ALU.mult, ALU.mult).then_inc(steps, 1)
                v.wait_ge(steps, 2)
                v.reciprocal(sc[:, 11:12], sc[:, 10:11])
                v.tensor_scalar(dscB[:, :], dscB[:, :], sc[:, 10:11], None, ALU.mult).then_inc(steps, 1)
                v.wait_ge(steps, 3)

            @block.gpsimd
            def _(g):
                g.wait_ge(steps, 1)
                g.partition_all_reduce(sc[:, 9:10], sc[:, 8:9], P, RMAX).then_inc(setup_g, 1)

            @block.sync
            def _(sp):
                sp.wait_ge(large_loaded, 16 * (n_large + 1))

        next_iteration()

        s2 = dict(att_a, has_mask=False, **beside_experts)
        s3 = att_b
        hq = pt[:, 0, 0:768].bitcast(BF16).rearrange("p (c t) -> p c t", c=NC1)
        pc = [buf[:, n, k:k + T] for buf in (pb, pt) for n in range(2) for k in (0, T)]
        gT = pc[0][0:HR, :]
        slg = pc[1][:, 0:G * SLOTS].rearrange("p (b s) -> p b s", b=G)
        srep = pc[1][:, G * SLOTS:2 * G * SLOTS].rearrange("p (b s) -> p b s", b=G)
        alpha = pc[2][:, 0:G * SLOTS].rearrange("p (b s) -> p b s", b=G)
        stop8 = pc[2][:, 256:256 + G * 8].rearrange("p (b s) -> p b s", b=G)
        srow = pc[2][:, 288:304]
        siT = pc[3][:, 0:256]
        aT = pc[3][:, 256:512].rearrange("p (q t) -> p q t", q=2)
        rz = pc[4][:, :].rearrange("p (q n) -> p q n", q=2)
        xn = pc[5][:, 0:256].rearrange("p (q n) -> p q n", q=2)
        hnew = pc[5][:, 256:512].rearrange("p (q n) -> p q n", q=2)
        hnT = pc[6][:, 0:256]
        sval = pc[6][:, 256:512].rearrange("p (q n) -> p q n", q=2)
        outT = pc[7][:, :]
        q3 = qm[:, 0:2, :]
        k3 = qm[:, 2:4, :]
        v3 = hT[:, 0:2, :]
        o3 = hT[:, 2:4, :]
        oT3 = hT[:, 4:6, :]
        sums = hT[:, 6, 0:2 * BLK].rearrange("p (u k) -> p u k", u=2)
        rc3 = hT[:, 6, 16:16 + BLK]

        def experts3_pe(pe, part, t):
            if part < 2 and t < NE3:
                k = t * C3 + part
                if k >= 1:
                    pe.wait_ge(moe["silu"], k)
                pe.matmul(ps[:, 5, :], f3[:, 0, t, part, :], yTm[:, :], start=True, stop=True)
                if k >= 1:
                    pe.wait_ge(moe["hid_dve"], k)
                pe.matmul(ps[:, 6, :], f3[:, 1, t, part, :], yTm[:, :], start=True, stop=True)\
                    .then_inc(moe["hid_psum"], 1)
            if part == 2 and 1 <= t <= NE3:
                pe.wait_ge(moe["hid_dve"], C3 * t)
                expert_pe(pe, t - 1, C3, f3[:, 2])

        def experts3_act(a, part, t):
            if t < NE3:
                k = t * C3 + part
                a.wait_ge(moe["hid_psum"], k + 1)
                if k >= 2:
                    a.wait_ge(moe["hid_dve"], k - 1)
                a.activation(u3[:, k % 2, :], ps[:, 5, :], ACT.Silu).then_inc(moe["silu"], 1)
            if t == 0 and part == 0:
                router_act(a)

        def experts3_dve(v, link, part, t):
            if part >= 1 and t < NE3:
                k = t * C3 + part - 1
                v.wait_ge(moe["silu"], k + 1)
                if k >= 8:
                    v.wait_ge(moe["expert"], (k - 8) // C3 + 1)
                v.tensor_tensor(hT[:, k % 8, :], ps[:, 6, :], u3[:, k % 2, :], ALU.mult).then_inc(moe["hid_dve"], 1)
            if part == 0 and t == 0:
                router_dve(v, link, "rb3")
            if part == 0 and 2 <= t <= NE3 + 1:
                combine_dve(v, t - 2, t - 2 < E3)

        def iteration_c(gf, gm):
            front_too, experts_too = gf is not None, gm is not None
            with nc.Block() as block:
                @block.sync
                def _(sp):
                    if front_too:
                        sp.dma_start(ctxT[:, :], ctxT_d[:, bass.ds(gf * T, T)]).then_inc(group_loaded, 16)
                        sp.wait_ge(group_loaded, 16)
                    if experts_too:
                        sp.wait_ge(x_kept, 1)
                        sp.dma_start(out_d.rearrange("b s d -> s b d")[:, bass.ds(gm * G, G), :], x_group(gm))\
                            .then_inc(out_stored, 16)

                @block.tensor
                def _(pe):
                    between = no_work if not experts_too else lambda part, t: experts3_pe(pe, part, t)
                    if experts_too:
                        transpose_y_pe(pe, experts, 1, 7)
                    if not front_too:
                        pe.wait_ge(experts.yT_ready, 1)
                        router_pe(pe, W("rw3"))
                        for t in range(NE3 + 1):
                            for part in range(3):
                                between(part, t)
                        return
                    pe.wait_ge(hq_ready, 1)
                    for b in range(G):
                        for c, (at, m) in enumerate(CH1):
                            j = pe.matmul(ps[:, 4, b * D:(b + 1) * D], hq[0:m, c, b * S:(b + 1) * S], wdq[0:m, c, :],
                                          start=(c == 0), stop=(c == NC1 - 1))
                    j.then_inc(down_psum, 1)
                    if experts_too:
                        pe.wait_ge(experts.yT_ready, 1)
                        router_pe(pe, W("rw3"))
                    pe.wait_ge(group_loaded, 16)
                    project_kv_pe(pe, s2, W("wk2"), W("wv2"))
                    transpose_y_pe(pe, front, 1, 4)
                    attention_pe(pe, s2, front, 1, kT, W("wq2"), between)
                    attention_out_pe(pe, s2, W("wo2"))
                    transpose_y_pe(pe, front, 2, 4)
                    pe.wait_ge(front.yT_ready, 2)
                    pe.matmul(ps[0:HR, 0, :], W("w1x"), yT[:, :], start=True, stop=True).then_inc(slot["hid_psum"], 1)
                    pe.wait_ge(slot["hid"], 1)
                    for b in range(G):
                        m = pe.matmul(ps[:, 1, b * SLOTS:(b + 1) * SLOTS], gT[:, b * S:(b + 1) * S], W("w2s", HR),
                                      start=True, stop=True)
                    m.then_inc(slot["logits"], 1)
                    pe.wait_ge(slot["alpha"], 1)
                    for b in range(G):
                        m = pe.matmul(ps[:, 2, b * SLOTS:(b + 1) * SLOTS], y[:, b, :], alpha[:, b, :], start=True,
                                      stop=True)
                    m.then_inc(slot["in_psum"], 1)
                    for b in range(G):
                        q, a = divmod(b, 2)
                        m = pe.matmul(ps[64 * a:64 * a + 64, 1, q:q + 1], alpha[:, b, :], ones[:, 0:1], start=True,
                                      stop=True)
                    m.then_inc(slot["wsum"], 1)
                    for q in range(2):
                        m = pe.transpose(ps[:, 4, q * P:(q + 1) * P],
                                         alpha[:, 2 * q:2 * q + 2, :].rearrange("p b s -> p (b s)"), ident)
                    m.then_inc(slot["aT_psum"], 1)
                    pe.wait_ge(slot["in_ready"], 1)
                    for q in range(2):
                        m = pe.matmul(ps[:, 2 + q, 0:3 * D], siT[:, q * P:(q + 1) * P], W("wih"), start=True, stop=True)
                    m.then_inc(slot["gates_psum"], 1)
                    pe.wait_ge(slot["new"], 1)
                    for q in range(2):
                        m = pe.transpose(ps[:, 0, q * P:(q + 1) * P], hnew[:, q, :], ident)
                    m.then_inc(slot["newT_psum"], 1)
                    pe.wait_ge(slot["newT"], 1)
                    for q in range(2):
                        m = pe.matmul(ps[:, 1, q * D:(q + 1) * D], hnT[:, q * P:(q + 1) * P], W("wvs"), start=True,
                                      stop=True)
                    m.then_inc(slot["val_psum"], 1)
                    pe.wait_ge(slot["val"], 1)
                    pe.wait_ge(slot["aT"], 1)
                    for b in range(G):
                        q, a = divmod(b, 2)
                        m = pe.matmul(ps[:, 2 + a, q * S:(q + 1) * S], sval[64 * a:64 * a + 64, q, :],
                                      aT[64 * a:64 * a + 64, q, :], start=True, stop=True)
                    m.then_inc(slot["oT_psum"], 1)
                    pe.wait_ge(slot["oT"], 1)
                    for b in range(G):
                        m = pe.matmul(ps[:, 4, b * D:(b + 1) * D], outT[:, b * S:(b + 1) * S], W("wos"), start=True,
                                      stop=True)
                    m.then_inc(slot["out_psum"], 1)
                    if experts_too:
                        pe.wait_ge(moe["combined"], NE3)
                    transpose_y_pe(pe, front, 3, 7)
                    pe.wait_ge(front.yT_ready, 3)

                    def project_q(c):
                        pe.matmul(ps[:, 7, :], q3_w[:, c, :], yT[:, :], start=True, stop=True).then_inc(s3["q_psum"], 1)

                    def project_k(c):
                        pe.wait_ge(s3["q_col"], c + 1)
                        pe.matmul(ps[:, 7, :], k3_w[:, c, :], ctxT[:, :], start=True, stop=True)\
                            .then_inc(s3["k_psum"], 1)

                    def project_v(c):
                        pe.wait_ge(s3["k_col"], c + 1)
                        for b in range(G):
                            m = pe.matmul(ps[:, 7, b * D:(b + 1) * D], ctxT[:, b * S:(b + 1) * S], v3_w[:, c, :],
                                          start=True, stop=True)
                        m.then_inc(s3["v_psum"], 1)

                    def scores(u, a):
                        for b in range(G):
                            m = pe.matmul(ps[:, 2 * (u % 2) + a, b * S:(b + 1) * S],
                                          q3[64 * a:64 * a + 64, u % 2, b * S:(b + 1) * S],
                                          k3[64 * a:64 * a + 64, u % 2, b * S:(b + 1) * S], start=True, stop=True)
                        if a:
                            m.then_inc(s3["scores"], 1)

                    def values(u, a):
                        for b in range(G):
                            k = G * a + b
                            m = pe.matmul(ps[:, 6, k * DH3:(k + 1) * DH3], pt[:, u % 2, k * S:(k + 1) * S],
                                          v3[:, u % 2, b * D + a * DH3:b * D + (a + 1) * DH3], start=True, stop=True)
                        if a:
                            m.then_inc(s3["pv"], 1)

                    project_q(0)
                    project_k(0)
                    project_v(0)
                    for step in range(IC3 + 3):
                        has_s, has_t, has_o, has_out = step < IC3, 0 < step <= IC3, 2 <= step < IC3 + 2, step >= 3
                        has_p = step + 1 < IC3
                        if has_s:
                            if step == 0:
                                pe.wait_ge(s3["k_col"], 1)
                            if step >= 2:
                                pe.wait_ge(s3["exps"], step - 1)
                            scores(step, 0)
                        if has_out:
                            u = step - 3
                            pe.wait_ge(s3["oT_ready"], u + 1)
                            for b in range(G):
                                m = pe.matmul(ps[:, 7, b * D:(b + 1) * D], oT3[:, u % 2, b * S:(b + 1) * S],
                                              o3_w[:, u, :], start=True, stop=True)
                            m.then_inc(s3["out_psum"], 1)
                        if has_s:
                            scores(step, 1)
                        if has_p:
                            if has_out:
                                pe.wait_ge(s3["chunk_added"], step - 2)
                            else:
                                pe.wait_ge(s3["v_row"], step + 1)
                            project_q(step + 1)
                        if has_t:
                            u = step - 1
                            pe.wait_ge(s3["exps"], u + 1)
                            if u >= 1:
                                pe.wait_ge(s3["p_hi"], u)
                                pe.wait_ge(s3["p_lo"], u)
                            for k in range(BLK):
                                m = pe.transpose(ps[:, 4 + k // 4, (k % 4) * S:(k % 4 + 1) * S],
                                                 pb[:, u % 2, k * S:(k + 1) * S], ident)
                                if k % 4 == 3:
                                    m.then_inc(s3["transposed"], 1)
                        if has_p:
                            project_k(step + 1)
                        if has_t:
                            u = step - 1
                            pe.wait_ge(s3["v_row"], u + 1)
                            pe.wait_ge(s3["p_hi"], u + 1)
                            if u >= 1:
                                pe.wait_ge(s3["normed"], u)
                            values(u, 0)
                        if has_p:
                            project_v(step + 1)
                        if has_t:
                            pe.wait_ge(s3["p_lo"], u + 1)
                            values(u, 1)
                        if has_o:
                            u = step - 2
                            pe.wait_ge(s3["normed"], u + 1)
                            if has_p:
                                pe.wait_ge(s3["v_row"], step + 2)
                            elif has_out:
                                pe.wait_ge(s3["chunk_added"], step - 2)
                            for b in range(G):
                                m = pe.transpose(ps[:, 7, b * P:(b + 1) * P], o3[:, u % 2, b * D:(b + 1) * D], ident)
                            m.then_inc(s3["oT_psum"], 1)

                @block.scalar
                def _(a):
                    between = no_work if not experts_too else lambda part, t: experts3_act(a, part, t)
                    if experts_too:
                        a.activation(xm[:, :, :], x_group(gm), ACT.Copy).then_inc(experts.x_ready, 1)
                    if front_too:
                        a.activation(xg[:, :, :], x_group(gf), ACT.Copy).then_inc(x_copied, 1)
                    if experts_too:
                        copy_yT_act(a, experts, 1, 7, yTm[:, :])
                    if not front_too:
                        for t in range(NE3):
                            for part in range(2):
                                between(part, t)
                        a.wait_ge(moe["combined"], NE3)
                        a.activation(x_group(gm), xm[:, :, :], ACT.Copy).then_inc(x_kept, 1)
                        return
                    keys_act(a, s2, W("bk2"))
                    a.wait_ge(s2["v_row"], 1)
                    values_act(a, s2, o)
                    queries_act(a, s2, front, 1, W("bq2"))
                    attention_act(a, s2, between)
                    attention_out_act(a, s2)
                    copy_yT_act(a, front, 2, 4, yT[:, :])
                    a.wait_ge(slot["hid_psum"], 1)
                    a.activation(gT, ps[0:HR, 0, :], ACT.Gelu, bias=c1[0:HR, :]).then_inc(slot["hid"], 1)
                    a.wait_ge(slot["shifted"], 1)
                    a.activation(slg, slg, ACT.Exp).then_inc(slot["exps"], 1)
                    a.wait_ge(slot["in_psum"], 1)
                    a.activation(siT, ps[:, 2, 0:256], ACT.Copy).then_inc(slot["in_ready"], 1)
                    a.wait_ge(slot["aT_psum"], 1)
                    a.activation(aT, ps[:, 4, 0:256].rearrange("p (q t) -> p q t", q=2), ACT.Copy)\
                        .then_inc(slot["aT"], 1)
                    a.wait_ge(slot["rz_in"], 1)
                    a.activation(rz, rz, ACT.Sigmoid).then_inc(slot["rz"], 1)
                    a.wait_ge(slot["n_in"], 1)
                    a.activation(xn, xn, ACT.Tanh).then_inc(slot["n"], 1)
                    a.wait_ge(slot["newT_psum"], 1)
                    a.activation(hnT, ps[:, 0, 0:256], ACT.Copy).then_inc(slot["newT"], 1)
                    a.wait_ge(slot["oT_psum"], 1)
                    a.activation(outT.rearrange("p (q a t) -> p a q t", q=2, a=2),
                                 ps[:, 2:4, 0:2 * S].rearrange("p a (q t) -> p a q t", q=2), ACT.Copy)\
                        .then_inc(slot["oT"], 1)
                    if experts_too:
                        a.wait_ge(moe["combined"], NE3)
                        a.activation(x_group(gm), xm[:, :, :], ACT.Copy).then_inc(x_kept, 1)
                    copy_yT_act(a, front, 3, 7, yT[:, :])

                    def project_q(c):
                        a.wait_ge(s3["q_psum"], c + 1)
                        a.activation(q3[:, c % 2, :], ps[:, 7, :], ACT.Copy, scale=DH3 ** -0.5).then_inc(s3["q_col"], 1)

                    def project_v(c):
                        a.wait_ge(s3["v_psum"], c + 1)
                        if c >= 2:
                            a.wait_ge(s3["pv"], c - 1)
                        a.activation(v3[:, c % 2, :], ps[:, 7, :], ACT.Copy).then_inc(s3["v_row"], 1)

                    project_q(0)
                    project_v(0)
                    for step in range(IC3 + 2):
                        if step + 1 < IC3:
                            project_q(step + 1)
                        if 0 < step <= IC3:
                            u = step - 1
                            a.wait_ge(s3["transposed"], 2 * u + 1)
                            if u >= 2:
                                a.wait_ge(s3["pv"], u - 1)
                            a.activation(pt[:, u % 2, 0:512], ps[:, 4, :], ACT.Copy).then_inc(s3["p_hi"], 1)
                        if step < IC3:
                            u = step
                            a.wait_ge(s3["maxed"], u + 1)
                            if u >= 2:
                                a.wait_ge(s3["transposed"], 2 * (u - 1))
                                a.wait_ge(s3["o_recip"], u - 1)
                            src = ps[:, 2 * (u % 2):2 * (u % 2) + 2, :].rearrange("p a k -> p (a k)")
                            for k in range(BLK):
                                m = a.activation(pb[:, u % 2, k * S:(k + 1) * S], src[:, k * S:(k + 1) * S], ACT.Exp,
                                                 bias=nm[:, u % 2, k:k + 1], accum_out=sums[:, u % 2, k:k + 1])
                            m.then_inc(s3["exps"], 1)
                        if step + 1 < IC3:
                            project_v(step + 1)
                        if step >= 2:
                            u = step - 2
                            a.wait_ge(s3["oT_psum"], u + 1)
                            if u >= 2:
                                a.wait_ge(s3["out_psum"], u - 1)
                            a.activation(oT3[:, u % 2, :], ps[:, 7, :], ACT.Copy).then_inc(s3["oT_ready"], 1)
                    a.wait_ge(front.x_ready, 4)
                    a.activation(x_group(gf), xg[:, :, :], ACT.Copy)

                @block.gpsimd
                def _(g):
                    if experts_too:
                        layernorm_pool(g, experts, 1)
                    if not front_too:
                        return
                    layernorm_pool(g, front, 1)
                    values_pool(g, s2, o)
                    add_bias_pool(g, front, 1, "bo2").then_inc(s2["bias_added"], 1)
                    layernorm_pool(g, front, 2)
                    add_bias_pool(g, front, 2, "bos").then_inc(slot["bias_added"], 1)
                    layernorm_pool(g, front, 3)
                    add_bias_pool(g, front, 3, "bout3").then_inc(s3["bias_added"], 1)

                @block.vector
                def _(v):
                    link = linker(v, router_steps)
                    between = no_work if not experts_too else lambda part, t: experts3_dve(v, link, part, t)
                    if experts_too:
                        layernorm_dve(v, experts, 1)
                    if not front_too:
                        for t in range(NE3 + 2):
                            for part in range(3):
                                between(part, t)
                        return
                    slink = linker(v, steps)
                    for m, c0, c1_ in ((P, 0, NC1 - 1), (CH1[-1][1], NC1 - 1, NC1)):
                        j = quantise(v, slink, hq[0:m, c0:c1_, :], h_all[0:m, bass.ds(gf * NC1 + c0, c1_ - c0), :],
                                     hT[0:m, c0:c1_, :], sc[0:m, 11:12])
                    j.then_inc(hq_ready, 1)
                    v.wait_ge(down_psum, 1)
                    slink(v.tensor_tensor(r0[:, :, :], tiles(4), dscB[:, :].unsqueeze(1).to_broadcast([P, G, D]),
                                         ALU.mult))
                    v.wait_ge(x_copied, 1)
                    v.tensor_tensor(xg[:, :, :], xg[:, :, :], r0[:, :, :], ALU.add).then_inc(front.x_ready, 1)
                    layernorm_stats_dve(v, front, 1)
                    values_dve(v, s2, "bv2")
                    layernorm_apply_dve(v, front, 1)
                    queries_dve(v, s2, s2["q_col"], 1, W("hms"))
                    attention_dve(v, s2, None, True, between)
                    between(0, NU + 2)
                    v.wait_ge(s2["bias_added"], 1)
                    v.wait_ge(s2["out_psum"], 1)
                    v.tensor_tensor(xg[:, :, :], tiles(4), xg[:, :, :], ALU.add).then_inc(front.x_ready, 1)
                    layernorm_dve(v, front, 2)
                    v.wait_ge(slot["logits"], 1)
                    slink(v.tensor_tensor(slg, tiles(1, SLOTS), row_bcast("b2s", G), ALU.add))
                    slink(v.tensor_scalar(slg, slg, sc[:, 5:6], None, ALU.mult))
                    for b in range(G):
                        j = v.max(stop8[:, b, :], slg[:, b, :])
                    slink(j)
                    for b in range(G):
                        j = v.match_replace(srep[:, b, :], stop8[:, b, :], slg[:, b, :], NEG)
                    slink(j)
                    v.tensor_tensor(srep, srep, slg, ALU.not_equal)
                    v.tensor_tensor(slg, slg, stop8[:, :, 0:1].to_broadcast([P, G, SLOTS]), ALU.subtract)\
                        .then_inc(slot["shifted"], 1)
                    v.wait_ge(slot["exps"], 1)
                    slink(v.tensor_tensor(alpha, slg, srep, ALU.mult))
                    slink(v.tensor_reduce(srow[:, 0:G], alpha, AX, ALU.add))
                    slink(v.reciprocal(srow[:, G:2 * G], srow[:, 0:G]))
                    v.tensor_tensor(alpha, alpha, srow[:, G:2 * G].unsqueeze(2).to_broadcast([P, G, SLOTS]),
                                    ALU.mult).then_inc(slot["alpha"], 1)
                    v.wait_ge(slot["wsum"], 1)
                    slink(v.tensor_scalar(srow[:, 8:10], ps[:, 1, 0:2], 1e-8, None, ALU.add))
                    slink(v.reciprocal(srow[:, 10:12], srow[:, 8:10]))
                    v.wait_ge(slot["gates_psum"], 1)
                    for q in range(2):
                        j = v.scalar_tensor_tensor(rz[:, q, :], ps[:, 2 + q, 0:2 * D], srow[:, 10 + q:11 + q],
                                                   crz[:, :], ALU.mult, ALU.add)
                    j.then_inc(slot["rz_in"], 1)
                    for q in range(2):
                        v.scalar_tensor_tensor(xn[:, q, :], ps[:, 2 + q, 2 * D:3 * D], srow[:, 10 + q:11 + q],
                                               R("bih")[:, 2 * D:3 * D], ALU.mult, ALU.add)
                    v.wait_ge(slot["rz"], 1)
                    both = [P, 2, D]
                    slink(v.tensor_tensor(rz[:, :, 0:D], rz[:, :, 0:D], hn_c[:, :].unsqueeze(1).to_broadcast(both),
                                         ALU.mult))
                    v.tensor_tensor(xn, xn, rz[:, :, 0:D], ALU.add).then_inc(slot["n_in"], 1)
                    v.wait_ge(slot["n"], 1)
                    slink(v.tensor_tensor(hnew, hs[:, :].unsqueeze(1).to_broadcast(both), xn, ALU.subtract))
                    slink(v.tensor_tensor(hnew, hnew, rz[:, :, D:2 * D], ALU.mult))
                    v.tensor_tensor(hnew, hnew, xn, ALU.add).then_inc(slot["new"], 1)
                    v.wait_ge(slot["val_psum"], 1)
                    v.tensor_tensor(sval, ps[:, 1, 0:2 * D].rearrange("p (q d) -> p q d", q=2), row_bcast("bvs", 2),
                                    ALU.add).then_inc(slot["val"], 1)
                    v.wait_ge(slot["out_psum"], 1)
                    v.wait_ge(slot["bias_added"], 1)
                    v.tensor_tensor(xg[:, :, :], tiles(4), xg[:, :, :], ALU.add).then_inc(front.x_ready, 1)
                    layernorm_dve(v, front, 3)

                    def project_k(c):
                        v.wait_ge(s3["k_psum"], c + 1)
                        v.tensor_copy(k3[:, c % 2, :], ps[:, 7, :]).then_inc(s3["k_col"], 1)

                    project_k(0)
                    for step in range(IC3 + 3):
                        if step >= 3:
                            u = step - 3
                            v.wait_ge(s3["out_psum"], u + 1)
                            v.wait_ge(s3["chunk_added"], u) if u else v.wait_ge(s3["bias_added"], 1)
                            j = v.tensor_tensor(xg[:, :, :], tiles(7), xg[:, :, :], ALU.add)
                            j.then_inc(s3["chunk_added"] if u < IC3 - 1 else front.x_ready, 1)
                        if step < IC3:
                            u = step
                            v.wait_ge(s3["scores"], u + 1)
                            if u >= 2:
                                v.wait_ge(s3["exps"], u - 1)
                            v.tensor_reduce(nm[:, u % 2, :], ps[:, 2 * (u % 2):2 * (u % 2) + 2, :].rearrange(
                                "p a (j k) -> p (a j) k", k=S), AX, ALU.max, negate=True).then_inc(s3["maxed"], 1)
                        if 0 < step <= IC3:
                            u = step - 1
                            v.wait_ge(s3["transposed"], 2 * u + 2)
                            if u >= 2:
                                v.wait_ge(s3["pv"], u - 1)
                            v.tensor_copy(pt[:, u % 2, 512:1024], ps[:, 5, :]).then_inc(s3["p_lo"], 1)
                        if step + 1 < IC3:
                            project_k(step + 1)
                        if 0 < step <= IC3:
                            v.wait_ge(s3["exps"], u + 1)
                            if u >= 1:
                                v.wait_ge(s3["normed"], u)
                            v.reciprocal(rc3, sums[:, u % 2, :]).then_inc(s3["o_recip"], 1)
                            v.wait_ge(s3["o_recip"], u + 1)
                            v.wait_ge(s3["pv"], u + 1)
                            if u >= 2:
                                v.wait_ge(s3["oT_psum"], u - 1)
                            v.tensor_tensor(o3[:, u % 2, :].rearrange("p (b a c) -> p a b c", b=G, a=2),
                                            ps[:, 6, :].rearrange("p (a b c) -> p a b c", a=2, b=G),
                                            rc3.rearrange("p (a b) -> p a b", a=2).unsqueeze(3)
                                            .to_broadcast([P, 2, G, DH3]), ALU.mult).then_inc(s3["normed"], 1)

            next_iteration()

        iteration_c(0, None)
        with nc.Fori(1, NG) as i:
            iteration_c(i, i - 1)
        iteration_c(None, NG - 1)

        with nc.Block() as block:
            @block.sync
            def _(sp):
                sp.wait_ge(out_stored, 16 * NG)


def pack(parts, names, height):
    return np.concatenate([np.asarray(parts[name], np.float32).reshape(height, -1) for name, _ in names], axis=1)


def kernel(**inputs):
    import concourse.bacc as bacc
    from concourse.bass_utils import run_bass_kernel_spmd

    a = {k: np.asarray(v) for k, v in inputs.items()}

    def col(v):
        return v.reshape(-1, 1)

    def pad(v):
        return np.concatenate([v, np.zeros((P - v.shape[0], v.shape[1]), v.dtype)], axis=0)

    h_of = np.arange(P) // DH % 4
    head = (h_of[:, None] == np.arange(4)[None, :]).astype(np.float32)
    below = np.tile((np.arange(E0)[None, :] < np.arange(E0)[:, None]).astype(np.float32).reshape(1, -1), (P, 1))
    parts = {
        "ident": np.eye(P, dtype=np.float32), "wo0": a["L0_xattn_wo_w"].T, "wr0": a["L0_ffn_Wr"],
        "b1_0": a["L0_ffn_b1"].reshape(E0 * C0, P).T, "b2_0": pad(a["L0_ffn_b2"]),
        "wq1": a["L1_xattn_wq"].T, "wk1": a["L1_xattn_wk"].T, "wv1": a["L1_xattn_wv"].T, "wo1": a["L1_xattn_wo"].T,
        "bq1": col(a["L1_xattn_bq"]), "bk1": col(a["L1_xattn_bk"]),
        "wq2": a["L2_xattn_Wq"], "wk2": a["L2_xattn_Wk"], "wv2": a["L2_xattn_Wv"], "wo2": a["L2_xattn_Wo"],
        "bq2": col(a["L2_xattn_bq"]), "bk2": col(a["L2_xattn_bk"]),
        "w1x": a["L2_ffn_w1"][:, :D].T, "w1m": a["L2_ffn_w1"][:, D:].T, "w2s": pad(a["L2_ffn_w2"].T),
        "b1s": pad(col(a["L2_ffn_b1"])), "wih": a["L2_ffn_gru_wih"].T, "whh": a["L2_ffn_gru_whh"].T,
        "wvs": a["L2_ffn_wv"].T, "wos": a["L2_ffn_wo"].T,
        "slot": np.tile(a["L2_ffn_slot_init"], (2, 1)), "slot_scale": np.tile(a["L2_ffn_slot_scale"], (2, 1)),
        "rw3": a["L3_ffn_rw"], "hm": head, "hms": head * np.float32(DH ** -0.5), "below": below,
    }
    rows = {
        "br0": a["L0_ffn_br"], "wo_b0": a["L0_xattn_wo_b"], "bv1": a["L1_xattn_bv"], "bo1": a["L1_xattn_bo"],
        "bv2": a["L2_xattn_bv"], "bo2": a["L2_xattn_bo"], "b2s": a["L2_ffn_b2"], "bih": a["L2_ffn_gru_bih"],
        "bhh": a["L2_ffn_gru_bhh"], "bvs": a["L2_ffn_bv"], "bos": a["L2_ffn_bo"], "bout3": a["L3_xattn_bout"],
        "rb3": a["L3_ffn_rb"], "clip_x": a["L1_ffn_clip_x"], "clip_down": a["L1_ffn_clip_down"],
        "tau": a["L2_ffn_tau"],
    }

    def down(v, chunks):
        return v.reshape(v.shape[0], chunks, P, v.shape[2]).transpose(2, 0, 1, 3).reshape(P, -1)

    def across(v):
        return v.transpose(1, 0, 2).reshape(P, -1)

    inner = IC3 * P
    e_in1 = np.concatenate([a["L3_ffn_ew1"], a["L3_ffn_sw1"][None]])
    e_in2 = np.concatenate([a["L3_ffn_ew2"], a["L3_ffn_sw2"][None]])
    e_out = np.concatenate([a["L3_ffn_ew3"], a["L3_ffn_sw3"][None]])
    arrays = {
        "x": a["x"], "ctx": a["ctx_1024"], "ctxT": a["ctx_1024"].reshape(B * S, D).T,
        "mask0": a["mask_Bx1xSxS2_ff0"].reshape(B, S, S), "mask1": a["mask_Bx1xSxS2_ik1"].reshape(B, S, S),
        "w": pack(parts, W_COLS, P), "rows": pack(rows, R_COLS, 1).reshape(-1),
        "big0": np.concatenate([across(a["L0_ffn_W1"]), down(a["L0_ffn_W2"], C0)], axis=1),
        "big3": np.concatenate([a["L3_xattn_Wq"], a["L3_xattn_Wkv"][:, :inner], a["L3_xattn_Wkv"][:, inner:],
                                down(a["L3_xattn_Wout"][None], IC3), across(e_in1), across(e_in2),
                                down(e_out, C3)], axis=1),
        "wg": a["L1_ffn_w_gate"], "wu": a["L1_ffn_w_up"], "wd": a["L1_ffn_w_down"],
    }
    arrays = {k: np.ascontiguousarray(v) for k, v in arrays.items()}
    nc = bacc.Bacc("TRN2", target_bir_lowering=False, num_devices=1)
    args = [nc.dram_tensor(f"in_{k}", v.shape, mybir.dt.from_np(v.dtype), kind="ExternalInput").ap()
            for k, v in arrays.items()]
    out = nc.dram_tensor("out", (B, S, D), F32, kind="ExternalOutput").ap()
    build(nc, *args, out)
    r = run_bass_kernel_spmd(nc, [{f"in_{k}": v for k, v in arrays.items()}], core_ids=[0])
    return r.results[0]["out"]
```

```python
from contextlib import ExitStack

import concourse.bass as bass
import numpy as np
from concourse import mybir

F32 = mybir.dt.float32
BF16 = mybir.dt.bfloat16
F16 = mybir.dt.float16
I32 = mybir.dt.int32
ALU = mybir.AluOpType
ACT = mybir.ActivationFunctionType
AX = mybir.AxisListType.X
RMAX = bass.bass_isa.ReduceOp.max

P = 128
B, S, D = 32, 128, 128
G = 4
NG = B // G
T = G * S
H = 16
DH = D // H
DH3 = 64
IC3 = H * DH3 // P
BLK = 8
NU = G * H // BLK
E0, HID0 = 8, 512
C0 = HID0 // P
E3, HID3 = 8, 256
C3 = HID3 // P
FF1 = 352
CH1 = [(0, 128), (128, 128), (256, 96)]
NC1 = len(CH1)
UNROLL_B = 4
SLOTS, TOPS, HR = 64, 8, 64
EPS = 1e-5
MAGIC = 1.5 * 2.0 ** 23
QMAX = 127.0
NEG = -1.0e30
PSCALE = 2.0 ** 14

W_COLS = [("ident", 128), ("wo0", 128), ("wr0", E0), ("b1_0", E0 * C0), ("b2_0", 128),
          ("wq1", 128), ("wk1", 128), ("wv1", 128), ("wo1", 128), ("bq1", 1), ("bk1", 1),
          ("wq2", 128), ("wk2", 128), ("wv2", 128), ("wo2", 128), ("bq2", 1), ("bk2", 1),
          ("w1x", HR), ("w1m", HR), ("w2s", SLOTS), ("b1s", 1), ("wih", 3 * D), ("whh", 3 * D),
          ("wvs", 128), ("wos", 128), ("slot", 128), ("slot_scale", 1), ("rw3", E3),
          ("hm", 4), ("hms", 4), ("hg", 4), ("below", E0 * E0)]
R_COLS = [("br0", E0), ("wo_b0", D), ("bv1", D), ("bo1", D), ("bv2", D), ("bo2", D), ("b2s", SLOTS),
          ("bih", 3 * D), ("bhh", 3 * D), ("bvs", D), ("bos", D), ("bout3", D), ("rb3", E3),
          ("clip_x", 1), ("clip_down", 1), ("tau", 1)]

PE_PLACES = (1, 2)
ACT_PLACES = (1, 2)
DVE_PLACES = (1, 2)
DVE_OUTPUT_PLACE = 3
PLAN_A = (2, (2, 1, 2, 1, 1, 2, 1, 1), 1, (1, 2, 1, 1, 2, 1, 1, 1), 0)
PLAN_C = (0, (2, 2, 2, 2, 2, 1, 2, 0, 1, 1))


def places(cols):
    at, out = 0, {}
    for name, n in cols:
        out[name] = (at, n)
        at += n
    return out, at


W_AT, W_N = places(W_COLS)
R_AT, R_N = places(R_COLS)
BIG0 = 2 * E0 * HID0
BIG3 = 4 * IC3 * D + 3 * (E3 + 1) * HID3
NE3 = E3 + 1


def build(nc, x_d, ctx_d, ctxT_d, mask0_d, mask1_d, w_d, r_d, big0_d, big3_d, wg_d, wu_d, wd_d, out_d):
    with ExitStack() as stack:
        def sb(name, shape, dt=F32):
            return stack.enter_context(nc.sbuf_tensor(name, shape, dt))

        def sem(name):
            return stack.enter_context(nc.semaphore(name))

        x_all = sb("x_all", [P, B, D])
        h_all = sb("h_all", [P, NG * NC1, T])
        big = sb("big", [P, max(BIG0, BIG3)])
        w = sb("w", [P, W_N])
        rows = sb("rows", [P, R_N])
        wgq = sb("wgq", [P, FF1], BF16)
        wuq = sb("wuq", [P, FF1], BF16)
        wdq = sb("wdq", [P, NC1, D], BF16)
        gsc = sb("gsc", [P, NC1])
        usc = sb("usc", [P, NC1])
        dscB = sb("dscB", [P, D])
        identb = sb("identb", [P, P], BF16)
        ones = sb("ones", [P, P])
        half = sb("half", [P, G])
        sc = sb("sc", [P, 16])
        hmax = sb("hmax", [P, NG * NC1])
        ymax = sb("ymax", [P, NG])
        crz = sb("crz", [P, 2 * D])
        hn_c = sb("hn_c", [P, D])
        hs = sb("hs", [P, D])
        hsT = sb("hsT", [P, P])
        smean = sb("smean", [P, 1])
        c1 = sb("c1", [P, 1])
        xg = sb("xg", [P, G, D])
        xm = sb("xm", [P, G, D])
        yTm = sb("yTm", [P, T])
        spare = sb("spare", [P, 2, T])
        ctxT = sb("ctxT", [P, T])
        mask1i = sb("mask1i", [P, G, S], I32)
        y = sb("y", [P, G, D])
        yT = sb("yT", [P, T])
        qT = sb("qT", [P, T])
        qm = sb("qm", [P, 4, T])
        kT = sb("kT", [P, T])
        r0 = sb("r0", [P, G, D])
        va = sb("va", [P, G, H, 3, DH + 1], BF16)
        pb = sb("pb", [P, 2, BLK * S])
        pt = sb("pt", [P, 2, BLK * S])
        ctx = spare[:, 0, :].rearrange("p (b d) -> p b d", b=G)
        mask0 = spare[:, 1, :].rearrange("p (b k) -> p b k", b=G)
        u3 = spare
        mask1 = mask1i[:, :, :].bitcast(F32)
        pth = pt[:, :, :].bitcast(F16)
        on = sb("on", [P, BLK, DH + 1])
        rc = sb("rc", [P, BLK])
        nm = sb("nm", [P, 2, BLK])
        o = sb("o", [P, G, D])
        oT = sb("oT", [P, T])
        hT = sb("hT", [P, 8, T])
        lg = sb("lg", [P, G, E0])
        cmp_a = sb("cmp_a", [P, G, E0 * E0])
        cmp_b = sb("cmp_b", [P, G, E0 * E0])
        sel = sb("sel", [P, G, E0])
        gate = sb("gate", [P, G, E0])
        gs = sb("gs", [P, 4 * G])
        ps = stack.enter_context(nc.psum_tensor("ps", [P, 8, 512], F32))

        def W(name, p=P):
            a, n = W_AT[name]
            return w[0:p, a:a + n]

        def R(name):
            a, n = R_AT[name]
            return rows[:, a:a + n]

        def row_bcast(name, n):
            return R(name).unsqueeze(1).to_broadcast([P, n, R_AT[name][1]])

        def tiles(k, n=D):
            return ps[:, k, 0:G * n].rearrange("p (b n) -> p b n", b=G)

        ident = W("ident")
        w1_0 = big[:, 0:E0 * HID0].rearrange("p (e c m) -> p e c m", e=E0, c=C0)
        w2_0 = big[:, E0 * HID0:BIG0].rearrange("p (e c m) -> p e c m", e=E0, c=C0)
        q3_w, k3_w, v3_w, o3_w = (big[:, i * IC3 * D:(i + 1) * IC3 * D].rearrange("p (c m) -> p c m", c=IC3)
                                  for i in range(4))
        f3 = big[:, 4 * IC3 * D:BIG3].rearrange("p (w e c m) -> p w e c m", w=3, e=NE3, c=C3)

        small_loaded = sem("small_loaded")
        large_loaded = sem("large_loaded")
        out_stored = sem("out_stored")
        setup_v = sem("setup_v")
        w_rounded = sem("w_rounded")
        w_turned = sem("w_turned")
        diag_ready = sem("diag_ready")
        scales_psum = sem("scales_psum")
        slots_ready = sem("slots_ready")
        slots_psum = sem("slots_psum")
        setup_g = sem("setup_g")
        counted = []

        def isem(name):
            s = sem(name)
            counted.append(s)
            return s

        group_loaded = isem("group_loaded")
        group_loaded2 = isem("group_loaded2")
        mask_loaded = isem("mask_loaded")

        class Stream:
            def __init__(self, name, x, y, yT):
                self.x, self.y, self.yT = x, y, yT
                self.x_ready = isem(f"x_ready_{name}")
                self.ln_stats = isem(f"ln_stats_{name}")
                self.ln_mean = isem(f"ln_mean_{name}")
                self.ln_var = isem(f"ln_var_{name}")
                self.ln_rstd = isem(f"ln_rstd_{name}")
                self.y_ready = isem(f"y_ready_{name}")
                self.yT_psum = isem(f"yT_psum_{name}")
                self.yT_ready = isem(f"yT_ready_{name}")
                self.st = sb(f"st_{name}", [P, G, 6])
                self.mv = sb(f"mv_{name}", [P, G, 2])
                self.ve = sb(f"ve_{name}", [P, G])
                self.rs = sb(f"rs_{name}", [P, G])

        front = Stream("front", xg, y, yT)
        gateT = qT[0:E0, :]
        expert_y = hT[:, 7, :].rearrange("p (b d) -> p b d", b=G)
        experts = Stream("experts", xm, expert_y, yTm)
        late = Stream("late", None, y, yT)
        x_kept = isem("x_kept")
        x_copied = isem("x_copied")
        down_psum = isem("down_psum")
        steps = isem("steps")
        router_steps = isem("router_steps")

        def attention_sems(n):
            names = ["q_psum", "k_psum", "v_psum", "q_col", "k_col", "v_row", "v_hi", "v_rest", "v_mid", "v_ready",
                     "q_ready", "scores", "masked", "maxed", "exps", "transposed", "p_hi", "p_lo", "pv",
                     "o_read", "o_recip", "normed", "oT_psum", "oT_ready", "out_psum", "bias_added", "keys",
                     "chunk_added"]
            return {name: isem(f"{name}_{n}") for name in names}

        att_a = attention_sems("a")
        att_b = attention_sems("b")
        moe = {name: isem(f"moe_{name}") for name in
               ["logits", "logit_row", "shifted", "gate_exp", "gates", "gateT_psum", "gateT", "hid_psum",
                "hid_act", "hid_dve", "expert", "combined", "b2_psum", "silu", "gated", "gate_psum"]}
        slot = {name: isem(f"slot_{name}") for name in
                ["hid_psum", "hid", "logits", "shifted", "exps", "alpha", "in_psum", "in_ready", "wsum", "aT_psum",
                 "aT", "gates_psum", "rz_in", "rz", "n_in", "n", "new", "newT_psum", "newT", "val_psum", "val",
                 "oT_psum", "oT", "out_psum", "bias_added"]}

        def linker(v, semaphore):
            count = [0]

            def link(m):
                count[0] += 1
                m.then_inc(semaphore, 1)
                v.wait_ge(semaphore, count[0])
            return link

        def layernorm_stats_dve(v, f, n, x_number):
            if x_number:
                v.wait_ge(f.x_ready, x_number)
            for b in range(G):
                m = v.bn_stats(f.st[:, b, :], f.x[:, b, :])
            m.then_inc(f.ln_stats, 1)
            v.wait_ge(f.ln_stats, n)
            for b in range(G):
                m = v.bn_aggr(f.mv[:, b, :], f.st[:, b, :])
            m.then_inc(f.ln_mean, 1)
            v.wait_ge(f.ln_mean, n)
            v.tensor_scalar(f.ve[:, :], f.mv[:, :, 1], EPS, None, ALU.add).then_inc(f.ln_var, 1)

        def layernorm_pool(g, f, n):
            g.wait_ge(f.ln_var, n)
            g.tensor_tensor(f.rs[:, :], f.ve[:, :], half[:, :], ALU.pow).then_inc(f.ln_rstd, 1)

        def layernorm_apply_dve(v, f, n):
            v.wait_ge(f.ln_rstd, n)
            for b in range(G):
                m = v.tensor_scalar(f.y[:, b, :], f.x[:, b, :], f.mv[:, b, 0:1], f.rs[:, b:b + 1], ALU.subtract,
                                    ALU.mult)
            m.then_inc(f.y_ready, 1)

        def layernorm_dve(v, f, n, x_number):
            layernorm_stats_dve(v, f, n, x_number)
            layernorm_apply_dve(v, f, n)

        def transpose_y_pe(pe, f, n, bank):
            pe.wait_ge(f.y_ready, n)
            for b in range(G):
                m = pe.transpose(ps[:, bank, b * P:(b + 1) * P], f.y[:, b, :], ident)
            m.then_inc(f.yT_psum, 1)

        def copy_yT_act(a, f, n, bank, out):
            a.wait_ge(f.yT_psum, n)
            a.activation(out, ps[:, bank, :], ACT.Copy).then_inc(f.yT_ready, 1)


        def project_k_pe(pe, s, wk):
            pe.matmul(ps[:, 1, :], wk, ctxT[:, :], start=True, stop=True).then_inc(s["k_psum"], 1)

        def project_q_pe(pe, s, f, n, wq):
            pe.wait_ge(f.yT_ready, n)
            pe.matmul(ps[:, 0, :], wq, f.yT[:, :], start=True, stop=True).then_inc(s["q_psum"], 1)

        def project_v_pe(pe, s, wv):
            for b in range(G):
                m = pe.matmul(ps[:, 3, b * D:(b + 1) * D], ctxT[:, b * S:(b + 1) * S], wv, start=True, stop=True)
            m.then_inc(s["v_psum"], 1)

        def attention_pe(pe, s, before_pv, between):
            pe.wait_ge(s["q_ready"], 1)
            scores_used = s["exps"] if not s["has_mask"] else s["masked"]
            per_unit = 1 if s["has_mask"] else 2
            for t in range(NU + 2):
                if t < NU:
                    b, c = divmod(t, 2)
                    pe.wait_ge(s["keys"], b + 1)
                    if t >= 1:
                        pe.wait_ge(scores_used, per_unit * t)
                    for k in range(BLK):
                        a, j = divmod(k, 4)
                        g = 2 * c + a
                        m = pe.matmul(ps[:, a, j * S:(j + 1) * S],
                                      qm[:, j, b * S:(b + 1) * S], km(b)[:, g, :], start=True, stop=True)
                    m.then_inc(s["scores"], 1)
                between(0, t)
                if 0 <= t - 1 < NU:
                    u = t - 1
                    if u >= 1:
                        pe.wait_ge(s["p_lo"], u)
                    elif s["has_projections"]:
                        pe.wait_ge(s["v_row"], 1)
                    for k in range(BLK):
                        if k % 4 == 0:
                            pe.wait_ge(s["exps"], 2 * u + 1 + k // 4)
                        m = pe.transpose(ps[:, 2 + k // 4, (k % 4) * S:(k % 4 + 1) * S],
                                         pb[:, u % 2, k * S:(k + 1) * S], ident)
                    m.then_inc(s["transposed"], 1)
                between(1, t)
                if t >= 2:
                    u = t - 2
                    b, c = divmod(u, 2)
                    if u == 0:
                        pe.wait_ge(s["v_ready"], 1)
                        if before_pv:
                            pe.wait_ge(*before_pv)
                    pe.wait_ge(s["p_lo"], u + 1)
                    if u >= 1:
                        pe.wait_ge(s["o_read"], u)
                    for k in range(BLK):
                        for part in range(2):
                            m = pe.matmul(ps[:, 4, k * 27:(k + 1) * 27],
                                          pth[:, u % 2, part * BLK * S + k * S:part * BLK * S + (k + 1) * S],
                                          va[:, b, BLK * c + k, :, :].rearrange("p t d -> p (t d)"),
                                          start=(part == 0), stop=(part == 1))
                    m.then_inc(s["pv"], 1)
                between(2, t)

        def attention_oT_pe(pe, s):
            pe.wait_ge(s["normed"], NU)
            for b in range(G):
                m = pe.transpose(ps[:, 4, b * P:(b + 1) * P], o[:, b, :], ident)
            m.then_inc(s["oT_psum"], 1)

        def attention_out_pe(pe, s, wo):
            pe.wait_ge(s["oT_ready"], 1)
            for b in range(G):
                m = pe.matmul(ps[:, 4, b * D:(b + 1) * D], oT[:, b * S:(b + 1) * S], wo, start=True, stop=True)
            m.then_inc(s["out_psum"], 1)

        def keys_act(a, s, bk):
            a.wait_ge(s["k_psum"], 1)
            a.activation(kT[:, :], ps[:, 1, :], ACT.Identity, bias=bk).then_inc(s["k_col"], 1)

        def values_act(a, s, v_src, part):
            heads = v_src[:, :, :].rearrange("p b (h d) -> p (b h) d", h=H)
            rest = r0[:, :, :].rearrange("p b (h d) -> p (b h) d", h=H)
            parts = va[:, :, :, :, :].rearrange("p b h t d -> p (b h) t d")
            if part == 0:
                if s["has_projections"]:
                    a.wait_ge(s["v_row"], 1)
                a.activation(parts[:, :, 0, 0:DH], heads, ACT.Copy).then_inc(s["v_hi"], 1)
            if part == 1:
                a.wait_ge(s["v_rest"], 1)
                a.activation(parts[:, :, 1, 0:DH], rest, ACT.Copy).then_inc(s["v_mid"], 1)

        def queries_act(a, s, bq):
            a.wait_ge(s["q_psum"], 1)
            a.activation(qT[:, :], ps[:, 0, :], ACT.Identity, bias=bq).then_inc(s["q_col"], 1)

        def attention_act(a, s, v_src, between):
            for t in range(NU + 2):
                between(0, t)
                if 1 <= t <= NU:
                    u = t - 1
                    a.wait_ge(s["transposed"], u + 1)
                    if u >= 2:
                        a.wait_ge(s["pv"], u - 1)
                    a.activation(pth[:, u % 2, 0:BLK * S], ps[:, 2:4, :].rearrange("p a k -> p (a k)"), ACT.Copy,
                                 scale=PSCALE).then_inc(s["p_hi"], 1)
                between(1, t)
                if t < NU:
                    u = t
                    a.wait_ge(s["maxed"], u + 1)
                    src = pb[:, u % 2, :] if s["has_mask"] else ps[:, 0:2, :].rearrange("p a k -> p (a k)")
                    for k in range(BLK):
                        m = a.activation(pb[:, u % 2, k * S:(k + 1) * S], src[:, k * S:(k + 1) * S], ACT.Exp,
                                         bias=nm[:, u % 2, k:k + 1])
                        if k % 4 == 3:
                            m.then_inc(s["exps"], 1)
                values_act(a, s, v_src, t)
                between(2, t)

        def attention_out_act(a, s):
            a.wait_ge(s["oT_psum"], 1)
            a.activation(oT[:, :], ps[:, 4, :], ACT.Copy).then_inc(s["oT_ready"], 1)

        def km(b):
            return (yT, oT)[b % 2][:, :].rearrange("p (g k) -> p g k", g=4)

        def keys_pool(g, s, k_in, b):
            if b == 0 and s["has_projections"]:
                g.wait_ge(s["q_psum"], 1)
            if b >= 2:
                g.wait_ge(s["scores"], 2 * (b - 1))
            g.tensor_tensor(km(b), k_in[:, b * S:(b + 1) * S].unsqueeze(1).to_broadcast([P, 4, S]),
                            W("hg").unsqueeze(2).to_broadcast([P, 4, S]), ALU.mult).then_inc(s["keys"], 1)

        def values_pool(g, s, v_src):
            heads = v_src[:, :, :].rearrange("p b (h d) -> p (b h) d", h=H)
            rest = r0[:, :, :].rearrange("p b (h d) -> p (b h) d", h=H)
            parts = va[:, :, :, :, :].rearrange("p b h t d -> p (b h) t d")
            g.wait_ge(s["v_hi"], 1)
            g.tensor_tensor(rest, heads, parts[:, :, 0, 0:DH], ALU.subtract).then_inc(s["v_rest"], 1)
            g.wait_ge(s["v_mid"], 1)
            g.tensor_tensor(parts[:, :, 2, 0:DH], rest, parts[:, :, 1, 0:DH], ALU.subtract).then_inc(s["v_ready"], 1)

        def values_dve(v, s, bias_v):
            v.wait_ge(s["v_psum"], 1)
            v.tensor_tensor(o[:, :, :], tiles(3), row_bcast(bias_v, G), ALU.add).then_inc(s["v_row"], 1)

        def queries_dve(v, s, q_there, n, heads_mask):
            v.wait_ge(q_there, n)
            for j in range(4):
                m = v.tensor_scalar(qm[:, j, :], qT[:, :], heads_mask[:, j:j + 1], None, ALU.mult)
            m.then_inc(s["q_ready"], 1)

        def attention_dve(v, s, mask_op, o_was_values, between):
            for t in range(NU + 2):
                between(0, t)
                if t < NU:
                    u = t
                    b = u // 2
                    sc_ps = ps[:, 0:2, :].rearrange("p a (j k) -> p (a j) k", k=S)
                    v.wait_ge(s["scores"], u + 1)
                    if mask_op is not None:
                        if u >= 2:
                            v.wait_ge(s["transposed"], u - 1)
                        buf = pb[:, u % 2, :].rearrange("p (j k) -> p j k", k=S)
                        mask_op(v, buf, sc_ps, b).then_inc(s["masked"], 1)
                        v.wait_ge(s["masked"], u + 1)
                        sc_ps = buf
                    if u >= 2:
                        v.wait_ge(s["exps"], 2 * (u - 1))
                    v.tensor_reduce(nm[:, u % 2, :], sc_ps, AX, ALU.max, negate=True).then_inc(s["maxed"], 1)
                between(1, t)
                if 0 <= t - 1 < NU:
                    u = t - 1
                    v.wait_ge(s["p_hi"], u + 1)
                    v.scalar_tensor_tensor(pth[:, u % 2, BLK * S:2 * BLK * S], ps[:, 2:4, :].rearrange("p a k -> p (a k)"),
                                           PSCALE, pth[:, u % 2, 0:BLK * S], ALU.mult,
                                           ALU.subtract).then_inc(s["p_lo"], 1)
                between(2, t)
                if t >= 2:
                    u = t - 2
                    b, c = divmod(u, 2)
                    v.wait_ge(s["pv"], u + 1)
                    if u >= 1:
                        v.wait_ge(s["normed"], u)
                    v.tensor_reduce(on[:, :, :], ps[:, 4, 0:BLK * 27].rearrange("p (k t d) -> p k d t", k=BLK, t=3), AX,
                                    ALU.add).then_inc(s["o_read"], 1)
                    v.wait_ge(s["o_read"], u + 1)
                    v.reciprocal(rc[:, :], on[:, :, DH]).then_inc(s["o_recip"], 1)
                    v.wait_ge(s["o_recip"], u + 1)
                    if u == 0 and o_was_values:
                        v.wait_ge(s["v_ready"], 1)
                    v.tensor_tensor(o[:, b, c * 64:(c + 1) * 64].rearrange("p (k d) -> p k d", d=DH), on[:, :, 0:DH],
                                    rc[:, :].unsqueeze(2).to_broadcast([P, BLK, DH]), ALU.mult).then_inc(s["normed"], 1)
                between(3, t)

        def add_bias_pool(g, f, n, bias):
            g.wait_ge(f.y_ready, n)
            return g.tensor_tensor(f.x[:, :, :], f.x[:, :, :], row_bcast(bias, G), ALU.add)

        def router_pe(pe, wr):
            for b in range(G):
                m = pe.matmul(ps[:, 7, b * E0:(b + 1) * E0], yTm[:, b * S:(b + 1) * S], wr, start=True, stop=True)
            m.then_inc(moe["logits"], 1)

        def router_dve(v, link, bias):
            v.wait_ge(moe["logits"], 1)
            link(v.tensor_tensor(lg[:, :, :], tiles(7, E0), row_bcast(bias, G), ALU.add))
            other = lg[:, :, :].unsqueeze(2).to_broadcast([P, G, E0, E0])
            own = lg[:, :, :].unsqueeze(3).to_broadcast([P, G, E0, E0])
            ca = cmp_a[:, :, :].rearrange("p b (e f) -> p b e f", e=E0)
            cb = cmp_b[:, :, :].rearrange("p b (e f) -> p b e f", e=E0)
            v.tensor_tensor(ca, other, own, ALU.is_gt)
            v.tensor_reduce(gs[:, 0:G], lg[:, :, :], AX, ALU.max)
            link(v.tensor_tensor(cb, other, own, ALU.is_equal))
            link(v.tensor_tensor(cmp_b[:, :, :], cmp_b[:, :, :],
                                 W("below").unsqueeze(1).to_broadcast([P, G, E0 * E0]), ALU.mult))
            v.tensor_tensor(lg[:, :, :], lg[:, :, :], gs[:, 0:G].unsqueeze(2).to_broadcast([P, G, E0]),
                            ALU.subtract).then_inc(moe["shifted"], 1)
            link(v.tensor_tensor(cmp_a[:, :, :], cmp_a[:, :, :], cmp_b[:, :, :], ALU.add))
            link(v.tensor_reduce(sel[:, :, :], ca, AX, ALU.add))
            link(v.tensor_scalar(sel[:, :, :], sel[:, :, :], 2.0, None, ALU.is_lt))

        def router_gates_dve(v, link):
            v.wait_ge(moe["gate_exp"], 1)
            link(v.tensor_tensor(gate[:, :, :], gate[:, :, :], sel[:, :, :], ALU.mult))
            link(v.tensor_reduce(gs[:, G:2 * G], gate[:, :, :], AX, ALU.add))
            link(v.reciprocal(gs[:, 2 * G:3 * G], gs[:, G:2 * G]))
            v.tensor_tensor(gate[:, :, :], gate[:, :, :], gs[:, 2 * G:3 * G].unsqueeze(2).to_broadcast([P, G, E0]),
                            ALU.mult).then_inc(moe["gates"], 1)
            v.wait_ge(moe["gates"], 1)

        def router_act(a):
            a.wait_ge(moe["shifted"], 1)
            a.activation(gate[:, :, :], lg[:, :, :], ACT.Exp).then_inc(moe["gate_exp"], 1)

        def expert_pe(pe, e, chunks, w_out):
            if e == 0:
                pe.wait_ge(moe["shifted"], 1)
            else:
                pe.wait_ge(moe["combined"], e)
            for b in range(G):
                for c in range(chunks):
                    m = pe.matmul(ps[:, 7, b * D:(b + 1) * D], hT[:, (e * chunks + c) % 8, b * S:(b + 1) * S],
                                  w_out[:, e, c, :], start=(c == 0), stop=(c == chunks - 1))
            m.then_inc(moe["expert"], 1)

        def combine_dve(v, e, gated):
            v.wait_ge(moe["expert"], e + 1)
            if e:
                v.wait_ge(moe["combined"], e)
            for b in range(G):
                m = v.scalar_tensor_tensor(xm[:, b, :], ps[:, 7, b * D:(b + 1) * D],
                                           gate[:, b, e:e + 1] if gated else 1.0, xm[:, b, :], ALU.mult, ALU.add)
            m.then_inc(moe["combined"], 1)

        HALF0, HALF1, OUTPUT = range(3)

        def item_order(n_experts):
            order = [HALF0, HALF1]
            for e in range(n_experts - 1):
                order += [3 * (e + 1) + HALF0, 3 * e + OUTPUT, 3 * (e + 1) + HALF1]
            return order + [3 * (n_experts - 1) + OUTPUT]

        order0, order3 = item_order(E0), item_order(NE3)

        def beside(work, order, first, counts, places, output_place=None):
            table, n = {}, first
            for t, count in enumerate(counts):
                at = 0
                for i in range(count):
                    at = max(at, output_place if order[n] % 3 == OUTPUT and output_place is not None else places[i])
                    table.setdefault((at, t), []).append(n)
                    n += 1

            def between(place, t):
                for n in table.get((place, t), ()):
                    work(n)
            return between

        def extended(between, extra):
            def both(place, t):
                extra(place, t)
                between(place, t)
            return both

        def experts0_pe(pe, n):
            e, kind = divmod(n, 3)
            if kind == OUTPUT:
                pe.wait_ge(moe["hid_act"], 2 * (e + 1))
                pe.wait_ge(moe["hid_dve"], 2 * (e + 1))
                expert_pe(pe, e, C0, w2_0)
                return
            for c in (2 * kind, 2 * kind + 1):
                k = e * C0 + c
                if k >= 2:
                    pe.wait_ge(moe["hid_act" if k % 2 == 0 else "hid_dve"], k // 2)
                pe.matmul(ps[:, 5 + k % 2, :], w1_0[:, e, c, :], yTm[:, :], start=True, stop=True)\
                    .then_inc(moe["hid_psum"], 1)

        def experts0_act(a, n):
            e, kind = divmod(n, 3)
            if kind != OUTPUT:
                k = e * C0 + 2 * kind
                a.wait_ge(moe["hid_psum"], k + 1)
                if k >= 8:
                    a.wait_ge(moe["expert"], (k - 8) // C0 + 1)
                a.activation(hT[:, k % 8, :], ps[:, 5, :], ACT.Relu, bias=W("b1_0")[:, k:k + 1])\
                    .then_inc(moe["hid_act"], 1)

        def experts0_dve(v, n):
            e, kind = divmod(n, 3)
            if kind == OUTPUT:
                combine_dve(v, e, True)
                return
            k = e * C0 + 2 * kind + 1
            v.wait_ge(moe["hid_psum"], k + 1)
            if k >= 8:
                v.wait_ge(moe["expert"], (k - 8) // C0 + 1)
            v.tensor_scalar(hT[:, k % 8, :], ps[:, 6, :], W("b1_0")[:, k:k + 1], 0.0, ALU.add, ALU.max)\
                .then_inc(moe["hid_dve"], 1)

        def gates_pe(pe):
            pe.wait_ge(moe["hid_act"], 2 * E0)
            for b in range(G):
                m = pe.transpose(ps[0:E0, 5, b * S:(b + 1) * S], gate[:, b, :], ident)
            m.then_inc(moe["gateT_psum"], 1)

        def gates_dve(v):
            v.wait_ge(moe["gateT_psum"], 1)
            v.tensor_copy(gateT[:, :], ps[0:E0, 5, :]).then_inc(moe["gateT"], 1)

        def biases_pe(pe):
            pe.wait_ge(moe["gateT"], 1)
            pe.wait_ge(moe["hid_dve"], 2 * E0)
            for b in range(G):
                m = pe.matmul(ps[:, 6, b * D:(b + 1) * D], gateT[:, b * S:(b + 1) * S], W("b2_0", E0),
                              start=True, stop=True)
            m.then_inc(moe["b2_psum"], 1)

        n_small, n_large = 9, 2
        with nc.Block() as block:
            @block.sync
            def _(sp):
                sp.dma_start(w[:, :], w_d).then_inc(small_loaded, 16)
                sp.dma_start(rows[:, :], r_d.partition_broadcast(P)).then_inc(small_loaded, 16)
                for k, src in enumerate((wg_d, wu_d)):
                    for c, (at, m) in enumerate(CH1):
                        sp.dma_start(hT[0:m, 3 * k + c, 0:D], src[at:at + m, :]).then_inc(small_loaded, 16)
                sp.dma_start(hT[:, 6, 0:FF1], wd_d).then_inc(small_loaded, 16)
                sp.dma_start(x_all[:, :, :], x_d.rearrange("b s d -> s b d")).then_inc(large_loaded, 16)
                sp.dma_start(big[:, 0:BIG0], big0_d).then_inc(large_loaded, 16)
                sp.wait_ge(large_loaded, 16 * n_large)

            @block.gpsimd
            def _(g):
                g.memset(ones[:, :], 1.0)
                g.memset(half[:, :], -0.5)
                g.memset(hmax[:, :], 0.0)
                g.memset(va[:, :, :, :, :], 0.0).then_inc(setup_g, 1)
                g.wait_ge(setup_g, 1)
                g.memset(va[:, :, :, 0, DH:DH + 1], 1.0).then_inc(setup_g, 1)

            @block.vector
            def _(v):
                link = linker(v, setup_v)
                v.memset(gsc[:, :], 0.0)
                v.memset(usc[:, :], 0.0)
                v.wait_ge(small_loaded, 16 * n_small)
                v.tensor_copy(identb[:, :], ident).then_inc(w_rounded, 1)
                for t in range(7):
                    m, n = (P, FF1) if t == 6 else (CH1[t % 3][1], D)
                    src = hT[0:m, t, 0:n]
                    scale = usc[0:m, t - 3:t - 2] if 3 <= t < 6 else (gsc[0:m, t:t + 1] if t < 3 else sc[0:m, 0:1])
                    link(v.tensor_reduce(sc[0:m, 1:2], src, AX, ALU.max, apply_absolute_value=True))
                    link(v.tensor_scalar(scale, sc[0:m, 1:2], 1.0 / QMAX, None, ALU.mult))
                    link(v.reciprocal(sc[0:m, 2:3], scale))
                    link(v.tensor_scalar(src, src, sc[0:m, 2:3], MAGIC, ALU.mult, ALU.add))
                    link(v.tensor_scalar(src, src, MAGIC, None, ALU.subtract))
                    v.tensor_scalar(pt[0:m, t % 2, 0:192].bitcast(BF16)[:, 0:n], src, QMAX, -QMAX - 1.0,
                                    ALU.min, ALU.max).then_inc(w_rounded, 1)
                    v.wait_ge(w_turned, t + 1)
                    pw = ps[:, t, 0:256].bitcast(BF16)
                    if t < 3:
                        v.tensor_copy(wgq[:, CH1[t][0]:CH1[t][0] + m], pw[:, 0:m])
                    elif t < 6:
                        v.tensor_copy(wuq[:, CH1[t - 3][0]:CH1[t - 3][0] + m], pw[:, 0:m])
                    else:
                        for c, (at, mc) in enumerate(CH1):
                            v.tensor_copy(wdq[0:mc, c, :], pw[0:mc, c * P:(c + 1) * P])
                v.tensor_scalar(hT[:, 7, 0:P], ident, sc[:, 0:1], None, ALU.mult).then_inc(diag_ready, 1)
                v.wait_ge(scales_psum, 1)
                v.tensor_copy(dscB[:, :], ps[:, 7, 0:P])
                link(v.tensor_scalar(sc[:, 4:5], R("tau"), -1.0, None, ALU.mult))
                link(v.tensor_tensor(sc[:, 4:5], sc[:, 4:5], R("tau"), ALU.max))
                link(v.tensor_scalar(sc[:, 4:5], sc[:, 4:5], 0.1, None, ALU.add))
                v.reciprocal(sc[:, 5:6], sc[:, 4:5])
                v.tensor_scalar(hs[:, :], W("slot"), W("slot_scale"), None, ALU.mult).then_inc(slots_ready, 1)
                v.wait_ge(slots_psum, 1)
                v.tensor_copy(hsT[:, :], ps[:, 1, 0:P])
                v.tensor_scalar(smean[:, :], ps[:, 2, 0:1], 1.0 / SLOTS, None, ALU.mult).then_inc(slots_ready, 1)
                v.wait_ge(slots_psum, 2)
                v.tensor_tensor(c1[0:HR, :], ps[0:HR, 3, 0:1], W("b1s", HR), ALU.add)
                link(v.tensor_tensor(crz[:, :], ps[:, 4, 0:2 * D], R("bhh")[:, 0:2 * D], ALU.add))
                v.tensor_tensor(crz[:, :], crz[:, :], R("bih")[:, 0:2 * D], ALU.add)
                v.tensor_tensor(hn_c[:, :], ps[:, 4, 2 * D:3 * D], R("bhh")[:, 2 * D:3 * D], ALU.add)

            @block.tensor
            def _(pe):
                for t in range(7):
                    pe.wait_ge(w_rounded, 1 + t + 1)
                    m = P if t == 6 else CH1[t % 3][1]
                    pw = ps[:, t, 0:256].bitcast(BF16)
                    src = pt[0:m, t % 2, 0:192].bitcast(BF16)
                    if t < 6:
                        i = pe.transpose(pw[:, 0:m], src[:, 0:D], identb[0:m, 0:m])
                    else:
                        for c, (at, mc) in enumerate(CH1):
                            i = pe.transpose(pw[0:mc, c * P:(c + 1) * P], src[:, at:at + mc], identb[:, :])
                    i.then_inc(w_turned, 1)
                pe.wait_ge(setup_g, 1)
                pe.wait_ge(diag_ready, 1)
                pe.matmul(ps[:, 7, 0:P], ones[:, :], hT[:, 7, 0:P], start=True, stop=True).then_inc(scales_psum, 1)
                pe.wait_ge(slots_ready, 1)
                pe.transpose(ps[:, 1, 0:P], hs[:, :], ident)
                pe.matmul(ps[:, 2, 0:1], hs[0:SLOTS, :], ones[0:SLOTS, 0:1], start=True, stop=True)\
                    .then_inc(slots_psum, 1)
                pe.wait_ge(slots_ready, 2)
                pe.matmul(ps[0:HR, 3, 0:1], W("w1m"), smean[:, :], start=True, stop=True)
                pe.matmul(ps[:, 4, 0:3 * D], hsT[:, :], W("whh"), start=True, stop=True).then_inc(slots_psum, 1)

            @block.scalar
            def _(a):
                a.wait_ge(small_loaded, 16 * n_small)
                a.activation(sc[:, 6:7], R("clip_x"), ACT.Sigmoid)
                a.activation(sc[:, 7:8], R("clip_down"), ACT.Sigmoid)

        first, last = counted[0].num, counted[-1].num
        assert [s.num for s in counted] == list(range(first, last + 1))

        def next_iteration():
            nc.gpsimd.sem_clear(range(first, last + 1))
            nc.all_engine_barrier()

        def mask0_add(v, out, scores, b):
            return v.tensor_tensor(out, scores, mask0[:, b, :].unsqueeze(1).to_broadcast([P, BLK, S]), ALU.add)

        def mask1_clip(v, out, scores, b):
            return v.scalar_tensor_tensor(out, scores, -100.0, mask1[:, b, :].unsqueeze(1).to_broadcast([P, BLK, S]),
                                          ALU.max, ALU.min)

        s0 = dict(att_a, has_mask=True, has_projections=False)
        s1 = dict(att_b, has_mask=True, has_projections=True)
        ctx_rows = ctx_d.rearrange("b s d -> s b d")
        mask0_rows = mask0_d.rearrange("b s d -> s b d")
        mask1_rows = mask1_d.rearrange("b s d -> s b d")

        def x_group(g):
            return x_all[:, bass.ds(g * G, G), :]

        A_START, A_STEPS0, A_MID, A_STEPS1, A_END = PLAN_A

        first0 = A_START
        first_mid = first0 + sum(A_STEPS0)
        first1 = first_mid + A_MID
        first_end = first1 + sum(A_STEPS1)
        assert first_end + A_END == 3 * E0 and A_START >= 2

        def iteration_a(g0, gm, g1):
            has_0, has_m, has_1 = g0 is not None, gm is not None, g1 is not None
            if has_0:
                front.x = x_group(g0)
                experts.x = x_group(g0)
            if has_1:
                late.x = x_group(g1)

            def in_attention(table):
                def extra(place, t):
                    if has_1 and (place, t) in table:
                        table[(place, t)]()
                return extra

            def without_attention(table):
                if has_1:
                    for key in table:
                        table[key]()

            with nc.Block() as block:
                @block.sync
                def _(sp):
                    if has_0:
                        sp.dma_start(ctxT[:, :], ctxT_d[:, bass.ds(g0 * T, T)]).then_inc(group_loaded, 16)
                        sp.dma_start(ctx[:, :, :], ctx_rows[:, bass.ds(g0 * G, G), :]).then_inc(group_loaded, 16)
                        sp.dma_start(mask0[:, :, :], mask0_rows[:, bass.ds(g0 * G, G), :]).then_inc(group_loaded, 16)
                        sp.wait_ge(group_loaded, 48)
                    if has_1:
                        sp.dma_start(mask1i[:, :, :], mask1_rows[:, bass.ds(g1 * G, G), :]).then_inc(mask_loaded, 16)
                        if has_0:
                            sp.wait_ge(s0["keys"], G)
                        sp.dma_start(ctxT[:, :], ctxT_d[:, bass.ds(g1 * T, T)]).then_inc(group_loaded2, 16)
                        sp.wait_ge(group_loaded2, 16)
                        sp.wait_ge(mask_loaded, 16)

                @block.tensor
                def _(pe):
                    def items(*numbers):
                        if has_m:
                            for n in numbers:
                                experts0_pe(pe, order0[n])

                    def late_yT():
                        if has_0:
                            pe.wait_ge(s0["masked"], NU)
                        transpose_y_pe(pe, late, 1, 0)

                    def late_k():
                        pe.wait_ge(group_loaded2, 16)
                        project_k_pe(pe, s1, W("wk1"))

                    late_work = {(1, NU): late_yT, (2, NU): late_k,
                                 (1, NU + 1): lambda: project_q_pe(pe, s1, late, 1, W("wq1"))}

                    if has_m:
                        router_pe(pe, W("wr0"))
                    items(0)
                    if has_0:
                        transpose_y_pe(pe, front, 1, 4)
                    items(*range(1, first0))
                    if has_0:
                        attention_pe(pe, s0, (front.yT_ready, 1),
                                     extended(beside(items, order0, first0, A_STEPS0, PE_PLACES), in_attention(late_work)))
                    else:
                        items(*range(first0, first_mid))
                        without_attention(late_work)
                    if has_1:
                        project_v_pe(pe, s1, W("wv1"))
                    items(*range(first_mid, first1))
                    if has_0:
                        attention_oT_pe(pe, s0)

                    def out_0(place, t):
                        if has_0 and (place, t) == (0, 0):
                            attention_out_pe(pe, s0, W("wo0"))

                    if has_1:
                        attention_pe(pe, s1, (front.x_ready, 1) if has_0 else None,
                                     extended(beside(items, order0, first1, A_STEPS1, PE_PLACES), out_0))
                    else:
                        out_0(0, 0)
                        items(*range(first1, first_end))
                    items(*range(first_end, 3 * E0))
                    if has_m:
                        gates_pe(pe)
                    if has_1:
                        attention_oT_pe(pe, s1)
                    if has_m:
                        biases_pe(pe)
                    if has_1:
                        attention_out_pe(pe, s1, W("wo1"))
                    if has_0:
                        if has_m:
                            pe.wait_ge(moe["combined"], E0)
                        transpose_y_pe(pe, experts, 1, 7)

                @block.scalar
                def _(a):
                    def items(*numbers):
                        if has_m:
                            for n in numbers:
                                experts0_act(a, order0[n])

                    late_work = {(2, NU): lambda: copy_yT_act(a, late, 1, 0, yT[:, :]),
                                 (0, NU + 1): lambda: keys_act(a, s1, W("bk1")),
                                 (2, NU + 1): lambda: queries_act(a, s1, W("bq1"))}
                    if has_m:
                        a.activation(xm[:, :, :], x_group(gm), ACT.Copy).then_inc(experts.x_ready, 1)
                    items(0)
                    if has_0:
                        copy_yT_act(a, front, 1, 4, qT[:, :])
                    items(1)
                    if has_m:
                        router_act(a)
                    items(*range(2, first0))
                    if has_0:
                        a.wait_ge(group_loaded, 48)
                        attention_act(a, s0, ctx, extended(beside(items, order0, first0, A_STEPS0, ACT_PLACES),
                                                           in_attention(late_work)))
                    else:
                        items(*range(first0, first_mid))
                        without_attention(late_work)
                    items(*range(first_mid, first1))
                    if has_0:
                        attention_out_act(a, s0)
                    if has_1:
                        attention_act(a, s1, o, beside(items, order0, first1, A_STEPS1, ACT_PLACES))
                    else:
                        items(*range(first1, first_end))
                    items(*range(first_end, 3 * E0))
                    if has_1:
                        attention_out_act(a, s1)
                    if has_0:
                        copy_yT_act(a, experts, 1, 7, yTm[:, :])

                @block.gpsimd
                def _(g):
                    if has_0:
                        layernorm_pool(g, front, 1)
                        g.wait_ge(group_loaded, 48)
                        keys_pool(g, s0, ctxT, 0)
                        keys_pool(g, s0, ctxT, 1)
                        values_pool(g, s0, ctx)
                        for b in range(2, G):
                            keys_pool(g, s0, ctxT, b)
                    if has_1:
                        layernorm_pool(g, late, 1)
                        g.wait_ge(late.y_ready, 1)
                        g.tensor_tensor(x_group(g1), x_group(g1), row_bcast("bo1", G), ALU.add)\
                            .then_inc(s1["bias_added"], 1)
                        g.wait_ge(s1["k_col"], 1)
                        keys_pool(g, s1, kT, 0)
                        if has_0:
                            g.wait_ge(s0["out_psum"], 1)
                        keys_pool(g, s1, kT, 1)
                        if has_0:
                            g.wait_ge(front.x_ready, 1)
                        values_pool(g, s1, o)
                        for b in range(2, G):
                            keys_pool(g, s1, kT, b)
                    if has_0:
                        layernorm_pool(g, experts, 1)
                    if has_1:
                        layernorm_pool(g, late, 2)

                @block.vector
                def _(v):
                    router_link = linker(v, router_steps)
                    link = linker(v, steps)

                    def items(*numbers):
                        if has_m:
                            for n in numbers:
                                experts0_dve(v, order0[n])

                    def late_mask():
                        v.wait_ge(mask_loaded, 16)
                        link(v.tensor_scalar(mask1[:, :, :], mask1i[:, :, :], 0.0, NEG, ALU.is_equal, ALU.mult))
                        v.tensor_scalar(mask1[:, :, :], mask1[:, :, :], 100.0, None, ALU.add)

                    def late_apply():
                        if has_0:
                            v.wait_ge(front.yT_psum, 1)
                        layernorm_apply_dve(v, late, 1)

                    late_work = {(3, NU - 4): late_mask, (3, NU - 3): lambda: layernorm_stats_dve(v, late, 1, 0),
                                 (3, NU - 2): late_apply}

                    if has_0:
                        layernorm_stats_dve(v, front, 1, 0)
                        layernorm_apply_dve(v, front, 1)
                    items(0, 1)
                    if has_m:
                        v.wait_ge(experts.x_ready, 1)
                        router_dve(v, router_link, "br0")
                    if has_0:
                        queries_dve(v, s0, front.yT_ready, 1, W("hm"))
                    if has_m:
                        router_gates_dve(v, router_link)
                    items(*range(2, first0))
                    if has_0:
                        v.wait_ge(group_loaded, 48)
                        attention_dve(v, s0, mask0_add, False, extended(
                            beside(items, order0, first0, A_STEPS0, DVE_PLACES, DVE_OUTPUT_PLACE),
                            in_attention(late_work)))
                    else:
                        items(*range(first0, first_mid))
                        without_attention(late_work)
                    if has_1:
                        queries_dve(v, s1, s1["q_col"], 1, W("hms"))
                    items(*range(first_mid, first1))
                    if has_1:
                        if has_0:
                            v.wait_ge(s0["oT_psum"], 1)
                        values_dve(v, s1, "bv1")

                    def out_0(place, t):
                        if has_0 and (place, t) == (3, 0):
                            v.wait_ge(s0["out_psum"], 1)
                            v.tensor_tensor(r0[:, :, :], tiles(4), row_bcast("wo_b0", G), ALU.add)\
                                .then_inc(s0["v_row"], 1)
                            v.wait_ge(s0["v_row"], 1)
                            v.scalar_tensor_tensor(x_group(g0), r0[:, :, :], 0.0, x_group(g0), ALU.max, ALU.add)\
                                .then_inc(front.x_ready, 1)

                    if has_1:
                        attention_dve(v, s1, mask1_clip, True,
                                      extended(beside(items, order0, first1, A_STEPS1, DVE_PLACES, DVE_OUTPUT_PLACE), out_0))
                    else:
                        out_0(3, 0)
                        items(*range(first1, first_end))
                    items(*range(first_end, 3 * E0))
                    if has_0:
                        v.wait_ge(front.x_ready, 1)
                        layernorm_stats_dve(v, experts, 1, 0)
                    if has_m:
                        gates_dve(v)
                    if has_0:
                        layernorm_apply_dve(v, experts, 1)
                    if has_m:
                        v.wait_ge(moe["b2_psum"], 1)
                        v.wait_ge(moe["combined"], E0)
                        v.tensor_tensor(x_group(gm), tiles(6), xm[:, :, :], ALU.add)
                    if has_1:
                        v.wait_ge(s1["bias_added"], 1)
                        v.wait_ge(s1["out_psum"], 1)
                        v.tensor_tensor(x_group(g1), tiles(4), x_group(g1), ALU.add).then_inc(late.x_ready, 1)
                        layernorm_stats_dve(v, late, 2, 1)
                        layernorm_apply_dve(v, late, 2)
                        v.wait_ge(late.y_ready, 2)
                        y3 = y[:, :, :].rearrange("p b d -> p (b d)")
                        v.tensor_copy(h_all[:, bass.ds(g1 * NC1, 1), :], y3.unsqueeze(1))
                        v.tensor_reduce(ymax[:, bass.ds(g1, 1)], y3, AX, ALU.max, apply_absolute_value=True)

            next_iteration()

        iteration_a(0, None, None)
        iteration_a(1, 0, None)
        with nc.Fori(2, NG) as i:
            iteration_a(i, i - 1, i - 2)
        iteration_a(None, NG - 1, NG - 2)
        iteration_a(None, None, NG - 1)

        with nc.Block() as block:
            @block.vector
            def _(v):
                v.tensor_reduce(sc[:, 8:9], ymax[:, :], AX, ALU.max).then_inc(steps, 1)
                v.wait_ge(setup_g, 3)
                v.tensor_scalar(sc[:, 10:11], sc[:, 9:10], 1.0 / QMAX, sc[:, 6:7], ALU.mult, ALU.mult).then_inc(steps, 1)
                v.wait_ge(steps, 2)
                v.reciprocal(sc[:, 11:12], sc[:, 10:11])
                v.tensor_scalar(gsc[:, :], gsc[:, :], sc[:, 10:11], None, ALU.mult)
                v.tensor_scalar(usc[:, :], usc[:, :], sc[:, 10:11], None, ALU.mult).then_inc(steps, 1)
                v.wait_ge(steps, 3)

            @block.gpsimd
            def _(g):
                g.wait_ge(steps, 1)
                g.partition_all_reduce(sc[:, 9:10], sc[:, 8:9], P, RMAX).then_inc(setup_g, 1)

            @block.sync
            def _(sp):
                sp.dma_start(big[:, 0:BIG3], big3_d).then_inc(large_loaded, 16)

        next_iteration()

        xq = [pt[:, 0, n * 256:(n + 1) * 256].bitcast(BF16) for n in range(2)]
        xqT = [pt[:, 1, n * 256:(n + 1) * 256].bitcast(BF16) for n in range(2)]
        with nc.Fori(0, NG // UNROLL_B) as i:
            with nc.Block() as block:
                @block.tensor
                def _(pe):
                    t_out = ps[:, 7, 0:256].bitcast(BF16)
                    for j in range(UNROLL_B):
                        pe.wait_ge(front.y_ready, j + 1)
                        if j:
                            pe.wait_ge(front.yT_ready, j)
                        for b in range(G):
                            m = pe.transpose(t_out[:, b * P:(b + 1) * P], xq[j % 2][:, b * D:(b + 1) * D],
                                             identb[:, :])
                        m.then_inc(front.yT_psum, 1)
                        pe.wait_ge(front.yT_ready, j + 1)
                        for c, (at, m) in enumerate(CH1):
                            if j:
                                pe.wait_ge(moe["silu"], (j - 1) * NC1 + c + 1)
                                pe.wait_ge(moe["hid_dve"], (j - 1) * NC1 + c + 1)
                            pe.matmul(ps[0:m, c, :], wgq[:, at:at + m], xqT[j % 2], start=True, stop=True)
                            pe.matmul(ps[0:m, 3 + c, :], wuq[:, at:at + m], xqT[j % 2], start=True, stop=True)\
                                .then_inc(moe["hid_psum"], 1)

                @block.scalar
                def _(a):
                    for j in range(UNROLL_B):
                        a.wait_ge(front.yT_psum, j + 1)
                        if j >= 2:
                            a.wait_ge(moe["hid_psum"], (j - 1) * NC1)
                        a.activation(xqT[j % 2], ps[:, 7, 0:256].bitcast(BF16), ACT.Copy)\
                            .then_inc(front.yT_ready, 1)
                        for c, (at, m) in enumerate(CH1):
                            a.wait_ge(moe["hid_psum"], j * NC1 + c + 1)
                            if j:
                                a.wait_ge(moe["hid_dve"], (j - 1) * NC1 + c + 1)
                            a.activation(hT[0:m, c, :], ps[0:m, c, :], ACT.Silu, scale=gsc[0:m, c:c + 1])\
                                .then_inc(moe["silu"], 1)

                @block.vector
                def _(v):
                    link = linker(v, steps)

                    def quantise_input(j):
                        if j >= 2:
                            v.wait_ge(front.yT_psum, j - 1)
                        source = h_all[:, bass.ds((i * UNROLL_B + j) * NC1, 1), :]
                        link(v.tensor_scalar(source, source, sc[:, 11:12], QMAX, ALU.mult, ALU.min))
                        link(v.tensor_scalar(source, source, -QMAX - 1.0, MAGIC, ALU.max, ALU.add))
                        v.tensor_scalar(xq[j % 2].unsqueeze(1), source, MAGIC, None, ALU.subtract)\
                            .then_inc(front.y_ready, 1)

                    quantise_input(0)
                    for j in range(UNROLL_B):
                        if j + 1 < UNROLL_B:
                            quantise_input(j + 1)
                        v.wait_ge(front.y_ready, j + 1)
                        for c, (at, m) in enumerate(CH1):
                            v.wait_ge(moe["silu"], j * NC1 + c + 1)
                            v.scalar_tensor_tensor(h_all[0:m, bass.ds((i * UNROLL_B + j) * NC1 + c, 1), :],
                                                   ps[0:m, 3 + c, :].unsqueeze(1), usc[0:m, c:c + 1],
                                                   hT[0:m, c, :].unsqueeze(1), ALU.mult, ALU.mult)\
                                .then_inc(moe["hid_dve"], 1)
                        for c, (at, m) in enumerate(CH1):
                            v.wait_ge(moe["hid_dve"], j * NC1 + c + 1)
                            h = h_all[0:m, bass.ds((i * UNROLL_B + j) * NC1 + c, 1), :]
                            v.tensor_reduce(hmax[0:m, bass.ds((i * UNROLL_B + j) * NC1 + c, 1)],
                                            h.rearrange("p a t -> p (a t)"), AX, ALU.max, apply_absolute_value=True)

            next_iteration()

        hq = spare[:, :, :].rearrange("p a t -> p (a t)").bitcast(BF16)[:, 0:NC1 * T]\
            .rearrange("p (c t) -> p c t", c=NC1)

        def quantise_hidden(v, link, g):
            def operation(n):
                block, kind = divmod(n, 3)
                m, c0, c1_ = ((P, 0, NC1 - 1), (CH1[-1][1], NC1 - 1, NC1))[block]
                h = h_all[0:m, bass.ds(g * NC1 + c0, c1_ - c0), :]
                if kind == 0:
                    i = v.tensor_scalar(h, h, sc[0:m, 11:12], QMAX, ALU.mult, ALU.min)
                elif kind == 1:
                    i = v.tensor_scalar(h, h, -QMAX - 1.0, MAGIC, ALU.max, ALU.add)
                else:
                    i = v.tensor_scalar(hq[0:m, c0:c1_, :], h, MAGIC, None, ALU.subtract)
                link(i)
            return operation

        with nc.Block() as block:
            @block.vector
            def _(v):
                v.tensor_reduce(sc[:, 8:9], hmax[:, :], AX, ALU.max).then_inc(steps, 1)
                v.wait_ge(setup_g, 4)
                v.tensor_scalar(sc[:, 10:11], sc[:, 9:10], 1.0 / QMAX, sc[:, 7:8], ALU.mult, ALU.mult).then_inc(steps, 1)
                v.wait_ge(steps, 2)
                v.reciprocal(sc[:, 11:12], sc[:, 10:11])
                v.tensor_scalar(dscB[:, :], dscB[:, :], sc[:, 10:11], None, ALU.mult).then_inc(steps, 1)
                v.wait_ge(steps, 3)
                first_quantised = quantise_hidden(v, linker(v, router_steps), 0)
                for n in range(6):
                    first_quantised(n)

            @block.gpsimd
            def _(g):
                g.wait_ge(steps, 1)
                g.partition_all_reduce(sc[:, 9:10], sc[:, 8:9], P, RMAX).then_inc(setup_g, 1)

            @block.sync
            def _(sp):
                sp.dma_start(ctxT[:, :], ctxT_d[:, 0:T]).then_inc(group_loaded, 16)
                sp.wait_ge(group_loaded, 16)
                sp.wait_ge(large_loaded, 16 * (n_large + 1))

        next_iteration()

        s2 = dict(att_a, has_mask=False, has_projections=True)
        s3 = att_b
        pc = [buf[:, n, k:k + T] for buf in (pb, pt) for n in range(2) for k in (0, T)]
        gT = pc[0][0:HR, :]
        slg = pc[1][:, 0:G * SLOTS].rearrange("p (b s) -> p b s", b=G)
        srep = pc[1][:, G * SLOTS:2 * G * SLOTS].rearrange("p (b s) -> p b s", b=G)
        alpha = pc[2][:, 0:G * SLOTS].rearrange("p (b s) -> p b s", b=G)
        stop8 = pc[2][:, 256:256 + G * 8].rearrange("p (b s) -> p b s", b=G)
        srow = pc[2][:, 288:304]
        siT = pc[3][:, 0:256]
        aT = pc[3][:, 256:512].rearrange("p (q t) -> p q t", q=2)
        rz = pc[4][:, :].rearrange("p (q n) -> p q n", q=2)
        xn = pc[5][:, 0:256].rearrange("p (q n) -> p q n", q=2)
        hnew = pc[5][:, 256:512].rearrange("p (q n) -> p q n", q=2)
        hnT = pc[6][:, 0:256]
        sval = pc[6][:, 256:512].rearrange("p (q n) -> p q n", q=2)
        outT = pc[7][:, :]
        q3 = qm[:, 0:2, :]
        k3 = qm[:, 2:4, :]
        v3 = [hT[:, n, :] for n in (0, 1, 7)]
        o3 = hT[:, 2:4, :]
        oT3 = hT[:, 4:6, :]
        sums = hT[:, 6, 0:2 * BLK].rearrange("p (u k) -> p u k", u=2)
        rc3 = hT[:, 6, 16:16 + BLK]

        def pair3(k, alone):
            return (0, 1) if alone and k % 2 else (5, 6)

        def experts3_pe(pe, n, alone):
            e, kind = divmod(n, 3)
            if kind == OUTPUT:
                pe.wait_ge(moe["hid_dve"], C3 * (e + 1))
                expert_pe(pe, e, C3, f3[:, 2])
                return
            k = e * C3 + kind
            gate_bank, up_bank = pair3(k, alone)
            before = k - 1 if alone else k
            if before >= 1:
                pe.wait_ge(moe["gated"], before)
            pe.matmul(ps[:, gate_bank, :], f3[:, 0, e, kind, :], yTm[:, :], start=True, stop=True)\
                .then_inc(moe["gate_psum"], 1)
            if before >= 1:
                pe.wait_ge(moe["hid_dve"], before)
            pe.matmul(ps[:, up_bank, :], f3[:, 1, e, kind, :], yTm[:, :], start=True, stop=True)\
                .then_inc(moe["hid_psum"], 1)

        def experts3_act(a, n, alone):
            e, kind = divmod(n, 3)
            if kind != OUTPUT:
                k = e * C3 + kind
                a.wait_ge(moe["gate_psum"], k + 1)
                if k >= 2:
                    a.wait_ge(moe["hid_dve"], k - 1)
                a.activation(u3[:, k % 2, :], ps[:, pair3(k, alone)[0], :], ACT.Tanh,
                             scale=0.5).then_inc(moe["silu"], 1)

        def experts3_dve(v, n, alone):
            e, kind = divmod(n, 3)
            if kind == OUTPUT:
                combine_dve(v, e, e < E3)
                return
            k = e * C3 + kind
            v.wait_ge(moe["silu"], k + 1)
            if k >= 8:
                v.wait_ge(moe["expert"], (k - 8) // C3 + 1)
            v.scalar_tensor_tensor(u3[:, k % 2, :], u3[:, k % 2, :], 1.0, ps[:, pair3(k, alone)[0], :], ALU.add,
                                   ALU.mult)\
                .then_inc(moe["gated"], 1)
            v.wait_ge(moe["gated"], k + 1)
            v.wait_ge(moe["hid_psum"], k + 1)
            v.scalar_tensor_tensor(hT[:, k % 8, :], ps[:, pair3(k, alone)[1], :], 0.5, u3[:, k % 2, :], ALU.mult,
                                   ALU.mult)\
                .then_inc(moe["hid_dve"], 1)

        C_START, C_STEPS = PLAN_C
        assert C_START + sum(C_STEPS) == 15 and C_START <= OUTPUT

        front.x, experts.x = xg, xm

        def iteration_c(gf, gm, gn):
            front_too, experts_too = gf is not None, gm is not None
            alone = not front_too
            with nc.Block() as block:
                @block.sync
                def _(sp):
                    if gn is not None:
                        if front_too:
                            sp.wait_ge(s3["v_psum"], IC3)
                        sp.dma_start(ctxT[:, :], ctxT_d[:, bass.ds(gn * T, T)]).then_inc(group_loaded, 16)
                    if experts_too:
                        sp.wait_ge(x_kept, 1)
                        sp.dma_start(out_d.rearrange("b s d -> s b d")[:, bass.ds(gm * G, G), :], x_group(gm))\
                            .then_inc(out_stored, 16)
                    if gn is not None:
                        sp.wait_ge(group_loaded, 16)

                @block.tensor
                def _(pe):
                    def items(*numbers):
                        if experts_too:
                            for n in numbers:
                                experts3_pe(pe, order3[n], alone)

                    if not front_too:
                        transpose_y_pe(pe, experts, 1, 7)
                        pe.wait_ge(experts.yT_ready, 1)
                        router_pe(pe, W("rw3"))
                        items(*range(3 * NE3))
                        return
                    for b in range(G):
                        for c, (at, m) in enumerate(CH1):
                            j = pe.matmul(ps[:, 4, b * D:(b + 1) * D], hq[0:m, c, b * S:(b + 1) * S], wdq[0:m, c, :],
                                          start=(c == 0), stop=(c == NC1 - 1))
                    j.then_inc(down_psum, 1)
                    project_k_pe(pe, s2, W("wk2"))
                    project_v_pe(pe, s2, W("wv2"))
                    transpose_y_pe(pe, front, 1, 4)
                    if experts_too:
                        transpose_y_pe(pe, experts, 1, 7)
                    project_q_pe(pe, s2, front, 1, W("wq2"))
                    if experts_too:
                        pe.wait_ge(experts.yT_ready, 1)
                        router_pe(pe, W("rw3"))
                    items(*range(C_START))
                    attention_pe(pe, s2, (front.yT_ready, 1), beside(items, order3, C_START, C_STEPS, PE_PLACES))
                    attention_oT_pe(pe, s2)
                    attention_out_pe(pe, s2, W("wo2"))
                    items(15, 16)
                    def project_q(c):
                        pe.matmul(ps[:, 7 if c else 4, :], q3_w[:, c, :], yT[:, :], start=True, stop=True)\
                            .then_inc(s3["q_psum"], 1)

                    def project_k(c):
                        if c:
                            pe.wait_ge(s3["q_col"], c + 1)
                        pe.matmul(ps[:, 7, :], k3_w[:, c, :], ctxT[:, :], start=True, stop=True)\
                            .then_inc(s3["k_psum"], 1)

                    def project_v(c):
                        pe.wait_ge(s3["k_col"], c + 1)
                        for b in range(G):
                            m = pe.matmul(ps[:, 7, b * D:(b + 1) * D], ctxT[:, b * S:(b + 1) * S], v3_w[:, c, :],
                                          start=True, stop=True)
                        m.then_inc(s3["v_psum"], 1)

                    transpose_y_pe(pe, front, 2, 4)
                    items(17)
                    pe.wait_ge(front.yT_ready, 2)
                    pe.matmul(ps[0:HR, 0, :], W("w1x"), yT[:, :], start=True, stop=True).then_inc(slot["hid_psum"], 1)
                    items(18)
                    pe.wait_ge(slot["hid"], 1)
                    for b in range(G):
                        m = pe.matmul(ps[:, 1, b * SLOTS:(b + 1) * SLOTS], gT[:, b * S:(b + 1) * S], W("w2s", HR),
                                      start=True, stop=True)
                    m.then_inc(slot["logits"], 1)
                    items(19, 20)
                    pe.wait_ge(slot["alpha"], 1)
                    for b in range(G):
                        m = pe.matmul(ps[:, 2, b * SLOTS:(b + 1) * SLOTS], y[:, b, :], alpha[:, b, :], start=True,
                                      stop=True)
                    m.then_inc(slot["in_psum"], 1)
                    for b in range(G):
                        q, a = divmod(b, 2)
                        m = pe.matmul(ps[64 * a:64 * a + 64, 1, q:q + 1], alpha[:, b, :], ones[:, 0:1], start=True,
                                      stop=True)
                    m.then_inc(slot["wsum"], 1)
                    for q in range(2):
                        m = pe.transpose(ps[:, 4, q * P:(q + 1) * P],
                                         alpha[:, 2 * q:2 * q + 2, :].rearrange("p b s -> p (b s)"), ident)
                    m.then_inc(slot["aT_psum"], 1)
                    items(21)
                    pe.wait_ge(slot["in_ready"], 1)
                    for q in range(2):
                        m = pe.matmul(ps[:, 2 + q, 0:3 * D], siT[:, q * P:(q + 1) * P], W("wih"), start=True, stop=True)
                    m.then_inc(slot["gates_psum"], 1)
                    items(22, 23, 24)
                    pe.wait_ge(slot["new"], 1)
                    for q in range(2):
                        m = pe.transpose(ps[:, 0, q * P:(q + 1) * P], hnew[:, q, :], ident)
                    m.then_inc(slot["newT_psum"], 1)
                    items(25)
                    pe.wait_ge(slot["newT"], 1)
                    for q in range(2):
                        m = pe.matmul(ps[:, 1, q * D:(q + 1) * D], hnT[:, q * P:(q + 1) * P], W("wvs"), start=True,
                                      stop=True)
                    m.then_inc(slot["val_psum"], 1)
                    pe.wait_ge(slot["val"], 1)
                    pe.wait_ge(slot["aT"], 1)
                    for b in range(G):
                        q, a = divmod(b, 2)
                        m = pe.matmul(ps[:, 2 + a, q * S:(q + 1) * S], sval[64 * a:64 * a + 64, q, :],
                                      aT[64 * a:64 * a + 64, q, :], start=True, stop=True)
                    m.then_inc(slot["oT_psum"], 1)
                    pe.wait_ge(slot["oT"], 1)
                    for b in range(G):
                        m = pe.matmul(ps[:, 4, b * D:(b + 1) * D], outT[:, b * S:(b + 1) * S], W("wos"), start=True,
                                      stop=True)
                    m.then_inc(slot["out_psum"], 1)
                    items(26)
                    if experts_too:
                        pe.wait_ge(moe["combined"], NE3)
                    project_k(0)
                    project_v(0)
                    transpose_y_pe(pe, front, 3, 4)
                    pe.wait_ge(front.yT_ready, 3)

                    def scores(u, a):
                        for b in range(G):
                            m = pe.matmul(ps[:, 2 * (u % 2) + a, b * S:(b + 1) * S],
                                          q3[64 * a:64 * a + 64, u % 2, b * S:(b + 1) * S],
                                          k3[64 * a:64 * a + 64, u % 2, b * S:(b + 1) * S], start=True, stop=True)
                        if a:
                            m.then_inc(s3["scores"], 1)

                    def values(u, a):
                        for b in range(G):
                            k = G * a + b
                            m = pe.matmul(ps[:, 6, k * DH3:(k + 1) * DH3], pt[:, u % 2, k * S:(k + 1) * S],
                                          v3[u % 3][:, b * D + a * DH3:b * D + (a + 1) * DH3], start=True, stop=True)
                        if a:
                            m.then_inc(s3["pv"], 1)

                    project_q(0)
                    for step in range(IC3 + 3):
                        has_s, has_t, has_o, has_out = step < IC3, 0 < step <= IC3, 2 <= step < IC3 + 2, step >= 3
                        has_p = step + 1 < IC3
                        if has_s:
                            if step == 0:
                                pe.wait_ge(s3["q_col"], 1)
                            if step >= 2:
                                pe.wait_ge(s3["exps"], step - 1)
                            scores(step, 0)
                        if has_out:
                            u = step - 3
                            pe.wait_ge(s3["oT_ready"], u + 1)
                            for b in range(G):
                                m = pe.matmul(ps[:, 7, b * D:(b + 1) * D], oT3[:, u % 2, b * S:(b + 1) * S],
                                              o3_w[:, u, :], start=True, stop=True)
                            m.then_inc(s3["out_psum"], 1)
                        if has_s:
                            scores(step, 1)
                        if has_p:
                            if has_out:
                                pe.wait_ge(s3["chunk_added"], step - 2)
                            else:
                                pe.wait_ge(s3["v_row"], step + 1)
                            project_q(step + 1)
                        if has_t:
                            u = step - 1
                            pe.wait_ge(s3["exps"], u + 1)
                            if u >= 1:
                                pe.wait_ge(s3["p_hi"], u)
                                pe.wait_ge(s3["p_lo"], u)
                            for k in range(BLK):
                                m = pe.transpose(ps[:, 4 + k // 4, (k % 4) * S:(k % 4 + 1) * S],
                                                 pb[:, u % 2, k * S:(k + 1) * S], ident)
                                if k % 4 == 3:
                                    m.then_inc(s3["transposed"], 1)
                        if has_p:
                            project_k(step + 1)
                        if has_t:
                            u = step - 1
                            pe.wait_ge(s3["v_row"], u + 1)
                            pe.wait_ge(s3["p_hi"], u + 1)
                            if u >= 1:
                                pe.wait_ge(s3["normed"], u)
                            values(u, 0)
                        if has_p:
                            project_v(step + 1)
                        if has_t:
                            pe.wait_ge(s3["p_lo"], u + 1)
                            values(u, 1)
                        if has_o:
                            u = step - 2
                            pe.wait_ge(s3["normed"], u + 1)
                            if has_p:
                                pe.wait_ge(s3["v_row"], step + 2)
                            elif has_out:
                                pe.wait_ge(s3["chunk_added"], step - 2)
                            for b in range(G):
                                m = pe.transpose(ps[:, 7, b * P:(b + 1) * P], o3[:, u % 2, b * D:(b + 1) * D], ident)
                            m.then_inc(s3["oT_psum"], 1)

                @block.scalar
                def _(a):
                    def items(*numbers):
                        if experts_too:
                            for n in numbers:
                                experts3_act(a, order3[n], alone)

                    def router(place, t):
                        if experts_too and (place, t) == (0, 1):
                            router_act(a)

                    if front_too:
                        a.activation(xg[:, :, :], x_group(gf), ACT.Copy).then_inc(x_copied, 1)
                    if experts_too:
                        a.activation(xm[:, :, :], x_group(gm), ACT.Copy).then_inc(experts.x_ready, 1)
                    if front_too:
                        keys_act(a, s2, W("bk2"))
                    if not front_too:
                        copy_yT_act(a, experts, 1, 7, yTm[:, :])
                        router(0, 1)
                        items(*range(3 * NE3))
                        a.wait_ge(moe["combined"], NE3)
                        a.activation(x_group(gm), xm[:, :, :], ACT.Copy).then_inc(x_kept, 1)
                        return
                    copy_yT_act(a, front, 1, 4, yT[:, :])
                    queries_act(a, s2, W("bq2"))
                    if experts_too:
                        copy_yT_act(a, experts, 1, 7, yTm[:, :])
                    items(*range(C_START))
                    attention_act(a, s2, o, extended(beside(items, order3, C_START, C_STEPS, ACT_PLACES), router))
                    attention_out_act(a, s2)
                    items(15, 16)
                    copy_yT_act(a, front, 2, 4, yT[:, :])
                    items(17)
                    a.wait_ge(slot["hid_psum"], 1)
                    a.activation(gT, ps[0:HR, 0, :], ACT.Gelu, bias=c1[0:HR, :]).then_inc(slot["hid"], 1)
                    items(18, 19)
                    a.wait_ge(slot["shifted"], 1)
                    a.activation(slg, slg, ACT.Exp).then_inc(slot["exps"], 1)
                    items(20)
                    a.wait_ge(slot["in_psum"], 1)
                    a.activation(siT, ps[:, 2, 0:256], ACT.Copy).then_inc(slot["in_ready"], 1)
                    a.wait_ge(slot["aT_psum"], 1)
                    a.activation(aT, ps[:, 4, 0:256].rearrange("p (q t) -> p q t", q=2), ACT.Copy)\
                        .then_inc(slot["aT"], 1)
                    items(21, 22)
                    a.wait_ge(slot["rz_in"], 1)
                    a.activation(rz, rz, ACT.Sigmoid).then_inc(slot["rz"], 1)
                    items(23)
                    a.wait_ge(slot["n_in"], 1)
                    a.activation(xn, xn, ACT.Tanh).then_inc(slot["n"], 1)
                    items(24)
                    a.wait_ge(slot["newT_psum"], 1)
                    a.activation(hnT, ps[:, 0, 0:256], ACT.Copy).then_inc(slot["newT"], 1)
                    items(25)
                    a.wait_ge(slot["oT_psum"], 1)
                    a.activation(outT.rearrange("p (q a t) -> p a q t", q=2, a=2),
                                 ps[:, 2:4, 0:2 * S].rearrange("p a (q t) -> p a q t", q=2), ACT.Copy)\
                        .then_inc(slot["oT"], 1)
                    if experts_too:
                        a.wait_ge(moe["combined"], NE3)
                        a.activation(x_group(gm), xm[:, :, :], ACT.Copy).then_inc(x_kept, 1)
                    copy_yT_act(a, front, 3, 4, yT[:, :])

                    def project_q(c):
                        a.wait_ge(s3["q_psum"], c + 1)
                        a.activation(q3[:, c % 2, :], ps[:, 7 if c else 4, :], ACT.Copy, scale=DH3 ** -0.5)\
                            .then_inc(s3["q_col"], 1)

                    project_q(0)
                    for step in range(IC3 + 2):
                        if step + 1 < IC3:
                            project_q(step + 1)
                        if 0 < step <= IC3:
                            u = step - 1
                            a.wait_ge(s3["transposed"], 2 * u + 1)
                            if u >= 2:
                                a.wait_ge(s3["pv"], u - 1)
                            a.activation(pt[:, u % 2, 0:512], ps[:, 4, :], ACT.Copy).then_inc(s3["p_hi"], 1)
                        if step < IC3:
                            u = step
                            a.wait_ge(s3["maxed"], u + 1)
                            if u >= 2:
                                a.wait_ge(s3["transposed"], 2 * (u - 1))
                                a.wait_ge(s3["o_recip"], u - 1)
                            src = ps[:, 2 * (u % 2):2 * (u % 2) + 2, :].rearrange("p a k -> p (a k)")
                            for k in range(BLK):
                                m = a.activation(pb[:, u % 2, k * S:(k + 1) * S], src[:, k * S:(k + 1) * S], ACT.Exp,
                                                 bias=nm[:, u % 2, k:k + 1], accum_out=sums[:, u % 2, k:k + 1])
                            m.then_inc(s3["exps"], 1)
                        if step >= 2:
                            u = step - 2
                            a.wait_ge(s3["oT_psum"], u + 1)
                            if u >= 2:
                                a.wait_ge(s3["out_psum"], u - 1)
                            a.activation(oT3[:, u % 2, :], ps[:, 7, :], ACT.Copy).then_inc(s3["oT_ready"], 1)
                    a.wait_ge(front.x_ready, 4)
                    a.activation(x_group(gf), xg[:, :, :], ACT.Copy)

                @block.gpsimd
                def _(g):
                    if not front_too:
                        layernorm_pool(g, experts, 1)
                        return
                    layernorm_pool(g, front, 1)
                    if experts_too:
                        layernorm_pool(g, experts, 1)
                    g.wait_ge(s2["k_col"], 1)
                    keys_pool(g, s2, kT, 0)
                    keys_pool(g, s2, kT, 1)
                    values_pool(g, s2, o)
                    for b in range(2, G):
                        keys_pool(g, s2, kT, b)
                    add_bias_pool(g, front, 1, "bo2").then_inc(s2["bias_added"], 1)
                    layernorm_pool(g, front, 2)
                    add_bias_pool(g, front, 2, "bos").then_inc(slot["bias_added"], 1)
                    layernorm_pool(g, front, 3)
                    add_bias_pool(g, front, 3, "bout3").then_inc(s3["bias_added"], 1)

                @block.vector
                def _(v):
                    link = linker(v, router_steps)

                    def items(*numbers):
                        if experts_too:
                            for n in numbers:
                                experts3_dve(v, order3[n], alone)

                    def router(place, t):
                        if experts_too and (place, t) == (3, 0):
                            router_dve(v, link, "rb3")
                        if experts_too and (place, t) == (3, 1):
                            router_gates_dve(v, link)

                    if not front_too:
                        layernorm_dve(v, experts, 1, 1)
                        router(3, 0)
                        router(3, 1)
                        items(*range(3 * NE3))
                        return
                    slink = linker(v, steps)
                    quantise_step = None if gn is None else quantise_hidden(v, slink, gn)
                    v.wait_ge(down_psum, 1)
                    slink(v.tensor_tensor(r0[:, :, :], tiles(4), dscB[:, :].unsqueeze(1).to_broadcast([P, G, D]),
                                         ALU.mult))
                    v.wait_ge(x_copied, 1)
                    v.tensor_tensor(xg[:, :, :], xg[:, :, :], r0[:, :, :], ALU.add).then_inc(front.x_ready, 1)
                    layernorm_stats_dve(v, front, 1, 1)
                    if experts_too:
                        layernorm_stats_dve(v, experts, 1, 1)
                    values_dve(v, s2, "bv2")
                    layernorm_apply_dve(v, front, 1)
                    if experts_too:
                        layernorm_apply_dve(v, experts, 1)
                    queries_dve(v, s2, s2["q_col"], 1, W("hms"))
                    items(*range(C_START))
                    attention_dve(v, s2, None, True,
                                  extended(beside(items, order3, C_START, C_STEPS, DVE_PLACES, DVE_OUTPUT_PLACE), router))
                    v.wait_ge(s2["bias_added"], 1)
                    v.wait_ge(s2["out_psum"], 1)
                    v.tensor_tensor(xg[:, :, :], tiles(4), xg[:, :, :], ALU.add).then_inc(front.x_ready, 1)
                    items(15)
                    layernorm_dve(v, front, 2, 2)
                    items(16, 17, 18)
                    v.wait_ge(slot["logits"], 1)
                    slink(v.tensor_tensor(slg, tiles(1, SLOTS), row_bcast("b2s", G), ALU.add))
                    slink(v.tensor_scalar(slg, slg, sc[:, 5:6], None, ALU.mult))
                    for b in range(G):
                        j = v.max(stop8[:, b, :], slg[:, b, :])
                    slink(j)
                    for b in range(G):
                        j = v.match_replace(srep[:, b, :], stop8[:, b, :], slg[:, b, :], NEG)
                    slink(j)
                    v.tensor_tensor(srep, srep, slg, ALU.not_equal)
                    v.tensor_tensor(slg, slg, stop8[:, :, 0:1].to_broadcast([P, G, SLOTS]), ALU.subtract)\
                        .then_inc(slot["shifted"], 1)
                    items(19)
                    v.wait_ge(slot["exps"], 1)
                    slink(v.tensor_tensor(alpha, slg, srep, ALU.mult))
                    slink(v.tensor_reduce(srow[:, 0:G], alpha, AX, ALU.add))
                    slink(v.reciprocal(srow[:, G:2 * G], srow[:, 0:G]))
                    v.tensor_tensor(alpha, alpha, srow[:, G:2 * G].unsqueeze(2).to_broadcast([P, G, SLOTS]),
                                    ALU.mult).then_inc(slot["alpha"], 1)
                    items(20)
                    v.wait_ge(slot["wsum"], 1)
                    slink(v.tensor_scalar(srow[:, 8:10], ps[:, 1, 0:2], 1e-8, None, ALU.add))
                    slink(v.reciprocal(srow[:, 10:12], srow[:, 8:10]))
                    items(21)
                    v.wait_ge(slot["gates_psum"], 1)
                    for q in range(2):
                        j = v.scalar_tensor_tensor(rz[:, q, :], ps[:, 2 + q, 0:2 * D], srow[:, 10 + q:11 + q],
                                                   crz[:, :], ALU.mult, ALU.add)
                    j.then_inc(slot["rz_in"], 1)
                    for q in range(2):
                        v.scalar_tensor_tensor(xn[:, q, :], ps[:, 2 + q, 2 * D:3 * D], srow[:, 10 + q:11 + q],
                                               R("bih")[:, 2 * D:3 * D], ALU.mult, ALU.add)
                    items(22)
                    v.wait_ge(slot["rz"], 1)
                    both = [P, 2, D]
                    slink(v.tensor_tensor(rz[:, :, 0:D], rz[:, :, 0:D], hn_c[:, :].unsqueeze(1).to_broadcast(both),
                                         ALU.mult))
                    v.tensor_tensor(xn, xn, rz[:, :, 0:D], ALU.add).then_inc(slot["n_in"], 1)
                    items(23)
                    v.wait_ge(slot["n"], 1)
                    slink(v.tensor_tensor(hnew, hs[:, :].unsqueeze(1).to_broadcast(both), xn, ALU.subtract))
                    slink(v.tensor_tensor(hnew, hnew, rz[:, :, D:2 * D], ALU.mult))
                    v.tensor_tensor(hnew, hnew, xn, ALU.add).then_inc(slot["new"], 1)
                    items(24, 25)
                    v.wait_ge(slot["val_psum"], 1)
                    v.tensor_tensor(sval, ps[:, 1, 0:2 * D].rearrange("p (q d) -> p q d", q=2), row_bcast("bvs", 2),
                                    ALU.add).then_inc(slot["val"], 1)

                    def project_k(c):
                        v.wait_ge(s3["k_psum"], c + 1)
                        v.tensor_copy(k3[:, c % 2, :], ps[:, 7, :]).then_inc(s3["k_col"], 1)

                    def project_v(c):
                        v.wait_ge(s3["v_psum"], c + 1)
                        if c >= 3:
                            v.wait_ge(s3["pv"], c - 2)
                        v.tensor_copy(v3[c % 3], ps[:, 7, :]).then_inc(s3["v_row"], 1)

                    v.wait_ge(slot["out_psum"], 1)
                    v.wait_ge(slot["bias_added"], 1)
                    v.tensor_tensor(xg[:, :, :], tiles(4), xg[:, :, :], ALU.add).then_inc(front.x_ready, 1)
                    layernorm_stats_dve(v, front, 3, 3)
                    items(26)
                    layernorm_apply_dve(v, front, 3)
                    project_k(0)
                    project_v(0)

                    for step in range(IC3 + 3):
                        if step >= 3:
                            u = step - 3
                            v.wait_ge(s3["out_psum"], u + 1)
                            v.wait_ge(s3["chunk_added"], u) if u else v.wait_ge(s3["bias_added"], 1)
                            j = v.tensor_tensor(xg[:, :, :], tiles(7), xg[:, :, :], ALU.add)
                            j.then_inc(s3["chunk_added"] if u < IC3 - 1 else front.x_ready, 1)
                        if step < IC3:
                            u = step
                            v.wait_ge(s3["scores"], u + 1)
                            if u >= 2:
                                v.wait_ge(s3["exps"], u - 1)
                            v.tensor_reduce(nm[:, u % 2, :], ps[:, 2 * (u % 2):2 * (u % 2) + 2, :].rearrange(
                                "p a (j k) -> p (a j) k", k=S), AX, ALU.max, negate=True).then_inc(s3["maxed"], 1)
                        if 0 < step <= IC3:
                            u = step - 1
                            v.wait_ge(s3["transposed"], 2 * u + 2)
                            if u >= 2:
                                v.wait_ge(s3["pv"], u - 1)
                            v.tensor_copy(pt[:, u % 2, 512:1024], ps[:, 5, :]).then_inc(s3["p_lo"], 1)
                        if step + 1 < IC3:
                            project_k(step + 1)
                        if step == 0:
                            project_v(1)
                        if gn is not None and 1 <= step <= 6:
                            quantise_step(step - 1)
                        if 0 < step <= IC3:
                            v.wait_ge(s3["exps"], u + 1)
                            if u >= 1:
                                v.wait_ge(s3["normed"], u)
                            v.reciprocal(rc3, sums[:, u % 2, :]).then_inc(s3["o_recip"], 1)
                            if step + 1 < IC3:
                                project_v(step + 1)
                            v.wait_ge(s3["o_recip"], u + 1)
                            v.wait_ge(s3["pv"], u + 1)
                            if u >= 2:
                                v.wait_ge(s3["oT_psum"], u - 1)
                            v.tensor_tensor(o3[:, u % 2, :].rearrange("p (b a c) -> p a b c", b=G, a=2),
                                            ps[:, 6, :].rearrange("p (a b c) -> p a b c", a=2, b=G),
                                            rc3.rearrange("p (a b) -> p a b", a=2).unsqueeze(3)
                                            .to_broadcast([P, 2, G, DH3]), ALU.mult).then_inc(s3["normed"], 1)

            next_iteration()

        iteration_c(0, None, 1)
        with nc.Fori(1, NG - 1) as i:
            iteration_c(i, i - 1, i + 1)
        iteration_c(NG - 1, NG - 2, None)
        iteration_c(None, NG - 1, None)

        with nc.Block() as block:
            @block.sync
            def _(sp):
                sp.wait_ge(out_stored, 16 * NG)


def pack(parts, names, height):
    return np.concatenate([np.asarray(parts[name], np.float32).reshape(height, -1) for name, _ in names], axis=1)


def kernel(**inputs):
    import concourse.bacc as bacc
    from concourse.bass_utils import run_bass_kernel_spmd

    a = {k: np.asarray(v) for k, v in inputs.items()}

    def col(v):
        return v.reshape(-1, 1)

    def pad(v):
        return np.concatenate([v, np.zeros((P - v.shape[0], v.shape[1]), v.dtype)], axis=0)

    h_of = np.arange(P) // DH % 4
    head = (h_of[:, None] == np.arange(4)[None, :]).astype(np.float32)
    below = np.tile((np.arange(E0)[None, :] < np.arange(E0)[:, None]).astype(np.float32).reshape(1, -1), (P, 1))
    parts = {
        "ident": np.eye(P, dtype=np.float32), "wo0": a["L0_xattn_wo_w"].T, "wr0": a["L0_ffn_Wr"],
        "b1_0": a["L0_ffn_b1"].reshape(E0 * C0, P).T, "b2_0": pad(a["L0_ffn_b2"]),
        "wq1": a["L1_xattn_wq"].T, "wk1": a["L1_xattn_wk"].T, "wv1": a["L1_xattn_wv"].T, "wo1": a["L1_xattn_wo"].T,
        "bq1": col(a["L1_xattn_bq"]), "bk1": col(a["L1_xattn_bk"]),
        "wq2": a["L2_xattn_Wq"], "wk2": a["L2_xattn_Wk"], "wv2": a["L2_xattn_Wv"], "wo2": a["L2_xattn_Wo"],
        "bq2": col(a["L2_xattn_bq"]), "bk2": col(a["L2_xattn_bk"]),
        "w1x": a["L2_ffn_w1"][:, :D].T, "w1m": a["L2_ffn_w1"][:, D:].T, "w2s": pad(a["L2_ffn_w2"].T),
        "b1s": pad(col(a["L2_ffn_b1"])), "wih": a["L2_ffn_gru_wih"].T, "whh": a["L2_ffn_gru_whh"].T,
        "wvs": a["L2_ffn_wv"].T, "wos": a["L2_ffn_wo"].T,
        "slot": np.tile(a["L2_ffn_slot_init"], (2, 1)), "slot_scale": np.tile(a["L2_ffn_slot_scale"], (2, 1)),
        "rw3": a["L3_ffn_rw"], "hm": head, "hms": head * np.float32(DH ** -0.5),
        "hg": (np.arange(P)[:, None] // 32 == np.arange(4)[None, :]).astype(np.float32), "below": below,
    }
    rows = {
        "br0": a["L0_ffn_br"], "wo_b0": a["L0_xattn_wo_b"], "bv1": a["L1_xattn_bv"], "bo1": a["L1_xattn_bo"],
        "bv2": a["L2_xattn_bv"], "bo2": a["L2_xattn_bo"], "b2s": a["L2_ffn_b2"], "bih": a["L2_ffn_gru_bih"],
        "bhh": a["L2_ffn_gru_bhh"], "bvs": a["L2_ffn_bv"], "bos": a["L2_ffn_bo"], "bout3": a["L3_xattn_bout"],
        "rb3": a["L3_ffn_rb"], "clip_x": a["L1_ffn_clip_x"], "clip_down": a["L1_ffn_clip_down"],
        "tau": a["L2_ffn_tau"],
    }

    def down(v, chunks):
        return v.reshape(v.shape[0], chunks, P, v.shape[2]).transpose(2, 0, 1, 3).reshape(P, -1)

    def across(v):
        return v.transpose(1, 0, 2).reshape(P, -1)

    inner = IC3 * P
    e_in1 = np.concatenate([a["L3_ffn_ew1"], a["L3_ffn_sw1"][None]])
    e_in2 = np.concatenate([a["L3_ffn_ew2"], a["L3_ffn_sw2"][None]])
    e_out = np.concatenate([a["L3_ffn_ew3"], a["L3_ffn_sw3"][None]])
    arrays = {
        "x": a["x"], "ctx": a["ctx_1024"], "ctxT": a["ctx_1024"].reshape(B * S, D).T,
        "mask0": a["mask_Bx1xSxS2_ff0"].reshape(B, S, S), "mask1": a["mask_Bx1xSxS2_ik1"].reshape(B, S, S),
        "w": pack(parts, W_COLS, P), "rows": pack(rows, R_COLS, 1).reshape(-1),
        "big0": np.concatenate([across(a["L0_ffn_W1"]), down(a["L0_ffn_W2"], C0)], axis=1),
        "big3": np.concatenate([a["L3_xattn_Wq"], a["L3_xattn_Wkv"][:, :inner], a["L3_xattn_Wkv"][:, inner:],
                                down(a["L3_xattn_Wout"][None], IC3), across(e_in1), across(e_in2),
                                down(e_out, C3)], axis=1),
        "wg": a["L1_ffn_w_gate"], "wu": a["L1_ffn_w_up"], "wd": a["L1_ffn_w_down"],
    }
    arrays = {k: np.ascontiguousarray(v) for k, v in arrays.items()}
    nc = bacc.Bacc("TRN2", target_bir_lowering=False, num_devices=1)
    args = [nc.dram_tensor(f"in_{k}", v.shape, mybir.dt.from_np(v.dtype), kind="ExternalInput").ap()
            for k, v in arrays.items()]
    out = nc.dram_tensor("out", (B, S, D), F32, kind="ExternalOutput").ap()
    build(nc, *args, out)
    r = run_bass_kernel_spmd(nc, [{f"in_{k}": v for k, v in arrays.items()}], core_ids=[0])
    return r.results[0]["out"]
```
